# Optimizing a Trainium2 kernel written in Bass

```python
import numpy as np
import jax
import jax.numpy as jnp

def _softmax(x, axis=-1):
    return jax.nn.softmax(x, axis=axis)

def _gelu(x):
    return jax.nn.gelu(x, approximate=True)

def _silu(x):
    return jax.nn.silu(x)

def _sigmoid(x):
    return jax.nn.sigmoid(x)

def _layernorm(x, axis=-1, eps=1e-05):
    m = jnp.mean(x, axis=axis, keepdims=True)
    v = jnp.var(x, axis=axis, keepdims=True)
    return (x - m) / jnp.sqrt(v + eps)

def _scatter_add(tgt, idx, src, axis=0):
    return tgt.at[idx].add(src)

def _segment_sum(src, seg, n):
    return jax.ops.segment_sum(src, seg, n)
kernel_name = 'mk_hybrid_d2_jaxref_r8_9ff8ad'

def setup_inputs(seed: int=0):
    np.random.seed(seed)
    _w = jnp.asarray

    def _L0_attn_a_setup():
        import jax, jax.numpy as jnp
        import numpy as np
        B, N, D = (4, 512, 128)
        H, F = (16, 32)
        HD = D // H
        EPS_ATTN = 1e-08
        EPS_LN = 1e-05

        def _layernorm(x, gamma, beta):
            mu = jnp.mean(x, axis=-1, keepdims=True)
            var = jnp.var(x, axis=-1, keepdims=True)
            return (x - mu) * jax.lax.rsqrt(var + EPS_LN) * gamma + beta
        key = jax.random.key(seed)
        ks = jax.random.split(key, 10)

        def kaiming(k, shape):
            fan_in = shape[1]
            return jax.random.normal(k, shape, jnp.float32) * jnp.sqrt(2.0 / fan_in)
        pm = jax.random.normal(ks[0], (H, HD, F), jnp.float32)
        return {'x': jax.random.normal(ks[1], (B, N, D), jnp.float32), 'proj': pm, 'w_qkv': kaiming(ks[2], (3 * D, D)), 'w_out': kaiming(ks[3], (D, D)), 'b_out': jnp.zeros((D,), jnp.float32), 'gamma': jnp.ones((D,), jnp.float32), 'beta': jnp.zeros((D,), jnp.float32), 'w1': kaiming(ks[4], (4 * D, D)), 'b1': jnp.zeros((4 * D,), jnp.float32), 'w2': kaiming(ks[5], (D, 4 * D)), 'b2': jnp.zeros((D,), jnp.float32)}
    _L0_attn_a_in = _L0_attn_a_setup()

    def _L0_attn_b_setup():
        import jax, jax.numpy as jnp
        import numpy as np
        D_MODEL = 128
        N_HEADS = 16
        D_HEAD = D_MODEL // N_HEADS
        ROPE_BASE = 10000.0

        def _rope_cos_sin(seq_len, dtype):
            inv_freq = 1.0 / ROPE_BASE ** (jnp.arange(0, D_HEAD, 2, dtype=jnp.float32) / D_HEAD)
            t = jnp.arange(seq_len, dtype=jnp.float32)
            freqs = jnp.einsum('t,d->td', t, inv_freq)
            freqs = jnp.concatenate([freqs, freqs], axis=-1)
            return (jnp.cos(freqs).astype(dtype), jnp.sin(freqs).astype(dtype))

        def _rotate_half(x):
            x1, x2 = jnp.split(x, 2, axis=-1)
            return jnp.concatenate([-x2, x1], axis=-1)
        key = jax.random.key(seed)
        k1, k2, k3, k4, k5 = jax.random.split(key, 5)
        std = 0.02 / np.sqrt(2 * 12)
        x = jax.random.normal(k1, (2, 256, D_MODEL), dtype=jnp.float32)
        qkv_w = jax.random.normal(k2, (3 * D_MODEL, D_MODEL), dtype=jnp.float32) * std
        qkv_b = jnp.zeros((3 * D_MODEL,), dtype=jnp.float32)
        proj_w = jax.random.normal(k3, (D_MODEL, D_MODEL), dtype=jnp.float32) * std
        proj_b = jnp.zeros((D_MODEL,), dtype=jnp.float32)
        return {'x': x, 'qkv_w': qkv_w, 'qkv_b': qkv_b, 'proj_w': proj_w, 'proj_b': proj_b}
    _L0_attn_b_in = _L0_attn_b_setup()

    def _L0_ffn_setup():
        import jax, jax.numpy as jnp
        import numpy as np
        IN_DIM, OUT_DIM, N_PROTO, RANK = (128, 128, 32, 16)
        key = jax.random.key(seed)
        ks = jax.random.split(key, 5)
        x = jax.random.normal(ks[0], (2, 512, IN_DIM), dtype=jnp.float32)
        prototypes = jax.random.normal(ks[1], (N_PROTO, IN_DIM), dtype=jnp.float32) * 0.02
        B = jax.random.normal(ks[2], (N_PROTO, RANK, IN_DIM), dtype=jnp.float32) * 0.02
        A = jax.random.normal(ks[3], (N_PROTO, OUT_DIM, RANK), dtype=jnp.float32) * 0.02
        bias = jnp.zeros((N_PROTO, OUT_DIM), dtype=jnp.float32)
        temp = jnp.asarray(1.0, dtype=jnp.float32)
        return {'x': x, 'prototypes': prototypes, 'B': B, 'A': A, 'bias': bias, 'temp': temp}
    _L0_ffn_in = _L0_ffn_setup()

    def _L1_attn_a_setup():
        import jax, jax.numpy as jnp
        from jax import lax
        import numpy as np
        D_MODEL = 128
        K = 32
        K_Q = 4
        N_ANCHOR = 4
        N_DECAY = K - N_ANCHOR
        M = 8
        KS = 4
        H = D_MODEL // K
        N_REP = K // K_Q
        DIM_K = D_MODEL
        DIM_DECAY = K
        DIM_Q = K_Q * H * M * 2
        TOTAL = DIM_K + DIM_DECAY + DIM_Q
        B, L = (2, 256)
        key = jax.random.key(seed)
        ks = jax.random.split(key, 8)
        x = jax.random.normal(ks[0], (B, L, D_MODEL), jnp.float32)
        W_in = jax.random.normal(ks[1], (D_MODEL, TOTAL), jnp.float32) * D_MODEL ** (-0.5)
        conv_k = jax.random.normal(ks[2], (KS, 1, DIM_K + DIM_DECAY), jnp.float32) * 0.3
        grid = np.linspace(-np.pi / 3, np.pi / 3, M)
        theta = jnp.asarray(np.tile(grid.reshape(1, 1, 1, 1, M), (1, 1, K, H, 1)), jnp.float32)
        decay_slopes = jnp.log(jnp.exp(jnp.asarray(np.geomspace(0.001, 0.1, N_DECAY), jnp.float32)) - 1.0)
        anchor_slopes = jnp.log(jnp.exp(jnp.asarray(np.geomspace(0.01, 0.1, N_ANCHOR), jnp.float32)) - 1.0)
        score_scale = jnp.ones((K,), jnp.float32)
        lim = float(np.sqrt(6.0 / (H + H)))
        W_re = jax.random.uniform(ks[3], (H, H), jnp.float32, -lim, lim)
        W_im = jax.random.uniform(ks[4], (H, H), jnp.float32, -lim, lim)
        norm_scale = jnp.ones((2 * H,), jnp.float32)
        W_out = jax.random.normal(ks[5], (D_MODEL, D_MODEL), jnp.float32) * D_MODEL ** (-0.5)
        return dict(x=x, W_in=W_in, conv_k=conv_k, theta=theta, decay_slopes=decay_slopes, anchor_slopes=anchor_slopes, score_scale=score_scale, W_re=W_re, W_im=W_im, norm_scale=norm_scale, W_out=W_out)
    _L1_attn_a_in = _L1_attn_a_setup()

    def _L1_attn_b_setup():
        import jax, jax.numpy as jnp
        import numpy as np
        import math
        B, L, H, D, HID = (2, 128, 16, 64, 128)

        def _rope_tables(seq_len, dim):
            inv_freq = 1.0 / 10000.0 ** (jnp.arange(0, dim, 2, dtype=jnp.float32) / dim)
            t = jnp.arange(seq_len, dtype=jnp.float32)
            freqs = jnp.outer(t, inv_freq)
            emb = jnp.concatenate([freqs, freqs], -1)
            return (jnp.cos(emb), jnp.sin(emb))

        def _rotate_half(x):
            x1, x2 = jnp.split(x, 2, axis=-1)
            return jnp.concatenate([-x2, x1], axis=-1)

        def _apply_rope(x, cos, sin):
            return x * cos + _rotate_half(x) * sin

        def _forward(x, w_qkv, w_o, log_p, log_a, w1, b1, w2, b2):
            Bx, Lx, _ = x.shape
            qkv = jnp.dot(x, w_qkv).reshape(Bx, Lx, 3, H, D)
            qkv = jnp.transpose(qkv, (2, 0, 3, 1, 4))
            q, k, v = (qkv[0], qkv[1], qkv[2])
            cos, sin = _rope_tables(Lx, D)
            cos, sin = (cos[None, None], sin[None, None])
            q = _apply_rope(q, cos, sin)
            k = _apply_rope(k, cos, sin)
            scale = 1.0 / math.sqrt(D)
            scores = jnp.einsum('bhid,bhjd->bhij', q, k) * scale
            pos = jnp.arange(Lx, dtype=jnp.float32)
            dist = jnp.abs(pos[None, :] - pos[:, None])
            p = jax.nn.softplus(log_p)
            a = jax.nn.softplus(log_a)
            kerple = -p * jnp.log1p(a * dist[None])
            attn_t = jnp.transpose(scores, (0, 2, 3, 1))
            kerple_t = jnp.broadcast_to(jnp.transpose(kerple, (1, 2, 0))[None], attn_t.shape)
            combined = jnp.concatenate([attn_t, kerple_t], axis=-1)
            hdn = jax.nn.gelu(jnp.dot(combined, w1) + b1, approximate=False)
            refined = jnp.dot(hdn, w2) + b2
            refined = jnp.transpose(refined, (0, 3, 1, 2))
            scores = scores + kerple[None] + refined
            causal = jnp.tril(jnp.ones((Lx, Lx), dtype=bool))
            scores = jnp.where(causal[None, None], scores, -jnp.inf)
            weights = jax.nn.softmax(scores, axis=-1)
            out = jnp.einsum('bhij,bhjd->bhid', weights, v)
            out = jnp.transpose(out, (0, 2, 1, 3)).reshape(Bx, Lx, H * D)
            return jnp.dot(out, w_o)
        key = jax.random.key(seed)
        ks = jax.random.split(key, 8)
        s = 0.02
        return {'x': jax.random.normal(ks[0], (B, L, HID), jnp.float32), 'w_qkv': jax.random.normal(ks[1], (HID, 3 * H * D), jnp.float32) * s, 'w_o': jax.random.normal(ks[2], (H * D, HID), jnp.float32) * s, 'log_p': jax.random.normal(ks[3], (H, 1, 1), jnp.float32) * 0.02, 'log_a': jax.random.normal(ks[4], (H, 1, 1), jnp.float32) * 0.02, 'w1': jax.random.normal(ks[5], (2 * H, 2 * H), jnp.float32) * s, 'b1': jnp.zeros((2 * H,), jnp.float32), 'w2': jax.random.normal(ks[6], (2 * H, H), jnp.float32) * s, 'b2': jnp.zeros((H,), jnp.float32)}
    _L1_attn_b_in = _L1_attn_b_setup()

    def _L1_ffn_setup():
        import jax, jax.numpy as jnp
        import numpy as np
        ALPHA = 1.0
        key = jax.random.key(seed)
        ks = jax.random.split(key, 7)
        B, S, IN, OUT = (8, 1024, 128, 128)
        RANK, DDIM, UDIM = (4, 100, 50)
        return {'hidden_states': jax.random.normal(ks[0], (B, S, IN), dtype=jnp.float32), 'W': jax.random.normal(ks[1], (OUT, IN), dtype=jnp.float32) * 0.02, 'b': jax.random.normal(ks[2], (OUT,), dtype=jnp.float32) * 0.02, 'lora_down': jax.random.normal(ks[3], (RANK, DDIM), dtype=jnp.float32) * 0.1, 'lora_up': jax.random.normal(ks[4], (UDIM, RANK), dtype=jnp.float32) * 0.1, 'down_aux': jax.random.normal(ks[5], (DDIM, IN), dtype=jnp.float32) * 0.03, 'up_aux': jax.random.normal(ks[6], (OUT, UDIM), dtype=jnp.float32) * 0.03}
    _L1_ffn_in = _L1_ffn_setup()
    _d = {'L0_attn_a_x': _L0_attn_a_in['x'], 'L0_attn_a_proj': _L0_attn_a_in['proj'], 'L0_attn_a_w_qkv': _L0_attn_a_in['w_qkv'], 'L0_attn_a_w_out': _L0_attn_a_in['w_out'], 'L0_attn_a_b_out': _L0_attn_a_in['b_out'], 'L0_attn_a_gamma': _L0_attn_a_in['gamma'], 'L0_attn_a_beta': _L0_attn_a_in['beta'], 'L0_attn_a_w1': _L0_attn_a_in['w1'], 'L0_attn_a_b1': _L0_attn_a_in['b1'], 'L0_attn_a_w2': _L0_attn_a_in['w2'], 'L0_attn_a_b2': _L0_attn_a_in['b2'], 'L0_attn_b_qkv_w': _L0_attn_b_in['qkv_w'], 'L0_attn_b_qkv_b': _L0_attn_b_in['qkv_b'], 'L0_attn_b_proj_w': _L0_attn_b_in['proj_w'], 'L0_attn_b_proj_b': _L0_attn_b_in['proj_b'], 'L0_ffn_prototypes': _L0_ffn_in['prototypes'], 'L0_ffn_B': _L0_ffn_in['B'], 'L0_ffn_A': _L0_ffn_in['A'], 'L0_ffn_bias': _L0_ffn_in['bias'], 'L0_ffn_temp': _L0_ffn_in['temp'], 'L1_attn_a_W_in': _L1_attn_a_in['W_in'], 'L1_attn_a_conv_k': _L1_attn_a_in['conv_k'], 'L1_attn_a_theta': _L1_attn_a_in['theta'], 'L1_attn_a_decay_slopes': _L1_attn_a_in['decay_slopes'], 'L1_attn_a_anchor_slopes': _L1_attn_a_in['anchor_slopes'], 'L1_attn_a_score_scale': _L1_attn_a_in['score_scale'], 'L1_attn_a_W_re': _L1_attn_a_in['W_re'], 'L1_attn_a_W_im': _L1_attn_a_in['W_im'], 'L1_attn_a_norm_scale': _L1_attn_a_in['norm_scale'], 'L1_attn_a_W_out': _L1_attn_a_in['W_out'], 'L1_attn_b_w_qkv': _L1_attn_b_in['w_qkv'], 'L1_attn_b_w_o': _L1_attn_b_in['w_o'], 'L1_attn_b_log_p': _L1_attn_b_in['log_p'], 'L1_attn_b_log_a': _L1_attn_b_in['log_a'], 'L1_attn_b_w1': _L1_attn_b_in['w1'], 'L1_attn_b_b1': _L1_attn_b_in['b1'], 'L1_attn_b_w2': _L1_attn_b_in['w2'], 'L1_attn_b_b2': _L1_attn_b_in['b2'], 'L1_ffn_W': _L1_ffn_in['W'], 'L1_ffn_b': _L1_ffn_in['b'], 'L1_ffn_lora_down': _L1_ffn_in['lora_down'], 'L1_ffn_lora_up': _L1_ffn_in['lora_up'], 'L1_ffn_down_aux': _L1_ffn_in['down_aux'], 'L1_ffn_up_aux': _L1_ffn_in['up_aux']}
    _x0 = _d['L0_attn_a_x']
    _d['L0_attn_a_x'] = jax.random.normal(jax.random.fold_in(jax.random.key(seed), 1), (8, 512, 128), dtype=_x0.dtype)
    del _x0
    return _d

def reference(L0_attn_a_x, L0_attn_a_proj, L0_attn_a_w_qkv, L0_attn_a_w_out, L0_attn_a_b_out, L0_attn_a_gamma, L0_attn_a_beta, L0_attn_a_w1, L0_attn_a_b1, L0_attn_a_w2, L0_attn_a_b2, L0_attn_b_qkv_w, L0_attn_b_qkv_b, L0_attn_b_proj_w, L0_attn_b_proj_b, L0_ffn_prototypes, L0_ffn_B, L0_ffn_A, L0_ffn_bias, L0_ffn_temp, L1_attn_a_W_in, L1_attn_a_conv_k, L1_attn_a_theta, L1_attn_a_decay_slopes, L1_attn_a_anchor_slopes, L1_attn_a_score_scale, L1_attn_a_W_re, L1_attn_a_W_im, L1_attn_a_norm_scale, L1_attn_a_W_out, L1_attn_b_w_qkv, L1_attn_b_w_o, L1_attn_b_log_p, L1_attn_b_log_a, L1_attn_b_w1, L1_attn_b_b1, L1_attn_b_w2, L1_attn_b_b2, L1_ffn_W, L1_ffn_b, L1_ffn_lora_down, L1_ffn_lora_up, L1_ffn_down_aux, L1_ffn_up_aux):

    def _L0_attn_a_ref(x, proj, w_qkv, w_out, b_out, gamma, beta, w1, b1, w2, b2):
        import jax, jax.numpy as jnp
        import numpy as np
        B, N, D = (4, 512, 128)
        H, F = (16, 32)
        HD = D // H
        EPS_ATTN = 1e-08
        EPS_LN = 1e-05

        def _layernorm(x, gamma, beta):
            mu = jnp.mean(x, axis=-1, keepdims=True)
            var = jnp.var(x, axis=-1, keepdims=True)
            return (x - mu) * jax.lax.rsqrt(var + EPS_LN) * gamma + beta
        residual = x
        b, n, d = x.shape
        qkv = x @ w_qkv.T
        q, k, v = jnp.split(qkv, 3, axis=-1)

        def to_heads(t):
            return t.reshape(b, n, H, HD).transpose(0, 2, 1, 3)
        q, k, v = (to_heads(q), to_heads(k), to_heads(v))
        q_f = jax.nn.elu(jnp.einsum('bhnd,hdf->bhnf', q, proj)) + 1.0
        k_f = jax.nn.elu(jnp.einsum('bhnd,hdf->bhnf', k, proj)) + 1.0
        kv = jnp.einsum('bhnf,bhnd->bhfd', k_f, v)
        attn = jnp.einsum('bhnf,bhfd->bhnd', q_f, kv)
        k_sum = jnp.sum(k_f, axis=2)
        z = 1.0 / (jnp.einsum('bhnf,bhf->bhn', q_f, k_sum) + EPS_ATTN)
        attn = attn * z[..., None]
        attn = attn.transpose(0, 2, 1, 3).reshape(b, n, d)
        x = residual + attn @ w_out.T + b_out
        x = _layernorm(x, gamma, beta)
        h = jax.nn.gelu(x @ w1.T + b1, approximate=False)
        x = x + h @ w2.T + b2
        x = _layernorm(x, gamma, beta)
        return x

    def _L0_attn_b_ref(x, qkv_w, qkv_b, proj_w, proj_b):
        import jax, jax.numpy as jnp
        import numpy as np
        D_MODEL = 128
        N_HEADS = 16
        D_HEAD = D_MODEL // N_HEADS
        ROPE_BASE = 10000.0

        def _rope_cos_sin(seq_len, dtype):
            inv_freq = 1.0 / ROPE_BASE ** (jnp.arange(0, D_HEAD, 2, dtype=jnp.float32) / D_HEAD)
            t = jnp.arange(seq_len, dtype=jnp.float32)
            freqs = jnp.einsum('t,d->td', t, inv_freq)
            freqs = jnp.concatenate([freqs, freqs], axis=-1)
            return (jnp.cos(freqs).astype(dtype), jnp.sin(freqs).astype(dtype))

        def _rotate_half(x):
            x1, x2 = jnp.split(x, 2, axis=-1)
            return jnp.concatenate([-x2, x1], axis=-1)
        B, S, D = x.shape
        H, Dh = (N_HEADS, D_HEAD)
        scale = 1.0 / np.sqrt(Dh)
        qkv = x @ qkv_w.T + qkv_b
        qkv = qkv.reshape(B, S, 3, H, Dh)
        q = jnp.transpose(qkv[:, :, 0], (0, 2, 1, 3))
        k = jnp.transpose(qkv[:, :, 1], (0, 2, 1, 3))
        v = jnp.transpose(qkv[:, :, 2], (0, 2, 1, 3))
        cos, sin = _rope_cos_sin(S, x.dtype)
        q = q * cos + _rotate_half(q) * sin
        k = k * cos + _rotate_half(k) * sin
        scores = jnp.einsum('bhsd,bhtd->bhst', q, k) * scale
        causal = jnp.triu(jnp.ones((S, S), dtype=bool), k=1)
        neg = jnp.finfo(scores.dtype).min
        scores = jnp.where(causal[None, None], neg, scores)
        probs = jax.nn.softmax(scores, axis=-1)
        ctx = jnp.einsum('bhst,bhtd->bhsd', probs, v)
        out = jnp.transpose(ctx, (0, 2, 1, 3)).reshape(B, S, D)
        out = out @ proj_w.T + proj_b
        return out

    def _L0_ffn_ref(x, prototypes, B, A, bias, temp):
        import jax, jax.numpy as jnp
        import numpy as np
        IN_DIM, OUT_DIM, N_PROTO, RANK = (128, 128, 32, 16)
        lead = x.shape[:-1]
        xf = x.reshape(-1, IN_DIM)
        x2 = jnp.sum(xf * xf, axis=1, keepdims=True)
        p2 = jnp.sum(prototypes * prototypes, axis=1)
        d2 = x2 + p2[None, :] - 2.0 * (xf @ prototypes.T)
        dists = jnp.sqrt(jnp.maximum(d2, 0.0))
        t = jnp.maximum(jnp.abs(temp), 0.1)
        w = jax.nn.softmax(-dists / t, axis=1)
        topw, topi = jax.lax.top_k(w, 2)
        topw = topw / jnp.sum(topw, axis=1, keepdims=True)
        out = jnp.zeros((xf.shape[0], OUT_DIM), dtype=xf.dtype)
        for tslot in range(2):
            idx = topi[:, tslot]
            wt = topw[:, tslot:tslot + 1]
            h = jnp.einsum('nri,ni->nr', B[idx], xf)
            y = jnp.einsum('nor,nr->no', A[idx], h) + bias[idx]
            out = out + wt * y
        return out.reshape(*lead, OUT_DIM)

    def _L1_attn_a_ref(x, W_in, conv_k, theta, decay_slopes, anchor_slopes, score_scale, W_re, W_im, norm_scale, W_out):
        import jax, jax.numpy as jnp
        from jax import lax
        import numpy as np
        D_MODEL = 128
        K = 32
        K_Q = 4
        N_ANCHOR = 4
        N_DECAY = K - N_ANCHOR
        M = 8
        KS = 4
        H = D_MODEL // K
        N_REP = K // K_Q
        DIM_K = D_MODEL
        DIM_DECAY = K
        DIM_Q = K_Q * H * M * 2
        TOTAL = DIM_K + DIM_DECAY + DIM_Q
        B, L = (2, 256)
        b, l, _ = x.shape
        z = x @ W_in
        z_mem = z[..., :DIM_K + DIM_DECAY]
        q_raw = z[..., DIM_K + DIM_DECAY:]
        zp = jnp.pad(z_mem, ((0, 0), (KS - 1, 0), (0, 0)))
        z_mem = lax.conv_general_dilated(zp, conv_k, window_strides=(1,), padding='VALID', dimension_numbers=('NWC', 'WIO', 'NWC'), feature_group_count=DIM_K + DIM_DECAY)
        k_val = z_mem[..., :DIM_K].reshape(b, l, K, H)
        s_raw = z_mem[..., -K:].reshape(b, l, K, 1)
        q = q_raw.reshape(b, l, K_Q, H, M, 2)
        q_re, q_im = (q[..., 0], q[..., 1])
        pos = jnp.arange(l, dtype=jnp.float32)
        slopes_d = jax.nn.softplus(decay_slopes).reshape(1, 1, N_DECAY, 1)
        dist = jnp.maximum(jnp.float32(l - 1) - pos, 0.0)
        lw_d = -slopes_d * dist[None, :, None, None]
        slopes_a = jax.nn.softplus(anchor_slopes).reshape(1, 1, N_ANCHOR, 1)
        lw_a = -slopes_a * pos[None, :, None, None]
        log_tw = jnp.concatenate([lw_d, lw_a], axis=2)
        log_p = jnp.clip(score_scale[None, None, :, None] * s_raw, -20.0, 20.0)
        p_w = jnp.exp(log_p + log_tw)
        phi = k_val[..., None] * theta
        re_k = jnp.cos(phi)
        im_k = jnp.sin(phi)
        den = jnp.cumsum(p_w[..., 0], axis=1)
        pwb = p_w[..., None]
        num_re = jnp.cumsum(pwb * re_k, axis=1)
        num_im = jnp.cumsum(pwb * im_k, axis=1)
        inv = lax.rsqrt(jnp.maximum(den, 0.0001))
        inv = (inv * inv)[..., None, None]
        s_re = (num_re * inv).reshape(b, l, K_Q, N_REP, H, M)
        s_im = (num_im * inv).reshape(b, l, K_Q, N_REP, H, M)
        qr = q_re.reshape(b, l, K_Q, 1, H, M)
        qi = q_im.reshape(b, l, K_Q, 1, H, M)
        out_re = jnp.sum(s_re * qr + s_im * qi, axis=-1).reshape(b, l, K, H)
        out_im = jnp.sum(s_im * qr - s_re * qi, axis=-1).reshape(b, l, K, H)
        y_re = out_re * norm_scale[:H] * jnp.diagonal(W_re)
        y_im = out_im * norm_scale[H:] * jnp.diagonal(W_im)
        y = jax.nn.silu((y_re + y_im).reshape(b, l, DIM_K))
        return y @ W_out

    def _L1_attn_b_ref(x, w_qkv, w_o, log_p, log_a, w1, b1, w2, b2):
        import jax, jax.numpy as jnp
        import numpy as np
        import math
        B, L, H, D, HID = (2, 128, 16, 64, 128)

        def _rope_tables(seq_len, dim):
            inv_freq = 1.0 / 10000.0 ** (jnp.arange(0, dim, 2, dtype=jnp.float32) / dim)
            t = jnp.arange(seq_len, dtype=jnp.float32)
            freqs = jnp.outer(t, inv_freq)
            emb = jnp.concatenate([freqs, freqs], -1)
            return (jnp.cos(emb), jnp.sin(emb))

        def _rotate_half(x):
            x1, x2 = jnp.split(x, 2, axis=-1)
            return jnp.concatenate([-x2, x1], axis=-1)

        def _apply_rope(x, cos, sin):
            return x * cos + _rotate_half(x) * sin

        def _forward(x, w_qkv, w_o, log_p, log_a, w1, b1, w2, b2):
            Bx, Lx, _ = x.shape
            qkv = jnp.dot(x, w_qkv).reshape(Bx, Lx, 3, H, D)
            qkv = jnp.transpose(qkv, (2, 0, 3, 1, 4))
            q, k, v = (qkv[0], qkv[1], qkv[2])
            cos, sin = _rope_tables(Lx, D)
            cos, sin = (cos[None, None], sin[None, None])
            q = _apply_rope(q, cos, sin)
            k = _apply_rope(k, cos, sin)
            scale = 1.0 / math.sqrt(D)
            scores = jnp.einsum('bhid,bhjd->bhij', q, k) * scale
            pos = jnp.arange(Lx, dtype=jnp.float32)
            dist = jnp.abs(pos[None, :] - pos[:, None])
            p = jax.nn.softplus(log_p)
            a = jax.nn.softplus(log_a)
            kerple = -p * jnp.log1p(a * dist[None])
            attn_t = jnp.transpose(scores, (0, 2, 3, 1))
            kerple_t = jnp.broadcast_to(jnp.transpose(kerple, (1, 2, 0))[None], attn_t.shape)
            combined = jnp.concatenate([attn_t, kerple_t], axis=-1)
            hdn = jax.nn.gelu(jnp.dot(combined, w1) + b1, approximate=False)
            refined = jnp.dot(hdn, w2) + b2
            refined = jnp.transpose(refined, (0, 3, 1, 2))
            scores = scores + kerple[None] + refined
            causal = jnp.tril(jnp.ones((Lx, Lx), dtype=bool))
            scores = jnp.where(causal[None, None], scores, -jnp.inf)
            weights = jax.nn.softmax(scores, axis=-1)
            out = jnp.einsum('bhij,bhjd->bhid', weights, v)
            out = jnp.transpose(out, (0, 2, 1, 3)).reshape(Bx, Lx, H * D)
            return jnp.dot(out, w_o)
        return _forward(x, w_qkv, w_o, log_p, log_a, w1, b1, w2, b2)

    def _L1_ffn_ref(hidden_states, W, b, lora_down, lora_up, down_aux, up_aux):
        import jax, jax.numpy as jnp
        import numpy as np
        ALPHA = 1.0
        lilora_weight = up_aux @ (lora_up @ (lora_down @ down_aux))
        base = jnp.einsum('bsi,oi->bso', hidden_states, W) + b
        delta = jnp.einsum('bsi,oi->bso', hidden_states, lilora_weight)
        return base + ALPHA * delta
    x = L0_attn_a_x
    x = x + _L0_attn_a_ref(_layernorm(x, axis=-1), L0_attn_a_proj, L0_attn_a_w_qkv, L0_attn_a_w_out, L0_attn_a_b_out, L0_attn_a_gamma, L0_attn_a_beta, L0_attn_a_w1, L0_attn_a_b1, L0_attn_a_w2, L0_attn_a_b2)
    x = x + _L0_ffn_ref(_layernorm(x, axis=-1), L0_ffn_prototypes, L0_ffn_B, L0_ffn_A, L0_ffn_bias, L0_ffn_temp)
    x = x + _L0_attn_b_ref(_layernorm(x, axis=-1), L0_attn_b_qkv_w, L0_attn_b_qkv_b, L0_attn_b_proj_w, L0_attn_b_proj_b)
    x = x + _L0_ffn_ref(_layernorm(x, axis=-1), L0_ffn_prototypes, L0_ffn_B, L0_ffn_A, L0_ffn_bias, L0_ffn_temp)
    x = x + _L1_attn_a_ref(_layernorm(x, axis=-1), L1_attn_a_W_in, L1_attn_a_conv_k, L1_attn_a_theta, L1_attn_a_decay_slopes, L1_attn_a_anchor_slopes, L1_attn_a_score_scale, L1_attn_a_W_re, L1_attn_a_W_im, L1_attn_a_norm_scale, L1_attn_a_W_out)
    x = x + _L1_ffn_ref(_layernorm(x, axis=-1), L1_ffn_W, L1_ffn_b, L1_ffn_lora_down, L1_ffn_lora_up, L1_ffn_down_aux, L1_ffn_up_aux)
    x = x + _L1_attn_b_ref(_layernorm(x, axis=-1), L1_attn_b_w_qkv, L1_attn_b_w_o, L1_attn_b_log_p, L1_attn_b_log_a, L1_attn_b_w1, L1_attn_b_b1, L1_attn_b_w2, L1_attn_b_b2)
    x = x + _L1_ffn_ref(_layernorm(x, axis=-1), L1_ffn_W, L1_ffn_b, L1_ffn_lora_down, L1_ffn_lora_up, L1_ffn_down_aux, L1_ffn_up_aux)
    return x

_drawn_inputs = setup_inputs


def setup_inputs(seed=0):
    import zlib

    import numpy as np

    out = dict(_drawn_inputs(seed))
    spreads = {'L0_attn_a_b_out': (0.0, 0.1),
     'L0_attn_a_gamma': (1.0, 0.2),
     'L0_attn_a_beta': (0.0, 0.1),
     'L0_attn_a_b1': (0.0, 0.1),
     'L0_attn_a_b2': (0.0, 0.1),
     'L0_attn_b_qkv_b': (0.0, 0.8),
     'L0_attn_b_proj_b': (0.0, 0.1),
     'L0_ffn_bias': (0.0, 0.1),
     'L1_attn_a_score_scale': (1.0, 0.6),
     'L1_attn_a_norm_scale': (1.0, 0.2),
     'L1_attn_b_b1': (0.0, 2.0),
     'L1_attn_b_b2': (0.0, 2.0)}
    factors = {'L0_attn_b_qkv_w': 8.0,
     'L0_attn_b_proj_w': 8.0,
     'L0_ffn_B': 3.988,
     'L0_ffn_A': 3.941,
     'L1_attn_a_anchor_slopes': 57.128,
     'L1_attn_b_log_p': 64.0,
     'L1_attn_b_log_a': 64.0,
     'L1_attn_b_w1': 64.0,
     'L1_attn_b_w2': 64.0,
     'L1_ffn_b': 9.389,
     'L1_ffn_lora_down': 4.104,
     'L1_ffn_lora_up': 4.019,
     'L1_ffn_down_aux': 3.769,
     'L1_ffn_up_aux': 3.843,
     'L1_attn_b_w_qkv': 5.092,
     'L1_attn_b_w_o': 5.502}
    for name, (base, spread) in spreads.items():
        noise = np.random.default_rng([zlib.crc32(name.encode()), seed]).standard_normal(out[name].shape)
        drawn = base * np.exp(spread * noise) if base else spread * noise
        out[name] = jnp.asarray(drawn.astype(out[name].dtype))
    for name, factor in factors.items():
        out[name] = (out[name] * factor).astype(out[name].dtype)
    return out
```

```python
from contextlib import ExitStack

import numpy as np
import concourse.bass as bass
from concourse import mybir

F32 = mybir.dt.float32
BF16 = mybir.dt.bfloat16
U32 = mybir.dt.uint32
ALU = mybir.AluOpType
ACT = mybir.ActivationFunctionType
AX = mybir.AxisListType

P = 128
D = 128
T = 512
TT = T // P
EPS_LN = 1e-5
A_HEADS, A_F = 16, 32
A_HD = D // A_HEADS
A_FEATS = A_HEADS * A_F
A_HIDDEN = 4 * D
EPS_ATTN = 1e-8
N_EXPERT, RANK = 32, 16
B_HEADS = 16
B_HD = D // B_HEADS
B_SCALE = float(1.0 / np.sqrt(B_HD))
C_K, C_KQ, C_ANCHOR, C_M, C_TAPS = 32, 4, 4, 8, 4
C_H = D // C_K
C_CHUNKS = C_K * C_H * C_M // P
MAGIC = 1.5 * 2.0 ** 23
TWO_PI = 6.283185
HALF_PI = 1.5707963
E_HEADS, E_HD = 16, 64
E_CH = 2 * E_HEADS
QROWS = P // E_HEADS
STEP = 32
TABLE = T + STEP
GROUPS = P // QROWS
E_SCALE = 1.0 / 8.0
MASKED = -1e30

PARTS = {
    "a": [("a_qkv", 3 * D), ("a_features", A_FEATS), ("a_out", D), ("a_w1", A_HIDDEN), ("a_w2", A_HIDDEN),
          ("a_gamma", D), ("a_beta", D), ("a_b1", 4), ("identity", P), ("a_kv_mask", 4 * P)],
    "f": [("f_proto", N_EXPERT), ("f_down", N_EXPERT * RANK), ("f_up", 4 * D), ("f_bias", D), ("f_temp", 1),
          ("expert_no", N_EXPERT), ("f_spread", N_EXPERT * RANK)],
    "b": [("b_q", D), ("b_qrot", D), ("b_k", D), ("b_krot", D), ("b_v", D), ("b_bias", 4), ("b_out", D),
          ("b_cos", T), ("b_sin", T)],
    "c": [("c_key", D), ("c_decay", D), ("c_taps_key", C_TAPS), ("c_taps_decay", C_TAPS), ("c_score_scale", 1),
          ("softplus_in", 3), ("c_theta", C_CHUNKS * P), ("c_qre", C_KQ * P), ("c_qim", C_KQ * P),
          ("c_out", D),
          ("c_steps", T), ("c_spread", C_CHUNKS * P), ("c_gather", C_CHUNKS * P)],
    "d": [("causal_mask", P), ("c_norm", 2 * P), ("c_diag", 2 * P), ("d_w", D), ("d_lora_down", 4), ("d_down_aux", D), ("d_lora_up", 50), ("d_up_aux", D)],
    "e": [("e_out", 8 * D), ("e_mix_scores", 2 * P), ("e_mix_kerple", 2 * P), ("e_mix_back", 2 * P),
          ("e_b1", 1), ("e_b2", 1), ("e_cos", T), ("e_sin", T), ("e_dist", TABLE), ("e_mask", TABLE)],
}
WIDTH = {g: sum(n for _, n in parts) for g, parts in PARTS.items()}
ROWS = [("ones", P), ("a_bo", D), ("a_b2", D), ("b_bv", D), ("b_bo", D), ("d_b", D)]
ROW_WIDTH = sum(n for _, n in ROWS)
SETUP_KERPLE, SETUP_DVE = 19, 24
E_PROJ = 5 * E_HEADS * E_HD


def build(nc, x, w_a, w_f, w_b, w_c, w_d, w_e, w_proj, rows, out, last=8):
    B = x.shape[0]
    weights_in = dict(a=w_a, f=w_f, b=w_b, c=w_c, d=w_d, e=w_e)
    ctx = ExitStack()
    with ctx:
        def sb(name, cols, dt=F32, parts=P):
            shape = [parts] + (list(cols) if type(cols) in (tuple, list) else [cols])
            return ctx.enter_context(nc.sbuf_tensor(name, shape, dt))

        def sem(name):
            return ctx.enter_context(nc.semaphore(name))

        W, weight_tiles = {}, {}
        ARENA = 4096 * 2 + 8192
        arena = sb("arena", ARENA)
        for g, parts in PARTS.items():
            tile = weight_tiles[g] = arena[:, ARENA - WIDTH[g]:] if g == "d" else sb(f"weights_{g}", WIDTH[g])
            at = 0
            for name, n in parts:
                W[name] = tile[:, at:at + n]
                at += n
        row_tile = sb("rows", ROW_WIDTH, parts=1)
        R, at = {}, 0
        for name, n in ROWS:
            R[name] = row_tile[0:1, at:at + n]
            at += n
        ident = W["identity"]
        mask_tile = sb("mask_and_identity_bf16", 2 * P, BF16)
        causal_mask, ident_bf = mask_tile[:, 0:P], mask_tile[:, P:2 * P]

        f_proto2 = sb("f_proto_squared", N_EXPERT)
        f_p2 = sb("f_proto_norm2", N_EXPERT)
        f_negtinv = sb("f_minus_inverse_temperature", 1)
        small = sb("prologue_small", 16)
        c_logdecay = W["c_steps"]
        d_weight = sb("d_weight", D)
        e_kerple = W["e_dist"]
        e_bias_table = W["e_mask"]
        e_hidden_table = sb("e_hidden_table", (2, TABLE))
        const = sb("constants", 8)
        half_pi, one_col, neg_half = const[:, 0:1], const[:, 1:2], const[:, 2:6]

        X = sb("x", (TT, D))
        XN = sb("x_normed", (TT, D))
        XT = sb("x_normed_feature", T)
        stats = sb("bn_stats", (TT, 6))
        mv = sb("mean_var", (TT, 2))
        varp = sb("var_plus_eps", TT)
        rstd = sb("rstd", TT)
        v_aug = sb("a_values_and_one", (TT, D + 1))
        b_val = sb("b_values_and_one", (TT, B_HEADS, B_HD + 1))
        V = sb("e_values_and_one", (TT, E_HEADS, E_HD + 1))
        tmp = sb("tmp", (4, T))
        mx = sb("row_max", 16)
        negmx = sb("minus_row_max", 16)
        FREG = sb("mixed_scores", (GROUPS, T))
        proj = FREG[:, :, :].rearrange("p g j -> p (g j)")[:, 0:E_PROJ]

        def carve():
            at = [0]

            def take(*shape):
                n = int(np.prod(shape))
                v = arena[:, at[0]:at[0] + n]
                at[0] += n
                assert at[0] <= ARENA
                if len(shape) == 2:
                    v = v.rearrange("p (a b) -> p a b", a=shape[0])
                if len(shape) == 3:
                    v = v.rearrange("p (a b c) -> p a b c", a=shape[0], b=shape[1])
                return v
            return take
        t = carve()
        a_qT, a_kT, a_qf, a_kf = t(T), t(T), t(4, T), t(TT, A_FEATS)
        a_kvbd, a_zbd, a_attn, a_z = t(4, P), t(4, P), t(T), t(T)
        a_r, a_hT, a_y = t(TT, D), t(4, T), t(TT, D)
        t = carve()
        f_xx, f_d, f_top, f_idx, f_idxf = t(TT), t(TT, N_EXPERT), t(TT, 8), t(TT, 8), t(TT, 8)
        f_w, f_gate, f_gateT, f_h, f_sq = t(8, TT), t(2 * TT, N_EXPERT), t(T), t(4, T), t(TT, D)
        t = carve()
        b_q, b_k, b_qs, b_ks = t(T), t(T), t(4, T), t(4, T)
        b_p, b_pT, b_rs, b_o, b_oT = t(4, T), t(2, T), t(16), t(TT, D), t(T)
        t = carve()
        c_z, c_conv, c_pw, c_inv, c_y = t(2, T + 4), t(2, T), t(T), t(T), t(T)
        c_rr, c_ff, c_re, c_im, c_pr, c_pi = t(2, T), t(2, T), t(2, T), t(2, T), t(2, T), t(2, T)
        c_nr, c_ni = t(2, T), t(2, T)
        t = carve()
        QT, KT, S = t(8, T), t(8, T), t(E_HEADS, T)
        PT = S.rearrange("p a b -> p (a b)").rearrange("p (jb i h) -> p jb i h", jb=TT, h=E_HEADS)
        e_hidden = sb("e_hidden", (2, 2, T))
        e_o, e_oT = (tmp[:, j:j + 2, :].rearrange("p a b -> p (a b)") for j in (0, 2))
        e_rs = sb("e_row_sum_inverse", 16)

        PS = ctx.enter_context(nc.psum_tensor("banks", [P, 8, 512], F32))

        rows_loaded = sem("rows_loaded")
        w_loaded = {g: sem(f"w_{g}_loaded") for g in PARTS}
        sequence_go = sem("sequence_go")
        setup_act = sem("setup_act")
        setup_dve = sem("setup_dve")
        setup_pe = sem("setup_pe")
        setup_pool = sem("setup_pool")

        cleared = []

        def seq_sem(name):
            cleared.append(sem(name))
            return cleared[-1]
        sequence_ended = seq_sem("sequence_ended")
        x_loaded = seq_sem("x_loaded")
        out_stored = seq_sem("out_stored")
        dve_step = seq_sem("dve_step")
        act_step = seq_sem("act_step")
        pool_step = seq_sem("pool_step")
        ln_var = seq_sem("ln_var")
        ln_rstd = seq_sem("ln_rstd")
        tr_in = seq_sem("tr_in")
        tr_psum = seq_sem("tr_psum")
        xT_ready = seq_sem("xT_ready")
        y_psum = seq_sem("y_psum")
        x_done = seq_sem("x_done")
        a_proj, a_qk, a_v = seq_sem("a_proj"), seq_sem("a_qk"), seq_sem("a_v")
        a_fpre, a_neg, a_exp, a_feat = seq_sem("a_fpre"), seq_sem("a_neg"), seq_sem("a_exp"), seq_sem("a_feat")
        a_kv, a_masked, a_att, a_attn_ready = seq_sem("a_kv"), seq_sem("a_masked"), seq_sem("a_att"), seq_sem("a_attn")
        a_h, a_gelu = seq_sem("a_h"), seq_sem("a_gelu")
        f_xp, f_xxd, f_d2, f_dist = seq_sem("f_xp"), seq_sem("f_xxd"), seq_sem("f_d2"), seq_sem("f_dist")
        f_diff, f_e2, f_gated = seq_sem("f_diff"), seq_sem("f_e2"), seq_sem("f_gated")
        f_gT, f_gTs, f_hp, f_hs, f_gh = seq_sem("f_gT"), seq_sem("f_gTs"), seq_sem("f_hp"), seq_sem("f_hs"), seq_sem("f_gh")
        b_proj, b_vs, b_rope = seq_sem("b_proj"), seq_sem("b_vs"), seq_sem("b_rope")
        b_spread = seq_sem("b_spread")
        b_sc, b_max, b_exp, b_tp = seq_sem("b_sc"), seq_sem("b_max"), seq_sem("b_exp"), seq_sem("b_tp")
        b_ptc = [seq_sem("b_ptc_dve"), seq_sem("b_ptc_act")]
        b_pv, b_od, b_ot, b_ots = seq_sem("b_pv"), seq_sem("b_od"), seq_sem("b_ot"), seq_sem("b_ots")
        c_zp, c_zs, c_cv, c_lp, c_pws = seq_sem("c_zp"), seq_sem("c_zs"), seq_sem("c_cv"), seq_sem("c_lp"), seq_sem("c_pws")
        c_up, c_mag, c_frac, c_trig = seq_sem("c_up"), seq_sem("c_mag"), seq_sem("c_frac"), seq_sem("c_trig")
        c_pwx, c_ab, c_prod, c_sum = seq_sem("c_pwx"), seq_sem("c_ab"), seq_sem("c_prod"), seq_sem("c_sum")
        c_query, c_weighted = seq_sem("c_query"), seq_sem("c_weighted")
        c_norm, c_silu = seq_sem("c_norm"), seq_sem("c_silu")
        e_w, e_qk, e_rope, e_add = seq_sem("e_w"), seq_sem("e_qk"), seq_sem("e_rope"), seq_sem("e_add")
        e_vp, e_vs, e_sc, e_evac = seq_sem("e_vp"), seq_sem("e_vs"), seq_sem("e_sc"), seq_sem("e_evac")
        e_dma = [seq_sem(f"e_dma{q}") for q in range(4)]
        e_zero = seq_sem("e_zero")
        e_m1, e_hadd, e_gelu, e_m2 = seq_sem("e_m1"), seq_sem("e_hadd"), seq_sem("e_gelu"), seq_sem("e_m2")
        e_fk, e_fin, e_nmx, e_exp = seq_sem("e_fk"), seq_sem("e_fin"), seq_sem("e_nmx"), seq_sem("e_exp")
        e_tp, e_ptc, e_pv, e_on = seq_sem("e_tp"), seq_sem("e_ptc"), seq_sem("e_pv"), seq_sem("e_on")
        e_ot, e_ots, e_y, e_x = seq_sem("e_ot"), seq_sem("e_ots"), seq_sem("e_y"), seq_sem("e_x")

        def width(ib, g):
            return P * ib + STEP * (g // 4 + 1)

        def table_at(ib, g):
            return T - 1 - (P * ib + QROWS * g)

        PV_BANKS = [(0, 0, 7), (1, 7, 14), (6, 14, 16)]

        block = ctx.enter_context(nc.Block())


        @block.sync
        def _(sp):
            sp.dma_start(row_tile[:, :], rows[:, :]).then_inc(rows_loaded, 16)
            for g in PARTS:
                sp.dma_start(weight_tiles[g][:, :], weights_in[g][:, :]).then_inc(w_loaded[g], 16)
            with sp.Fori(0, B) as b:
                sp.dma_start(X[:, :, :], x[bass.ds(b, 1)].rearrange("o (t p) d -> p (o t) d", p=P)).then_inc(x_loaded, 16)
                sp.dma_start(proj, w_proj[:, :]).then_inc(e_w, 16)
                if last >= 3:
                    sp.wait_ge(b_rope, 2)
                    for dd in range(B_HD):
                        for src, dst in ((b_q, b_qs), (b_k, b_ks)):
                            sp.dma_start(dst[dd::32, :, :], src[16 * dd:16 * dd + 16, :]).then_inc(b_spread, 16)
                if last >= 7:
                    for ib in range(TT):
                        sp.wait_ge(e_evac, 16 * (ib + 1))
                        if ib == 0:
                            sp.wait_ge(e_qk, 16)
                            sp.wait_ge(e_vp, 8)
                        else:
                            sp.wait_ge(e_tp, 4 * sum(range(1, ib + 1)))
                        for g in range(GROUPS):
                            n = width(ib, g)
                            sp.dma_start(FREG[:, g, 0:n],
                                         S[QROWS * g:QROWS * (g + 1), :, 0:n]).then_inc(e_dma[g // 4], 16)
                sp.wait_ge(x_done, 1)
                sp.dma_start(out[bass.ds(b, 1)].rearrange("o (t p) d -> p (o t) d", p=P), X[:, :, :]).then_inc(out_stored, 16)
                sp.wait_ge(out_stored, 16)
                sp.wait_ge(e_w, 16)
                sp.wait_ge(sequence_ended, 4)
                for s in cleared:
                    sp.sem_clear(s)
                sp.sem_inc(sequence_go, 1)

        @block.gpsimd
        def _(pool):
            def settle(ins):
                pool_count[0] += 1
                ins.then_inc(pool_step, 1)
                pool.wait_ge(pool_step, pool_count[0])

            pool_count = [0]
            nc.gpsimd.memset(half_pi, HALF_PI).then_inc(setup_pool, 1)
            nc.gpsimd.memset(one_col, 1.0).then_inc(setup_pool, 1)
            nc.gpsimd.memset(neg_half, -0.5).then_inc(setup_pool, 1)
            nc.gpsimd.memset(const[:, 6:7], 0.5).then_inc(setup_pool, 1)
            nc.gpsimd.memset(v_aug[:, :, D:D + 1], 1.0).then_inc(setup_pool, 1)
            nc.gpsimd.memset(b_val[:, :, :, B_HD:B_HD + 1], 1.0).then_inc(setup_pool, 1)
            nc.gpsimd.memset(V[:, :, :, E_HD:E_HD + 1], 1.0).then_inc(setup_pool, 1)
            pool.wait_ge(setup_pool, 7)

            def ln(k):
                pool.wait_ge(ln_var, k + 1)
                nc.gpsimd.tensor_tensor(rstd[:, :], varp[:, :], neg_half, ALU.pow).then_inc(ln_rstd, 1)

            def mixture(k, ln_no):
                ln(ln_no)
                pool.wait_ge(f_d2, k + 1)
                d = f_d.rearrange("p t e -> p (t e)")
                nc.gpsimd.tensor_tensor(d, d, const[:, 6:7].to_broadcast([P, TT * N_EXPERT]), ALU.pow).then_inc(f_dist, 1)

            with pool.Fori(0, B) as b:
                pool_count[0] = 0
                for k in range(3):
                    ln(k)
                if last >= 2:
                    mixture(0, 3)
                if last >= 3:
                    ln(4)
                if last >= 4:
                    mixture(1, 5)
                if last >= 5:
                    ln(6)
                if last >= 6:
                    ln(7)
                if last >= 7:
                    ln(8)
                    for n in range(16):
                        pool.wait_ge(e_rope, n + 1)
                        dst = QT if n % 2 == 0 else KT
                        pair = tmp[:, 2 * (n % 2):2 * (n % 2) + 2, :]
                        nc.gpsimd.tensor_tensor(dst[:, n // 2, :], pair[:, 0, :], pair[:, 1, :], ALU.add).then_inc(e_add, 1)
                    for ib in range(TT):
                        if ib == 0:
                            pool.wait_ge(e_qk, 16)
                            pool.wait_ge(e_vp, 8)
                        else:
                            pool.wait_ge(e_tp, 4 * sum(range(1, ib + 1)))
                        for gq in range(3):
                            nc.gpsimd.memset(FREG[:, 4 * gq:4 * gq + 4, width(ib, 4 * gq):P * (ib + 1)], 0.0).then_inc(e_zero, 1)
                        for g in range(GROUPS):
                            n = GROUPS * ib + g
                            w = width(ib, g)
                            pool.wait_ge(e_m1, 2 * (n + 1))
                            f = FREG[:, g, 0:w]
                            nc.gpsimd.tensor_tensor(f, f, e_bias_table[:, table_at(ib, g):table_at(ib, g) + w],
                                                    ALU.add).then_inc(e_fk, 1)
                if last >= 8:
                    ln(9)
                pool.drain().then_inc(sequence_ended, 1)
                pool.wait_ge(sequence_go, b + 1)

        @block.scalar
        def _(act):
            A = nc.scalar.activation
            act_count = [0]

            def settle(ins):
                act_count[0] += 1
                ins.then_inc(act_step, 1)
                act.wait_ge(act_step, act_count[0])

            act.wait_ge(setup_pool, 7)
            act.wait_ge(w_loaded["c"], 16)
            sp_in = W["softplus_in"]
            A(small[:, 0:3], sp_in, ACT.Abs).then_inc(setup_act, 1)
            act.wait_ge(setup_act, 1)
            A(small[:, 3:6], small[:, 0:3], ACT.Exp, scale=-1.0).then_inc(setup_act, 1)
            act.wait_ge(setup_act, 2)
            A(small[:, 6:9], small[:, 3:6], ACT.Ln, bias=one_col).then_inc(setup_act, 1)
            act.wait_ge(w_loaded["e"], 16)
            act.wait_ge(setup_dve, 1)
            A(e_kerple, e_kerple, ACT.Ln, scale=small[:, 11:12], bias=one_col).then_inc(setup_act, 1)
            act.wait_ge(setup_pe, 1)
            A(f_p2[:, :], PS[:, 0, 0:N_EXPERT], ACT.Copy).then_inc(setup_act, 1)
            act.wait_ge(setup_pe, 2)
            A(tmp[0:4, 0, 0:P], PS[0:4, 1, 0:P], ACT.Copy).then_inc(setup_act, 1)
            act.wait_ge(setup_pe, 3)
            A(tmp[0:50, 1, 0:P], PS[0:50, 2, 0:P], ACT.Copy).then_inc(setup_act, 1)

            def feature_layout(k):
                act.wait_ge(tr_psum, k + 1)
                A(XT[:, :], PS[:, 7, :], ACT.Copy).then_inc(xT_ready, 1)

            def linear_attention():
                feature_layout(0)
                act.wait_ge(a_proj, 1)
                A(a_qT, PS[:, 0, :], ACT.Copy).then_inc(a_qk, 1)
                act.wait_ge(a_proj, 2)
                A(a_kT, PS[:, 1, :], ACT.Copy).then_inc(a_qk, 1)
                for n in range(8):
                    act.wait_ge(a_neg, n + 1)
                    A(tmp[:, n % 2, :], tmp[:, n % 2, :], ACT.Exp).then_inc(a_exp, 1)
                feature_layout(1)
                for c in range(4):
                    act.wait_ge(a_h, c + 1)
                    A(a_hT[:, c, :], PS[:, c, :], ACT.Gelu, bias=W["a_b1"][:, c:c + 1]).then_inc(a_gelu, 1)

            def mixture(k, tr):
                act.wait_ge(tr_in, tr + 1)
                for tt in range(TT):
                    A(f_sq[:, tt, :], XN[:, tt, :], ACT.Square, accum_out=f_xx[:, tt:tt + 1]).then_inc(f_xxd, 1)
                feature_layout(tr)
                act.wait_ge(f_diff, k + 1)
                A(f_w[:, 1, :], f_w[:, 0, :], ACT.Exp).then_inc(f_e2, 1)
                act.wait_ge(f_gT, k + 1)
                A(f_gateT[0:N_EXPERT, :], PS[0:N_EXPERT, 1, :], ACT.Copy).then_inc(f_gTs, 1)
                for c in range(4):
                    act.wait_ge(f_hp, 4 * k + c + 1)
                    A(f_h[:, c, :], PS[:, 2 + c % 2, :], ACT.Copy).then_inc(f_hs, 1)

            def causal_attention():
                feature_layout(3)
                act.wait_ge(b_proj, 3)
                A(b_val[:, :, :, 0:B_HD], PS[:, 4, :].rearrange("p (t h d) -> p t h d", t=TT, h=B_HEADS),
                  ACT.Copy).then_inc(b_vs, 1)
                for n in range(64):
                    ib, h = n // 16, n % 16
                    w = P * (ib + 1)
                    if h % 2 == 0:
                        act.wait_ge(b_max, n // 2 + 1)
                    if n >= 4:
                        act.wait_ge(b_tp, n - 3)
                    A(b_p[:, n % 4, 0:w], PS[:, n % 4, 0:w], ACT.Exp, scale=B_SCALE,
                      bias=negmx[:, 4 * (n // 2 % 2) + n % 2:4 * (n // 2 % 2) + n % 2 + 1]).then_inc(b_exp, 1)
                    if n % 2 == 1 and n >= 3:
                        copy_pT(n - 2)
                copy_pT(63)
                act.wait_ge(b_ot, 1)
                A(b_oT, PS[:, 4, :], ACT.Copy).then_inc(b_ots, 1)

            def copy_pT(m):
                w = P * (m // 16 + 1)
                act.wait_ge(b_tp, m + 1)
                if m >= 2:
                    act.wait_ge(b_pv, m - 1)
                A(b_pT[:, 1, 0:w], PS[:, 5, 0:w], ACT.Copy).then_inc(b_ptc[1], 1)

            def phase_memory():
                feature_layout(5)
                for j in range(2):
                    act.wait_ge(c_zp, j + 1)
                    A(c_z[:, j, 0:3], const[:, 0:3], ACT.Copy, scale=0.0).then_inc(c_zs, 1)
                    A(c_z[:, j, 3:3 + T], PS[:, j, :], ACT.Copy).then_inc(c_zs, 1)
                act.wait_ge(c_lp, 1)
                A(c_pw, c_pw, ACT.Exp).then_inc(c_pws, 1)
                for c in range(C_CHUNKS):
                    act.wait_ge(c_up, c + 1)
                    if c >= 2:
                        act.wait_ge(c_frac, c - 1)
                    A(c_rr[:, c % 2, :], PS[:, c % 2, :], ACT.Copy, bias=MAGIC).then_inc(c_mag, 1)
                    act.wait_ge(c_frac, c + 1)
                    if c >= 2:
                        act.wait_ge(c_prod, 2 * (c - 1))
                    A(c_im[:, c % 2, :], c_ff[:, c % 2, :], ACT.Sin, scale=-TWO_PI).then_inc(c_trig, 1)
                    A(c_re[:, c % 2, :], c_ff[:, c % 2, :], ACT.Abs).then_inc(c_ab, 1)
                    act.wait_ge(c_ab, c + 1)
                    A(c_re[:, c % 2, :], c_re[:, c % 2, :], ACT.Sin, scale=-TWO_PI, bias=half_pi).then_inc(c_trig, 1)
                act.wait_ge(c_norm, 1)
                A(c_y, c_y, ACT.Silu).then_inc(c_silu, 1)

            def mixed_attention():
                feature_layout(7)
                for r in range(8):
                    act.wait_ge(e_vp, r + 1)
                    A(V[:, r // 2, 8 * (r % 2):8 * (r % 2) + 8, 0:E_HD],
                      PS[:, 4 + r % 2, :].rearrange("p (h d) -> p h d", h=8), ACT.Copy).then_inc(e_vs, 1)
                for ib in range(TT):
                    w = P * (ib + 1)
                    if ib:
                        act.wait_ge(e_pv, 3 * ib)
                    for h in range(E_HEADS):
                        act.wait_ge(e_sc, 16 * ib + h + 1)
                        A(S[:, h, 0:w], PS[:, h % 2, 0:w], ACT.Copy, scale=E_SCALE).then_inc(e_evac, 1)
                    for g in range(GROUPS):
                        n = GROUPS * ib + g
                        act.wait_ge(e_hadd, 2 * n + 2)
                        hid = e_hidden[:, n % 2, :, 0:width(ib, g)]
                        A(hid, hid, ACT.Gelu).then_inc(e_gelu, 1)
                    act.wait_ge(e_nmx, ib + 1)
                    for g in range(GROUPS):
                        f = FREG[:, g, 0:width(ib, g)]
                        A(f, f, ACT.Exp, bias=negmx[:, g:g + 1]).then_inc(e_exp, 1)
                    for j in range(2):
                        act.wait_ge(e_ot, 2 * ib + j + 1)
                        A(e_oT[:, 512 * j:512 * (j + 1)], PS[:, 2 + j, :], ACT.Copy).then_inc(e_ots, 1)

            with act.Fori(0, B) as b:
                act_count[0] = 0
                linear_attention()
                if last >= 2:
                    mixture(0, 2)
                if last >= 3:
                    causal_attention()
                if last >= 4:
                    mixture(1, 4)
                if last >= 5:
                    phase_memory()
                if last >= 6:
                    feature_layout(6)
                if last >= 7:
                    mixed_attention()
                if last >= 8:
                    feature_layout(8)
                act.drain().then_inc(sequence_ended, 1)
                act.wait_ge(sequence_go, b + 1)

        @block.vector
        def _(dve):
            V_ = nc.vector
            count = [0]

            def settle(ins):
                count[0] += 1
                ins.then_inc(dve_step, 1)
                dve.wait_ge(dve_step, count[0])

            done = [0]

            def setup(ins):
                done[0] += 1
                ins.then_inc(setup_dve, 1)
                dve.wait_ge(setup_dve, done[0])
            dve.wait_ge(w_loaded["c"], 16)
            dve.wait_ge(w_loaded["d"], 16)
            dve.wait_ge(w_loaded["e"], 16)
            dve.wait_ge(setup_act, 3)
            setup(V_.scalar_tensor_tensor(small[:, 9:12], W["softplus_in"], 0.0, small[:, 6:9], ALU.max, ALU.add))
            setup(V_.tensor_scalar(c_logdecay, c_logdecay, small[:, 9:10], -1.0, ALU.mult, ALU.mult))
            setup(V_.tensor_scalar(W["c_theta"], W["c_theta"], float(1.0 / (2.0 * np.pi)), None, ALU.mult))
            setup(V_.tensor_tensor(W["c_norm"], W["c_norm"], W["c_diag"], ALU.mult))
            c1, c2 = (W["c_norm"][:, j * P:(j + 1) * P].unsqueeze(1).to_broadcast([P, C_KQ, P]) for j in range(2))
            qre, qim = (W[n].rearrange("p (k n) -> p k n", k=C_KQ) for n in ("c_qre", "c_qim"))
            t1, t2, t3, t4 = (tmp[:, j, :].rearrange("p (k n) -> p k n", k=C_KQ) for j in range(4))
            for dst, q, c in ((t1, qre, c1), (t2, qim, c2), (t3, qim, c1), (t4, qre, c2)):
                setup(V_.tensor_tensor(dst, q, c, ALU.mult))
            setup(V_.tensor_tensor(qre, t1, t2, ALU.subtract))
            setup(V_.tensor_tensor(qim, t3, t4, ALU.add))
            dve.wait_ge(w_loaded["f"], 16)
            setup(V_.tensor_tensor(f_proto2[:, :], W["f_proto"], W["f_proto"], ALU.mult))
            setup(V_.tensor_scalar(small[:, 12:13], W["f_temp"], -1.0, None, ALU.mult))
            setup(V_.tensor_tensor(small[:, 12:13], small[:, 12:13], W["f_temp"], ALU.max))
            setup(V_.tensor_scalar(small[:, 12:13], small[:, 12:13], 0.1, -1.0, ALU.max, ALU.mult))
            setup(V_.reciprocal(f_negtinv[:, :], small[:, 12:13]))
            dve.wait_ge(setup_pe, 4)
            setup(V_.tensor_tensor(d_weight[:, :], PS[:, 3, 0:D], W["d_w"], ALU.add))
            dve.wait_ge(w_loaded["a"], 16)
            setup(V_.tensor_copy(causal_mask, W["causal_mask"]))
            setup(V_.tensor_copy(ident_bf, ident))
            dve.wait_ge(setup_act, 4)
            setup(V_.tensor_scalar(e_kerple, e_kerple, small[:, 10:11], -1.0, ALU.mult, ALU.mult))
            KERPLE_READY = done[0]
            setup(V_.scalar_tensor_tensor(e_bias_table, e_kerple, W["e_b2"], e_bias_table, ALU.add, ALU.add))
            for half in range(2):
                dve.wait_ge(setup_pe, 5 + half)
                setup(V_.tensor_scalar(e_hidden_table[:, half, 0:512], PS[:, 4 + half, :], W["e_b1"], None, ALU.add))
                setup(V_.tensor_scalar(e_hidden_table[:, half, 512:TABLE], PS[:, 6 + half, 0:STEP], W["e_b1"], None, ALU.add))
            assert KERPLE_READY == SETUP_KERPLE and done[0] == SETUP_DVE

            def ln_stats(k, src):
                for tt in range(TT):
                    ins = V_.bn_stats(stats[:, tt, :], src[:, tt, :])
                settle(ins)
                for tt in range(TT):
                    ins = V_.bn_aggr(mv[:, tt, :], stats[:, tt, :])
                settle(ins)
                V_.tensor_scalar(varp[:, :], mv[:, :, 1], EPS_LN, None, ALU.add).then_inc(ln_var, 1)
                dve.wait_ge(ln_rstd, k + 1)

            def normalise(dst, src):
                for tt in range(TT):
                    ins = V_.tensor_scalar(dst[:, tt, :], src[:, tt, :], mv[:, tt, 0:1], rstd[:, tt:tt + 1],
                                           ALU.subtract, ALU.mult)
                return ins

            def layer_norm(k):
                ln_stats(k, X)
                normalise(XN, X).then_inc(tr_in, 1)

            def add_y(y_no):
                dve.wait_ge(y_psum, y_no)
                settle(V_.tensor_tensor(X[:, :, :], PS[:, 6, :].rearrange("p (t d) -> p t d", t=TT), X[:, :, :], ALU.add))

            def scaled_and_shifted(buf):
                for name, op in (("a_gamma", ALU.mult), ("a_beta", ALU.add)):
                    row = W[name].unsqueeze(1).to_broadcast([P, TT, D])
                    ins = V_.tensor_tensor(buf, buf, row, op)
                    if name == "a_gamma":
                        settle(ins)
                return ins

            def linear_attention():
                layer_norm(0)
                dve.wait_ge(tr_in, 1)
                dve.wait_ge(a_proj, 3)
                V_.tensor_copy(v_aug[:, :, 0:D], PS[:, 2, :].rearrange("p (t d) -> p t d", t=TT)).then_inc(a_v, 1)
                feats = [a_qf[:, c, :] for c in range(4)] + [a_kf[:, c, :] for c in range(4)]
                for n in range(9):
                    if n < 8:
                        dve.wait_ge(a_fpre, n + 1)
                        if n >= 2:
                            dve.wait_ge(a_feat, n - 1)
                        V_.tensor_scalar(tmp[:, n % 2, :], PS[:, 3 + n % 3, :], 0.0, None, ALU.min).then_inc(a_neg, 1)
                    if n >= 1:
                        m = n - 1
                        dve.wait_ge(a_exp, m + 1)
                        V_.scalar_tensor_tensor(feats[m], PS[:, 3 + m % 3, :], 0.0, tmp[:, m % 2, :],
                                                ALU.max, ALU.add).then_inc(a_feat, 1)
                mask = W["a_kv_mask"].rearrange("p (c n) -> p c n", c=4)
                for c in range(4):
                    dve.wait_ge(a_kv, 2 * (c // 2) + 2)
                    at = (c % 2) * (D + 1)
                    V_.tensor_tensor(a_kvbd[:, c, :], PS[:, c // 2, at:at + D], mask[:, c, :], ALU.mult).then_inc(a_masked, 1)
                    V_.tensor_scalar(a_zbd[:, c, :], mask[:, c, :], PS[:, c // 2, at + D:at + D + 1], None, ALU.mult).then_inc(a_masked, 1)
                dve.wait_ge(a_att, 2)
                settle(V_.tensor_scalar(a_z, PS[:, 3, :], EPS_ATTN, None, ALU.add))
                settle(V_.reciprocal(a_z, a_z))
                V_.tensor_tensor(a_attn, PS[:, 2, :], a_z, ALU.mult).then_inc(a_attn_ready, 1)
                dve.wait_ge(y_psum, 1)
                settle(V_.tensor_tensor(a_r, PS[:, 6, :].rearrange("p (t d) -> p t d", t=TT), XN[:, :, :], ALU.add))
                ln_stats(1, a_r)
                settle(normalise(a_r, a_r))
                scaled_and_shifted(a_r).then_inc(tr_in, 1)
                dve.wait_ge(tr_in, 2)
                dve.wait_ge(y_psum, 2)
                settle(V_.tensor_tensor(a_y, PS[:, 6, :].rearrange("p (t d) -> p t d", t=TT), a_r, ALU.add))
                ln_stats(2, a_y)
                settle(normalise(a_y, a_y))
                settle(scaled_and_shifted(a_y))
                settle(V_.tensor_tensor(X[:, :, :], X[:, :, :], a_y, ALU.add))

            def mixture(k, ln_no, y_no):
                layer_norm(ln_no)
                dve.wait_ge(f_xp, k + 1)
                dve.wait_ge(f_xxd, 4 * (k + 1))
                for tt in range(TT):
                    ins = V_.tensor_scalar(f_d[:, tt, :], f_p2[:, :], f_xx[:, tt:tt + 1], None, ALU.add)
                settle(ins)
                settle(V_.scalar_tensor_tensor(f_d, PS[:, 0, 0:TT * N_EXPERT].rearrange("p (t e) -> p t e", t=TT), -2.0,
                                               f_d, ALU.mult, ALU.add))
                V_.tensor_scalar(f_d, f_d, 0.0, None, ALU.max).then_inc(f_d2, 1)
                dve.wait_ge(f_dist, k + 1)
                settle(V_.tensor_scalar(f_d, f_d, f_negtinv[:, :], None, ALU.mult))
                for tt in range(TT):
                    ins = V_.max(f_top[:, tt, :], f_d[:, tt, :])
                settle(ins)
                idx = f_idx.bitcast(U32)
                for tt in range(TT):
                    ins = V_.max_index(idx[:, tt, :], f_top[:, tt, :], f_d[:, tt, :])
                settle(ins)
                V_.tensor_tensor(f_w[:, 0, :], f_top[:, :, 1], f_top[:, :, 0], ALU.subtract).then_inc(f_diff, 1)
                settle(V_.tensor_copy(f_idxf, idx))
                dve.wait_ge(f_e2, k + 1)
                settle(V_.tensor_scalar(f_w[:, 2, :], f_w[:, 1, :], 1.0, None, ALU.add))
                settle(V_.reciprocal(f_w[:, 2, :], f_w[:, 2, :]))
                settle(V_.tensor_tensor(f_w[:, 3, :], f_w[:, 1, :], f_w[:, 2, :], ALU.mult))
                for tt in range(TT):
                    for j in range(2):
                        ins = V_.tensor_scalar(f_gate[:, TT * j + tt, :], W["expert_no"], f_idxf[:, tt, j:j + 1],
                                               f_w[:, 2 + j, tt:tt + 1], ALU.is_equal, ALU.mult)
                settle(ins)
                V_.tensor_tensor(f_gate[:, 0:TT, :], f_gate[:, 0:TT, :], f_gate[:, TT:, :], ALU.add).then_inc(f_gated, 1)
                for c in range(4):
                    dve.wait_ge(f_hs, 4 * k + c + 1)
                    V_.tensor_tensor(f_h[:, c, :], PS[:, 4 + c % 2, :], f_h[:, c, :], ALU.mult).then_inc(f_gh, 1)
                add_y(y_no)

            def causal_attention():
                layer_norm(4)
                for j, dst in enumerate((b_q, b_k)):
                    dve.wait_ge(b_proj, j + 1)
                    bias = W["b_bias"]
                    V_.scalar_tensor_tensor(tmp[:, 0, :], PS[:, 2 * j, :], bias[:, 2 * j:2 * j + 1], W["b_cos"], ALU.add, ALU.mult)
                    settle(V_.scalar_tensor_tensor(tmp[:, 1, :], PS[:, 2 * j + 1, :], bias[:, 2 * j + 1:2 * j + 2],
                                                   W["b_sin"], ALU.add, ALU.mult))
                    V_.tensor_tensor(dst, tmp[:, 0, :], tmp[:, 1, :], ALU.add).then_inc(b_rope, 1)
                    dve.wait_ge(b_rope, j + 1)

                def pair_max(u):
                    w = P * (u // 8 + 1)
                    dve.wait_ge(b_sc, 2 * u + 2)
                    s = 4 * (u % 2)
                    settle(V_.tensor_reduce(mx[:, s:s + 2], PS[:, 2 * (u % 2):2 * (u % 2) + 2, 0:w], AX.X, ALU.max))
                    if u >= 2:
                        dve.wait_ge(b_exp, 2 * u - 2)
                    V_.tensor_scalar(negmx[:, s:s + 2], mx[:, s:s + 2], -B_SCALE, None, ALU.mult).then_inc(b_max, 1)

                pair_max(0)
                for u in range(32):
                    if u < 31:
                        pair_max(u + 1)
                    m = 2 * u
                    w = P * (m // 16 + 1)
                    dve.wait_ge(b_tp, m + 1)
                    if m >= 2:
                        dve.wait_ge(b_pv, m - 1)
                    V_.tensor_copy(b_pT[:, 0, 0:w], PS[:, 4, 0:w]).then_inc(b_ptc[0], 1)
                    if u % 8 == 7:
                        ib = u // 8
                        dve.wait_ge(b_pv, 16 * (ib + 1))
                        o = PS[:, 6 + ib % 2, 0:B_HEADS * (B_HD + 1)].rearrange("p (h d) -> p h d", h=B_HEADS)
                        settle(V_.reciprocal(b_rs, o[:, :, B_HD]))
                        V_.tensor_tensor(b_o[:, ib, :].rearrange("p (h d) -> p h d", h=B_HEADS), o[:, :, 0:B_HD],
                                         b_rs.unsqueeze(2).to_broadcast([P, B_HEADS, B_HD]), ALU.mult).then_inc(b_od, 1)
                add_y(4)

            def phase_memory():
                layer_norm(6)
                taps = [W["c_taps_key"], W["c_taps_decay"]]
                for j in range(2):
                    dve.wait_ge(c_zs, 2 * j + 2)
                    settle(V_.tensor_scalar(c_conv[:, j, :], c_z[:, j, 0:T], taps[j][:, 0:1], None, ALU.mult))
                    for s in range(1, C_TAPS):
                        ins = V_.scalar_tensor_tensor(c_conv[:, j, :], c_z[:, j, s:s + T], taps[j][:, s:s + 1],
                                                      c_conv[:, j, :], ALU.mult, ALU.add)
                        if s < C_TAPS - 1:
                            settle(ins)
                    ins.then_inc(c_cv, 1)
                dve.wait_ge(c_cv, 2)
                settle(V_.tensor_scalar(c_pw, c_conv[:, 1, :], W["c_score_scale"], 20.0, ALU.mult, ALU.min))
                V_.scalar_tensor_tensor(c_pw, c_pw, -20.0, c_logdecay, ALU.max, ALU.add).then_inc(c_lp, 1)
                ones = one_col.to_broadcast([P, T])
                dve.wait_ge(c_pws, 1)
                settle(V_.tensor_tensor_scan(c_inv, ones, c_pw, 0.0, ALU.mult, ALU.add))
                settle(V_.tensor_scalar(c_inv, c_inv, 0.0001, None, ALU.max))
                settle(V_.reciprocal(c_inv, c_inv))
                for c in range(C_CHUNKS):
                    i = c % 2
                    dve.wait_ge(c_mag, c + 1)
                    if c >= 2:
                        dve.wait_ge(c_trig, 2 * (c - 1))
                        dve.wait_ge(c_ab, c - 1)
                    V_.scalar_tensor_tensor(c_ff[:, i, :], c_rr[:, i, :], MAGIC, PS[:, i, :], ALU.subtract, ALU.subtract).then_inc(c_frac, 1)
                    dve.wait_ge(c_trig, 2 * c + 2)
                    dve.wait_ge(c_pwx, c + 1)
                    if c >= 2:
                        dve.wait_ge(c_sum, c - 1)
                    V_.tensor_tensor(c_pr[:, i, :], PS[:, 2 + i, :], c_re[:, i, :], ALU.mult)
                    V_.tensor_tensor(c_pi[:, i, :], PS[:, 2 + i, :], c_im[:, i, :], ALU.mult).then_inc(c_prod, 2)
                    dve.wait_ge(c_prod, 2 * c + 2)
                    V_.tensor_tensor_scan(c_nr[:, i, :], ones, c_pr[:, i, :], 0.0, ALU.mult, ALU.add)
                    settle(V_.tensor_tensor_scan(c_ni[:, i, :], ones, c_pi[:, i, :], 0.0, ALU.mult, ALU.add))
                    dve.wait_ge(c_query, c // 2 + 1)
                    V_.tensor_tensor(c_pr[:, i, :], PS[:, 4, :], c_nr[:, i, :], ALU.mult)
                    V_.tensor_tensor(c_pi[:, i, :], PS[:, 5, :], c_ni[:, i, :], ALU.mult).then_inc(c_weighted, 1)
                dve.wait_ge(c_sum, C_CHUNKS)
                V_.tensor_tensor(c_y, PS[:, 6, :], c_inv, ALU.mult).then_inc(c_norm, 1)
                add_y(6)

            def mixed_attention():
                layer_norm(8)
                for n in range(16):
                    dve.wait_ge(e_qk, n + 1)
                    if n >= 2:
                        dve.wait_ge(e_add, n - 1)
                    k = 2 * (n % 2)
                    V_.tensor_tensor(tmp[:, k, :], PS[:, k, :], W["e_cos"], ALU.mult)
                    V_.tensor_tensor(tmp[:, k + 1, :], PS[:, k + 1, :], W["e_sin"], ALU.mult).then_inc(e_rope, 1)
                for ib in range(TT):
                    def hidden(n):
                        g = n % GROUPS
                        w, at = width(ib, g), table_at(ib, g)
                        for half in range(2):
                            dve.wait_ge(e_m1, 2 * n + half + 1)
                            if half == 0 and n >= 2:
                                dve.wait_ge(e_m2, n - 1)
                            V_.tensor_tensor(e_hidden[:, n % 2, half, 0:w], PS[:, 2 + 2 * (n % 2) + half, 0:w],
                                             e_hidden_table[:, half, at:at + w], ALU.add).then_inc(e_hadd, 1)

                    hidden(GROUPS * ib)
                    for g in range(GROUPS):
                        n = GROUPS * ib + g
                        w = width(ib, g)
                        if g + 1 < GROUPS:
                            hidden(n + 1)
                        dve.wait_ge(e_m2, n + 1)
                        dve.wait_ge(e_fk, n + 1)
                        f = FREG[:, g, 0:w]
                        V_.tensor_tensor_reduce(out=f, in0=PS[:, 6 + n % 2, 0:w], in1=f, scale=1.0, scalar=-3e38,
                                                op0=ALU.add, op1=ALU.max, accum_out=mx[:, g:g + 1]).then_inc(e_fin, 1)
                    dve.wait_ge(e_fin, GROUPS * (ib + 1))
                    V_.tensor_scalar(negmx[:, :], mx[:, :], -1.0, None, ALU.mult).then_inc(e_nmx, 1)
                    first = 4 * sum(range(1, ib + 1))
                    for k in range(4 * (ib + 1)):
                        gq, jb = k // (ib + 1), k % (ib + 1)
                        dve.wait_ge(e_tp, first + k + 1)
                        V_.tensor_copy(PT[:, jb, 32 * gq:32 * gq + 32, :].rearrange("p i h -> p (i h)"),
                                       PS[:, 2 + k % 4, :]).then_inc(e_ptc, 1)
                    for j, (bank, h0, h1) in enumerate(PV_BANKS):
                        dve.wait_ge(e_pv, 3 * ib + j + 1)
                        o = PS[:, bank, 0:(h1 - h0) * (E_HD + 1)].rearrange("p (h d) -> p h d", h=h1 - h0)
                        settle(V_.reciprocal(e_rs[:, h0:h1], o[:, :, E_HD]))
                        V_.tensor_tensor(e_o[:, E_HD * h0:E_HD * h1].rearrange("p (h d) -> p h d", h=h1 - h0), o[:, :, 0:E_HD],
                                         e_rs[:, h0:h1].unsqueeze(2).to_broadcast([P, h1 - h0, E_HD]), ALU.mult).then_inc(e_on, 1)
                    dve.wait_ge(e_y, ib + 1)
                    V_.tensor_tensor(X[:, ib, :], PS[:, 7, 0:D], X[:, ib, :], ALU.add).then_inc(e_x, 1)
                dve.wait_ge(e_x, TT)

            with dve.Fori(0, B) as b:
                count[0] = 0
                dve.wait_ge(x_loaded, 16)
                linear_attention()
                if last >= 2:
                    mixture(0, 3, 3)
                if last >= 3:
                    causal_attention()
                if last >= 4:
                    mixture(1, 5, 5)
                if last >= 5:
                    phase_memory()
                if last >= 6:
                    layer_norm(7)
                    add_y(7)
                if last >= 7:
                    mixed_attention()
                if last >= 8:
                    layer_norm(9)
                    add_y(8)
                dve.nop().then_inc(x_done, 1)
                dve.drain().then_inc(sequence_ended, 1)
                dve.wait_ge(sequence_go, b + 1)

        @block.tensor
        def _(pe):
            mm = nc.tensor.matmul

            pe.wait_ge(setup_pool, 7)
            pe.wait_ge(rows_loaded, 16)
            pe.wait_ge(setup_dve, 11)
            mm(PS[:, 0, 0:N_EXPERT], one_col.to_broadcast([P, P]), f_proto2[:, :], start=True, stop=True).then_inc(setup_pe, 1)
            pe.wait_ge(w_loaded["d"], 16)
            mm(PS[0:4, 1, 0:P], W["d_lora_down"][0:100, :], W["d_down_aux"][0:100, :], start=True, stop=True).then_inc(setup_pe, 1)
            pe.wait_ge(setup_act, 6)
            mm(PS[0:50, 2, 0:P], W["d_lora_up"][0:4, :], tmp[0:4, 0, 0:P], start=True, stop=True).then_inc(setup_pe, 1)
            pe.wait_ge(setup_act, 7)
            mm(PS[:, 3, 0:P], tmp[0:50, 1, 0:P], W["d_up_aux"][0:50, :], start=True, stop=True).then_inc(setup_pe, 1)
            pe.wait_ge(w_loaded["e"], 16)
            pe.wait_ge(setup_dve, SETUP_KERPLE)
            for half in range(2):
                w = W["e_mix_kerple"][:, P * half:P * (half + 1)]
                mm(PS[:, 4 + half, :], w, e_kerple[:, 0:512], start=True, stop=True)
                mm(PS[:, 6 + half, 0:STEP], w, e_kerple[:, 512:TABLE], start=True, stop=True).then_inc(setup_pe, 1)

            def feature_layout(k, src):
                pe.wait_ge(tr_in, k + 1)
                for tt in range(TT):
                    ins = nc.tensor.transpose(PS[:, 7, P * tt:P * (tt + 1)], src[:, tt, :], ident)
                ins.then_inc(tr_psum, 1)

            def tok(t, tt):
                return t[:, P * tt:P * (tt + 1)]

            def linear_attention():
                pe.wait_ge(w_loaded["a"], 16)
                feature_layout(0, XN)
                pe.wait_ge(xT_ready, 1)
                mm(PS[:, 0, :], W["a_qkv"][:, 0:D], XT[:, :], start=True, stop=True).then_inc(a_proj, 1)
                mm(PS[:, 1, :], W["a_qkv"][:, D:2 * D], XT[:, :], start=True, stop=True).then_inc(a_proj, 1)
                for tt in range(TT):
                    ins = mm(PS[:, 2, D * tt:D * (tt + 1)], tok(XT, tt), W["a_qkv"][:, 2 * D:3 * D], start=True, stop=True)
                ins.then_inc(a_proj, 1)
                for n in range(8):
                    c = n % 4
                    pe.wait_ge(a_qk, 1 if n < 4 else 2)
                    if n >= 3:
                        pe.wait_ge(a_feat, n - 2)
                    bank = PS[:, 3 + n % 3, :]
                    if n < 4:
                        ins = mm(bank, W["a_features"][:, P * c:P * (c + 1)], a_qT, start=True, stop=True)
                    else:
                        ins = mm(bank, tok(a_kT, c), W["a_features"], start=True, stop=True)
                    ins.then_inc(a_fpre, 1)
                pe.wait_ge(a_feat, 8)
                pe.wait_ge(a_v, 1)
                for c in range(4):
                    at = (c % 2) * (D + 1)
                    for tt in range(TT):
                        ins = mm(PS[:, c // 2, at:at + D + 1], a_kf[:, tt, P * c:P * (c + 1)], v_aug[:, tt, :],
                                 start=tt == 0, stop=tt == TT - 1)
                    ins.then_inc(a_kv, 1)
                pe.wait_ge(a_masked, 8)
                for bank, w in ((2, a_kvbd), (3, a_zbd)):
                    for c in range(4):
                        ins = mm(PS[:, bank, :], w[:, c, :], a_qf[:, c, :], start=c == 0, stop=c == 3)
                    ins.then_inc(a_att, 1)
                pe.wait_ge(a_attn_ready, 1)
                for tt in range(TT):
                    y = PS[:, 6, D * tt:D * (tt + 1)]
                    mm(y, tok(a_attn, tt), W["a_out"], start=True, stop=False)
                    ins = mm(y, R["ones"], R["a_bo"], start=False, stop=True)
                ins.then_inc(y_psum, 1)
                feature_layout(1, a_r)
                pe.wait_ge(xT_ready, 2)
                for c in range(4):
                    mm(PS[:, c, :], W["a_w1"][:, P * c:P * (c + 1)], XT[:, :], start=True, stop=True).then_inc(a_h, 1)
                pe.wait_ge(a_gelu, 4)
                w2 = W["a_w2"].rearrange("p (c d) -> p c d", c=4)
                for tt in range(TT):
                    y = PS[:, 6, D * tt:D * (tt + 1)]
                    for c in range(4):
                        mm(y, tok(a_hT[:, c, :], tt), w2[:, c, :], start=c == 0, stop=False)
                    ins = mm(y, R["ones"], R["a_b2"], start=False, stop=True)
                ins.then_inc(y_psum, 1)

            def mixture(k, tr):
                feature_layout(tr, XN)
                pe.wait_ge(xT_ready, tr + 1)
                for tt in range(TT):
                    d = PS[:, 0, N_EXPERT * tt:N_EXPERT * (tt + 1)]
                    ins = mm(d, tok(XT, tt), W["f_proto"], start=True, stop=True)
                ins.then_inc(f_xp, 1)
                pe.wait_ge(f_gated, k + 1)
                for tt in range(TT):
                    ins = nc.tensor.transpose(PS[0:N_EXPERT, 1, P * tt:P * (tt + 1)], f_gate[:, tt, :], ident)
                ins.then_inc(f_gT, 1)
                pe.wait_ge(f_gTs, k + 1)
                gT = f_gateT[0:N_EXPERT, :]
                for c in range(4):
                    if c >= 2:
                        pe.wait_ge(f_gh, 4 * k + c - 1)
                    mm(PS[:, 4 + c % 2, :], W["f_spread"][0:N_EXPERT, P * c:P * (c + 1)], gT, start=True, stop=True)
                    mm(PS[:, 2 + c % 2, :], W["f_down"][:, P * c:P * (c + 1)], XT[:, :], start=True, stop=True).then_inc(f_hp, 1)
                pe.wait_ge(f_gh, 4 * (k + 1))
                up = W["f_up"].rearrange("p (c d) -> p c d", c=4)
                for tt in range(TT):
                    y = PS[:, 6, D * tt:D * (tt + 1)]
                    for c in range(4):
                        mm(y, tok(f_h[:, c, :], tt), up[:, c, :], start=c == 0, stop=False)
                    ins = mm(y, gT[:, P * tt:P * (tt + 1)], W["f_bias"][0:N_EXPERT, :], start=False, stop=True)
                ins.then_inc(y_psum, 1)

            def causal_attention():
                feature_layout(3, XN)
                pe.wait_ge(xT_ready, 4)
                for j, name in enumerate(("b_q", "b_qrot", "b_k", "b_krot")):
                    ins = mm(PS[:, j, :], W[name], XT[:, :], start=True, stop=True)
                    if j % 2 == 1:
                        ins.then_inc(b_proj, 1)
                for tt in range(TT):
                    v = PS[:, 4, D * tt:D * (tt + 1)]
                    mm(v, tok(XT, tt), W["b_v"], start=True, stop=False)
                    ins = mm(v, R["ones"], R["b_bv"], start=False, stop=True)
                ins.then_inc(b_proj, 1)

                def scores(u):
                    for n in (2 * u, 2 * u + 1):
                        ib, h = n // 16, n % 16
                        at, c = 32 * (h % 4), h // 4
                        if n >= 4:
                            pe.wait_ge(b_exp, n - 3)
                        mm(PS[:, n % 4, 0:P * (ib + 1)], b_qs[at:at + 8, c, P * ib:P * (ib + 1)],
                           b_ks[at:at + 8, c, 0:P * (ib + 1)], start=True, stop=False)
                        mm(PS[:, n % 4, P * ib:P * (ib + 1)], ident_bf, causal_mask, start=False, stop=True).then_inc(b_sc, 1)

                pe.wait_ge(b_vs, 1)
                pe.wait_ge(b_spread, 2 * B_HD * 16)
                scores(0)
                for u in range(32):
                    if u + 1 < 32:
                        scores(u + 1)
                    for n in (2 * u, 2 * u + 1):
                        ib = n // 16
                        pe.wait_ge(b_exp, n + 1)
                        if n >= 2:
                            pe.wait_ge(b_ptc[n % 2], n // 2)
                        for jb in range(ib + 1):
                            ins = nc.tensor.transpose(PS[:, 4 + n % 2, P * jb:P * (jb + 1)],
                                                      b_p[:, n % 4, P * jb:P * (jb + 1)], ident)
                        ins.then_inc(b_tp, 1)
                    for n in (2 * u, 2 * u + 1):
                        ib, h = n // 16, n % 16
                        pe.wait_ge(b_ptc[n % 2], n // 2 + 1)
                        if h == 0 and ib >= 2:
                            pe.wait_ge(b_od, ib - 1)
                        o = PS[:, 6 + ib % 2, (B_HD + 1) * h:(B_HD + 1) * (h + 1)]
                        for jb in range(ib + 1):
                            ins = mm(o, b_pT[:, n % 2, P * jb:P * (jb + 1)], b_val[:, jb, h, :], start=jb == 0, stop=jb == ib)
                        ins.then_inc(b_pv, 1)
                pe.wait_ge(b_od, TT)
                for ib in range(TT):
                    ins = nc.tensor.transpose(PS[:, 4, P * ib:P * (ib + 1)], b_o[:, ib, :], ident)
                ins.then_inc(b_ot, 1)
                pe.wait_ge(b_ots, 1)
                for tt in range(TT):
                    y = PS[:, 6, D * tt:D * (tt + 1)]
                    mm(y, tok(b_oT, tt), W["b_out"], start=True, stop=False)
                    ins = mm(y, R["ones"], R["b_bo"], start=False, stop=True)
                ins.then_inc(y_psum, 1)

            def phase_memory():
                feature_layout(5, XN)
                pe.wait_ge(xT_ready, 6)
                for j, name in enumerate(("c_key", "c_decay")):
                    mm(PS[:, j, :], W[name], XT[:, :], start=True, stop=True).then_inc(c_zp, 1)
                pe.wait_ge(c_zs, 4)
                pe.wait_ge(c_cv, 1)
                for c in range(C_CHUNKS):
                    cols = slice(P * c, P * (c + 1))
                    if c >= 2:
                        pe.wait_ge(c_frac, c - 1)
                    mm(PS[:, c % 2, :], W["c_theta"][:, cols], c_conv[:, 0, :], start=True, stop=True).then_inc(c_up, 1)
                    if c == 0:
                        pe.wait_ge(c_pws, 1)
                    if c >= 2:
                        pe.wait_ge(c_prod, 2 * (c - 1))
                    mm(PS[:, 2 + c % 2, :], W["c_spread"][:, cols], c_pw, start=True, stop=True).then_inc(c_pwx, 1)
                    if c >= 1:
                        gather(c - 1)
                    if c % 2 == 0:
                        kq = c // 2
                        mm(PS[:, 4, :], W["c_qre"][:, P * kq:P * (kq + 1)], XT[:, :], start=True, stop=True)
                        mm(PS[:, 5, :], W["c_qim"][:, P * kq:P * (kq + 1)], XT[:, :], start=True, stop=True).then_inc(c_query, 1)
                gather(C_CHUNKS - 1)
                pe.wait_ge(c_silu, 1)
                for tt in range(TT):
                    ins = mm(PS[:, 6, D * tt:D * (tt + 1)], tok(c_y, tt), W["c_out"], start=True, stop=True)
                ins.then_inc(y_psum, 1)

            def gather(c):
                pe.wait_ge(c_weighted, c + 1)
                w = W["c_gather"][:, P * c:P * (c + 1)]
                mm(PS[:, 6, :], w, c_pr[:, c % 2, :], start=c == 0, stop=False)
                mm(PS[:, 6, :], w, c_pi[:, c % 2, :], start=False, stop=c == C_CHUNKS - 1).then_inc(c_sum, 1)

            def adapted_linear(tr):
                feature_layout(tr, XN)
                pe.wait_ge(xT_ready, tr + 1)
                for tt in range(TT):
                    y = PS[:, 6, D * tt:D * (tt + 1)]
                    mm(y, tok(XT, tt), d_weight[:, :], start=True, stop=False)
                    ins = mm(y, R["ones"], R["d_b"], start=False, stop=True)
                ins.then_inc(y_psum, 1)

            def mixed_attention():
                feature_layout(7, XN)
                pe.wait_ge(xT_ready, 8)
                pe.wait_ge(e_w, 16)
                n_ch = E_HEADS * E_HD
                for n in range(16):
                    at = 2 * n_ch * (n % 2) + P * (n // 2)
                    k = 2 * (n % 2)
                    if n >= 2:
                        pe.wait_ge(e_rope, n - 1)
                    mm(PS[:, k, :], proj[:, at:at + P], XT[:, :], start=True, stop=True)
                    mm(PS[:, k + 1, :], proj[:, at + n_ch:at + n_ch + P], XT[:, :], start=True, stop=True).then_inc(e_qk, 1)
                for r in range(8):
                    if r >= 2:
                        pe.wait_ge(e_vs, r - 1)
                    mm(PS[:, 4 + r % 2, :], tok(XT, r // 2), proj[:, 4 * n_ch + 512 * (r % 2):4 * n_ch + 512 * (r % 2 + 1)],
                       start=True, stop=True).then_inc(e_vp, 1)
                pe.wait_ge(e_rope, 16)
                pe.wait_ge(e_add, 16)
                pe.wait_ge(e_vs, 8)
                for ib in range(TT):
                    w = P * (ib + 1)
                    for h in range(E_HEADS):
                        n = 16 * ib + h
                        if n >= 2:
                            pe.wait_ge(e_evac, n - 1)
                        if ib and h < 2:
                            pe.wait_ge(e_on, 3 * ib)
                        at = 64 * (h % 2)
                        mm(PS[:, h % 2, 0:w], QT[at:at + 64, h // 2, P * ib:P * (ib + 1)], KT[at:at + 64, h // 2, 0:w],
                           start=True, stop=True).then_inc(e_sc, 1)

                    def mix(n):
                        g = n % GROUPS
                        pe.wait_ge(e_dma[g // 4], 64 * (ib + 1))
                        if g == 0 and ib:
                            pe.wait_ge(e_ots, 2 * ib)
                            pe.wait_ge(e_ptc, 4 * sum(range(1, ib + 1)))
                            pe.wait_ge(e_x, ib)
                        if n >= 2:
                            pe.wait_ge(e_hadd, 2 * (n - 1))
                        for half in range(2):
                            mm(PS[:, 2 + 2 * (n % 2) + half, 0:width(ib, g)], W["e_mix_scores"][:, P * half:P * (half + 1)],
                               FREG[:, g, 0:width(ib, g)], start=True, stop=True).then_inc(e_m1, 1)

                    mix(GROUPS * ib)
                    for g in range(GROUPS):
                        n = GROUPS * ib + g
                        if g + 1 < GROUPS:
                            mix(n + 1)
                        pe.wait_ge(e_gelu, n + 1)
                        if n >= 2:
                            pe.wait_ge(e_fin, n - 1)
                        for half in range(2):
                            ins = mm(PS[:, 6 + n % 2, 0:width(ib, g)], W["e_mix_back"][:, P * half:P * (half + 1)],
                                     e_hidden[:, n % 2, half, 0:width(ib, g)], start=half == 0, stop=half == 1)
                        ins.then_inc(e_m2, 1)
                    first = 4 * sum(range(1, ib + 1))
                    pe.wait_ge(e_zero, 3 * (ib + 1))
                    for k in range(4 * (ib + 1)):
                        gq, jb = k // (ib + 1), k % (ib + 1)
                        pe.wait_ge(e_exp, GROUPS * ib + 4 * gq + 4)
                        if k >= 4:
                            pe.wait_ge(e_ptc, first + k - 3)
                        for g4 in range(4):
                            ins = nc.tensor.transpose(PS[:, 2 + k % 4, P * g4:P * (g4 + 1)],
                                                      FREG[:, 4 * gq + g4, P * jb:P * (jb + 1)], ident)
                        ins.then_inc(e_tp, 1)
                    pe.wait_ge(e_ptc, first + 4 * (ib + 1))
                    for bank, h0, h1 in PV_BANKS:
                        for h in range(h0, h1):
                            o = PS[:, bank, (E_HD + 1) * (h - h0):(E_HD + 1) * (h - h0 + 1)]
                            for jb in range(ib + 1):
                                ins = mm(o, PT[:, jb, :, h], V[:, jb, h, :], start=jb == 0, stop=jb == ib)
                        ins.then_inc(e_pv, 1)
                    pe.wait_ge(e_on, 3 * (ib + 1))
                    for j in range(2):
                        for c in range(4):
                            ins = nc.tensor.transpose(PS[:, 2 + j, P * c:P * (c + 1)], e_o[:, P * (4 * j + c):P * (4 * j + c + 1)], ident)
                        ins.then_inc(e_ot, 1)
                    pe.wait_ge(e_ots, 2 * (ib + 1))
                    for c in range(8):
                        ins = mm(PS[:, 7, 0:D], e_oT[:, P * c:P * (c + 1)], W["e_out"][:, D * c:D * (c + 1)],
                                 start=c == 0, stop=c == 7)
                    ins.then_inc(e_y, 1)

            with pe.Fori(0, B) as b:
                linear_attention()
                if last >= 2:
                    mixture(0, 2)
                if last >= 3:
                    causal_attention()
                if last >= 4:
                    mixture(1, 4)
                if last >= 5:
                    phase_memory()
                if last >= 6:
                    adapted_linear(6)
                if last >= 7:
                    mixed_attention()
                if last >= 8:
                    adapted_linear(8)
                pe.drain().then_inc(sequence_ended, 1)
                pe.wait_ge(sequence_go, b + 1)


def _pack(group, pieces):
    got = []
    for name, n in PARTS[group]:
        a = np.asarray(pieces[name])
        a = a.reshape(a.shape[0], -1)
        assert a.shape[1] == n, (name, a.shape)
        got.append(np.concatenate([a, np.zeros((P - a.shape[0], n), np.float32)]) if a.shape[0] < P else a)
    return np.ascontiguousarray(np.concatenate(got, axis=1), dtype=np.float32)


def _layout(i):
    g = {k: np.asarray(v) for k, v in i.items()}
    f4 = np.float32
    eye = np.eye(P, dtype=f4)
    col = np.arange(P)
    out = {}
    proj = g["L0_attn_a_proj"]
    feats = np.zeros((P, A_FEATS), f4)
    for h in range(A_HEADS):
        feats[A_HD * h:A_HD * (h + 1), A_F * h:A_F * (h + 1)] = proj[h]
    kv_mask = np.zeros((P, 4, P), f4)
    for c in range(4):
        kv_mask[:, c, :] = (4 * c + col[:, None] // A_F) == (col[None, :] // A_HD)
    rep = lambda v, n=P: np.broadcast_to(v.reshape(1, -1), (n, v.size))
    out["w_a"] = _pack("a", dict(
        a_qkv=g["L0_attn_a_w_qkv"].T, a_features=feats, a_out=g["L0_attn_a_w_out"].T, a_w1=g["L0_attn_a_w1"].T,
        a_w2=g["L0_attn_a_w2"].T.reshape(4, P, D).transpose(1, 0, 2), a_gamma=rep(g["L0_attn_a_gamma"]),
        a_beta=rep(g["L0_attn_a_beta"]), a_b1=g["L0_attn_a_b1"].reshape(4, P).T, identity=eye, a_kv_mask=kv_mask))
    spread = np.zeros((N_EXPERT, N_EXPERT * RANK), f4)
    for e in range(N_EXPERT):
        spread[e, RANK * e:RANK * (e + 1)] = 1
    out["w_f"] = _pack("f", dict(
        f_proto=g["L0_ffn_prototypes"].T, f_down=g["L0_ffn_B"].reshape(-1, D).T,
        f_up=g["L0_ffn_A"].transpose(0, 2, 1).reshape(4, P, D).transpose(1, 0, 2), f_bias=g["L0_ffn_bias"],
        f_temp=np.broadcast_to(g["L0_ffn_temp"].reshape(1, 1), (P, 1)), expert_no=rep(np.arange(N_EXPERT, dtype=f4)),
        f_spread=spread))
    def rope(hd, n):
        inv = (1.0 / np.float32(10000.0) ** (np.arange(0, hd, 2, dtype=f4) / f4(hd))).astype(f4)
        fr = np.arange(T, dtype=f4)[None, :] * inv[:, None]
        cos, sin = np.cos(fr), np.sin(fr)
        return (np.tile(np.concatenate([cos, cos]), (n, 1)).astype(f4), np.tile(np.concatenate([-sin, sin]), (n, 1)).astype(f4))

    def rot(hd, n):
        return (np.arange(n) // hd) * hd + (np.arange(n) % hd + hd // 2) % hd
    w, bias = g["L0_attn_b_qkv_w"], g["L0_attn_b_qkv_b"]
    o = B_HD * (4 * (col % 4) + col // 4 % 4) + col // 16
    r = rot(B_HD, D)[o]
    cos, sin = (t[o] for t in rope(B_HD, B_HEADS))
    out["w_b"] = _pack("b", dict(
        b_q=w[0:D][o].T, b_qrot=w[0:D][r].T, b_k=w[D:2 * D][o].T, b_krot=w[D:2 * D][r].T, b_v=w[2 * D:].T,
        b_bias=np.stack([bias[0:D][o], bias[0:D][r], bias[D:2 * D][o], bias[D:2 * D][r]], 1), b_out=g["L0_attn_b_proj_w"].T,
        b_cos=cos, b_sin=sin))
    W_in, ck = g["L1_attn_a_W_in"], g["L1_attn_a_conv_k"][:, 0, :]
    key_of = col // C_H
    theta = np.zeros((P, C_CHUNKS, P), f4)
    c_spread = np.zeros((P, C_CHUNKS, P), f4)
    c_gather = np.zeros((P, C_CHUNKS, P), f4)
    k4, hh, m = col // (C_H * C_M), col // C_M % C_H, col % C_M
    for c in range(C_CHUNKS):
        row = (4 * c + k4) * C_H + hh
        theta[row, c, col] = g["L1_attn_a_theta"][0, 0, 4 * c + k4, hh, m]
        c_spread[row, c, col] = 1
        c_gather[col, c, row] = 1
    q = W_in[:, D + C_K:].reshape(D, C_KQ, C_H, C_M, 2)
    rep_q = lambda a: np.broadcast_to(a[:, :, None], (D, C_KQ, 4, C_H, C_M)).reshape(D, C_KQ * P)
    ns = g["L1_attn_a_norm_scale"]
    d_re, d_im = (g[f"L1_attn_a_W_{x}"][np.arange(C_H), np.arange(C_H)] for x in ("re", "im"))
    pos = np.arange(T, dtype=f4)
    steps = np.where((key_of < C_K - C_ANCHOR)[:, None], f4(T - 1) - pos[None], pos[None]).astype(f4)
    slopes = np.concatenate([g["L1_attn_a_decay_slopes"], g["L1_attn_a_anchor_slopes"]])[key_of]
    eh = col % E_HEADS
    out["w_c"] = _pack("c", dict(
        c_key=W_in[:, 0:D], c_decay=W_in[:, D + key_of], c_taps_key=ck[:, 0:D].T, c_taps_decay=ck[:, D + key_of].T,
        c_score_scale=g["L1_attn_a_score_scale"][key_of][:, None],
        softplus_in=np.stack([slopes, g["L1_attn_b_log_p"].reshape(-1)[eh], g["L1_attn_b_log_a"].reshape(-1)[eh]], 1),
        c_theta=theta, c_qre=rep_q(q[..., 0]), c_qim=rep_q(q[..., 1]),
        c_out=g["L1_attn_a_W_out"], c_steps=steps, c_spread=c_spread, c_gather=c_gather))
    out["w_d"] = _pack("d", dict(
        causal_mask=np.where(col[None, :] <= col[:, None], 0, MASKED),
        c_norm=np.concatenate([rep(ns[hh]), rep(ns[C_H + hh])], 1), c_diag=np.concatenate([rep(d_re[hh]), rep(d_im[hh])], 1),
        d_w=g["L1_ffn_W"].T, d_lora_down=g["L1_ffn_lora_down"].T, d_down_aux=g["L1_ffn_down_aux"],
        d_lora_up=g["L1_ffn_lora_up"].T, d_up_aux=g["L1_ffn_up_aux"].T))
    w1, w2 = g["L1_attn_b_w1"], g["L1_attn_b_w2"]
    s1, k1, s2 = (np.zeros((P, 2, P), f4) for _ in range(3))
    for i in range(QROWS):
        half, i4 = i // 4, i % 4
        rows_, cols_ = slice(E_HEADS * i, E_HEADS * (i + 1)), slice(E_CH * i4, E_CH * (i4 + 1))
        s1[rows_, half, cols_] = w1[0:E_HEADS]
        k1[rows_, half, cols_] = w1[E_HEADS:]
        s2[cols_, half, rows_] = w2
    dist = (col // E_HEADS)[:, None] + (T - 1) - np.arange(TABLE)[None, :]
    cos, sin = rope(E_HD, 2)
    out["w_e"] = _pack("e", dict(
        e_out=g["L1_attn_b_w_o"].reshape(8, P, D).transpose(1, 0, 2), e_mix_scores=s1, e_mix_kerple=k1, e_mix_back=s2,
        e_b1=g["L1_attn_b_b1"][col % E_CH][:, None], e_b2=g["L1_attn_b_b2"][eh][:, None], e_cos=cos, e_sin=sin,
        e_dist=np.abs(dist).astype(f4), e_mask=np.where(dist >= 0, 0, MASKED).astype(f4)))
    wq = g["L1_attn_b_w_qkv"].reshape(P, 3, E_HEADS * E_HD)
    r = rot(E_HD, E_HEADS * E_HD)
    out["w_proj"] = np.ascontiguousarray(np.concatenate([wq[:, 0], wq[:, 0][:, r], wq[:, 1], wq[:, 1][:, r], wq[:, 2]], 1))
    rows = dict(ones=np.ones(P, f4), a_bo=g["L0_attn_a_b_out"], a_b2=g["L0_attn_a_b2"], b_bv=bias[2 * D:],
                b_bo=g["L0_attn_b_proj_b"], d_b=g["L1_ffn_b"])
    out["rows"] = np.ascontiguousarray(np.concatenate([rows[n] for n, _ in ROWS]).reshape(1, -1))
    return out


ORDER = ["w_a", "w_f", "w_b", "w_c", "w_d", "w_e", "w_proj", "rows"]
LAST = 8


def kernel(**inputs):
    import concourse.bacc as bacc
    from concourse.bass_utils import run_bass_kernel_spmd

    x = np.ascontiguousarray(inputs["L0_attn_a_x"])
    arrays = {"x": x, **_layout(inputs)}
    nc = bacc.Bacc("TRN2", target_bir_lowering=False, num_devices=1)
    args = [nc.dram_tensor(n + "_dram", arrays[n].shape, mybir.dt.from_np(arrays[n].dtype), kind="ExternalInput").ap()
            for n in ["x"] + ORDER]
    out = nc.dram_tensor("out_dram", x.shape, F32, kind="ExternalOutput").ap()
    build(nc, *args, out, last=LAST)
    got = run_bass_kernel_spmd(nc, [{n + "_dram": a for n, a in arrays.items()}], core_ids=[0])
    return got.results[0]["out_dram"]
```

```python
from contextlib import ExitStack

import numpy as np
import concourse.bass as bass
from concourse import mybir

F32 = mybir.dt.float32
BF16 = mybir.dt.bfloat16
U32 = mybir.dt.uint32
ALU = mybir.AluOpType
ACT = mybir.ActivationFunctionType
AX = mybir.AxisListType

P = 128
D = 128
T = 512
TT = T // P
EPS_LN = 1e-5
A_HEADS, A_F = 16, 32
A_HD = D // A_HEADS
A_FEATS = A_HEADS * A_F
A_HIDDEN = 4 * D
EPS_ATTN = 1e-8
N_EXPERT, RANK = 32, 16
B_HEADS = 16
B_HD = D // B_HEADS
B_SCALE = float(1.0 / np.sqrt(B_HD))
C_K, C_KQ, C_ANCHOR, C_M, C_TAPS = 32, 4, 4, 8, 4
C_H = D // C_K
C_CHUNKS = C_K * C_H * C_M // P
MAGIC = 1.5 * 2.0 ** 23
TWO_PI = 6.283185
HALF_PI = 1.5707963
E_HEADS, E_HD = 16, 64
E_CH = 2 * E_HEADS
QROWS = P // E_HEADS
STEP = 32
TABLE = T + STEP
GROUPS = P // QROWS
E_SCALE = 1.0 / 8.0
MASKED = -1e30

PARTS = {
    "a": [("a_qkv", 3 * D), ("a_features", A_FEATS), ("a_out", D), ("a_w1", A_HIDDEN), ("a_w2", A_HIDDEN),
          ("a_gamma", D), ("a_beta", D), ("a_b1", 4), ("identity", P), ("a_kv_mask", 4 * P)],
    "f": [("f_proto", N_EXPERT), ("f_down", N_EXPERT * RANK), ("f_up", 4 * D), ("f_bias", D), ("f_temp", 1),
          ("expert_no", N_EXPERT), ("f_spread", N_EXPERT * RANK)],
    "b": [("b_q", D), ("b_qrot", D), ("b_k", D), ("b_krot", D), ("b_v", D), ("b_bias", 4), ("b_out", D),
          ("b_cos", T), ("b_sin", T)],
    "c": [("c_key", D), ("c_decay", D), ("c_taps_key", C_TAPS), ("c_taps_decay", C_TAPS), ("c_score_scale", 1),
          ("softplus_in", 3), ("c_theta", C_CHUNKS * P), ("c_qre", C_KQ * P), ("c_qim", C_KQ * P),
          ("c_out", D),
          ("c_steps", T), ("c_spread", C_CHUNKS * P), ("c_gather", C_CHUNKS * P)],
    "d": [("causal_masks", 2 * P), ("c_norm", 2 * P), ("c_diag", 2 * P), ("d_w", D), ("d_lora_down", 4), ("d_down_aux", D), ("d_lora_up", 50), ("d_up_aux", D)],
    "e": [("e_out", 8 * D), ("e_mix_scores", 2 * P), ("e_mix_kerple", 2 * P), ("e_mix_back", 2 * P),
          ("e_b1", 1), ("e_b2", 1), ("e_cos", T), ("e_sin", T), ("e_dist", TABLE), ("e_mask", TABLE)],
}
WIDTH = {g: sum(n for _, n in parts) for g, parts in PARTS.items()}
ROWS = [("ones", P), ("a_bo", D), ("a_b2", D), ("b_bv", D), ("b_bo", D), ("d_b", D)]
ROW_WIDTH = sum(n for _, n in ROWS)
SETUP_KERPLE, SETUP_DVE = 19, 24
E_PROJ = 5 * E_HEADS * E_HD


def build(nc, x, w_a, w_f, w_b, w_c, w_d, w_e, w_proj, rows, out, last=8):
    B = x.shape[0]
    weights_in = dict(a=w_a, f=w_f, b=w_b, c=w_c, d=w_d, e=w_e)
    ctx = ExitStack()
    with ctx:
        def sb(name, cols, dt=F32, parts=P):
            shape = [parts] + (list(cols) if type(cols) in (tuple, list) else [cols])
            return ctx.enter_context(nc.sbuf_tensor(name, shape, dt))

        def sem(name):
            return ctx.enter_context(nc.semaphore(name))

        W, weight_tiles = {}, {}
        ARENA = 4096 * 2 + 8192
        arena = sb("arena", ARENA)
        for g, parts in PARTS.items():
            tile = weight_tiles[g] = arena[:, ARENA - WIDTH[g]:] if g == "d" else sb(f"weights_{g}", WIDTH[g])
            at = 0
            for name, n in parts:
                W[name] = tile[:, at:at + n]
                at += n
        row_tile = sb("rows", ROW_WIDTH, parts=1)
        R, at = {}, 0
        for name, n in ROWS:
            R[name] = row_tile[0:1, at:at + n]
            at += n
        ident = W["identity"]
        mask_tile = sb("masks_and_identity_bf16", 3 * P, BF16)
        causal_mask, causal_mask_T, ident_bf = (mask_tile[:, P * j:P * (j + 1)] for j in range(3))

        f_proto2 = sb("f_proto_squared", N_EXPERT)
        f_p2 = sb("f_proto_norm2", N_EXPERT)
        f_negtinv = sb("f_minus_inverse_temperature", 1)
        small = sb("prologue_small", 16)
        c_logdecay = W["c_steps"]
        d_weight = sb("d_weight", D)
        e_kerple = W["e_dist"]
        e_bias_table = W["e_mask"]
        e_hidden_table = sb("e_hidden_table", (2, TABLE))
        const = sb("constants", 8)
        half_pi, one_col, neg_half = const[:, 0:1], const[:, 1:2], const[:, 2:6]

        X = sb("x", (TT, D))
        XN = sb("x_normed", (TT, D))
        XT = sb("x_normed_feature", T)
        stats = sb("bn_stats", (TT, 6))
        mv = sb("mean_var", (TT, 2))
        varp = sb("var_plus_eps", TT)
        rstd = sb("rstd", TT)
        v_aug = sb("a_values_and_one", (TT, D + 1))
        b_val = sb("b_values_and_one", (TT, B_HEADS, B_HD + 1))
        V = sb("e_values", (TT, E_HEADS, E_HD))
        tmp = sb("tmp", (4, T))
        mx = sb("row_max", 16)
        negmx = sb("minus_row_max", 16)
        FREG = sb("mixed_scores", (GROUPS, T))
        proj = FREG[:, :, :].rearrange("p g j -> p (g j)")[:, 0:E_PROJ]

        def carve():
            at = [0]

            def take(*shape):
                n = int(np.prod(shape))
                v = arena[:, at[0]:at[0] + n]
                at[0] += n
                assert at[0] <= ARENA
                if len(shape) == 2:
                    v = v.rearrange("p (a b) -> p a b", a=shape[0])
                if len(shape) == 3:
                    v = v.rearrange("p (a b c) -> p a b c", a=shape[0], b=shape[1])
                return v
            return take
        t = carve()
        a_qT, a_kT, a_qf, a_kf = t(T), t(T), t(4, T), t(TT, A_FEATS)
        a_kvbd, a_zbd, a_attn, a_z = t(4, P), t(4, P), t(T), t(T)
        a_r, a_hT, a_y = t(TT, D), t(4, T), t(TT, D)
        t = carve()
        f_xx, f_d, f_top, f_idx, f_idxf = t(TT), t(TT, N_EXPERT), t(TT, 8), t(TT, 8), t(TT, 8)
        f_w, f_gate, f_gateT, f_h, f_sq = t(8, TT), t(2 * TT, N_EXPERT), t(T), t(4, T), t(TT, D)
        f_near = t(TT, 2)
        t = carve()
        b_q, b_k, b_rest = t(T), t(T), t(T)
        b_parts = t(2 * 3, T // 2).bitcast(BF16)
        b_qs, b_ks = t(8, T // 2).bitcast(BF16), t(8, T // 2).bitcast(BF16)
        b_pT, b_rs, b_o, b_oT = t(4, T), t(16), t(TT, D), t(T)
        b_negmax, b_maxrest = t(16), t(16)
        b_maxparts, b_maxT = t(24).bitcast(BF16), t(2, P // 2).bitcast(BF16)
        t = carve()
        c_z, c_conv, c_pw, c_inv, c_y = t(2, T + 4), t(2, T), t(T), t(T), t(T)
        c_rr, c_ff, c_re, c_im, c_pr, c_pi = t(2, T), t(2, T), t(2, T), t(2, T), t(2, T), t(2, T)
        c_nr, c_ni = t(2, T), t(2, T)
        t = carve()
        QT, KT, S = t(8, T), t(8, T), t(E_HEADS, T)
        PT = S.rearrange("p a b -> p (a b)").rearrange("p (jb i h) -> p jb i h", jb=TT, h=E_HEADS)
        e_hidden = sb("e_hidden", (2, 2, T))
        e_oT = tmp[:, 0:2, :].rearrange("p a b -> p (a b)")
        e_sum, e_rs = sb("e_row_sum", 16), sb("e_row_sum_inverse", 16)

        PS = ctx.enter_context(nc.psum_tensor("banks", [P, 8, 512], F32))

        rows_loaded = sem("rows_loaded")
        w_loaded = {g: sem(f"w_{g}_loaded") for g in PARTS}
        sequence_go = sem("sequence_go")
        setup_act = sem("setup_act")
        setup_dve = sem("setup_dve")
        setup_pe = sem("setup_pe")
        setup_pool = sem("setup_pool")

        cleared = []

        def seq_sem(name):
            cleared.append(sem(name))
            return cleared[-1]
        sequence_ended = seq_sem("sequence_ended")
        x_loaded = seq_sem("x_loaded")
        out_stored = seq_sem("out_stored")
        dve_step = seq_sem("dve_step")
        act_step = seq_sem("act_step")
        pool_step = seq_sem("pool_step")
        ln_var = seq_sem("ln_var")
        ln_rstd = seq_sem("ln_rstd")
        tr_in = seq_sem("tr_in")
        tr_psum = seq_sem("tr_psum")
        xT_ready = seq_sem("xT_ready")
        y_psum = seq_sem("y_psum")
        x_done = seq_sem("x_done")
        a_proj, a_qk, a_v = seq_sem("a_proj"), seq_sem("a_qk"), seq_sem("a_v")
        a_fpre, a_neg, a_exp, a_feat = seq_sem("a_fpre"), seq_sem("a_neg"), seq_sem("a_exp"), seq_sem("a_feat")
        a_kv, a_masked, a_att, a_attn_ready = seq_sem("a_kv"), seq_sem("a_masked"), seq_sem("a_att"), seq_sem("a_attn")
        a_h, a_gelu = seq_sem("a_h"), seq_sem("a_gelu")
        f_xp, f_xxd, f_d2, f_dist = seq_sem("f_xp"), seq_sem("f_xxd"), seq_sem("f_d2"), seq_sem("f_dist")
        f_spread_up = seq_sem("f_spread_up")
        f_diff, f_e2, f_gated = seq_sem("f_diff"), seq_sem("f_e2"), seq_sem("f_gated")
        f_gT, f_gTs, f_hp, f_hs, f_gh = seq_sem("f_gT"), seq_sem("f_gTs"), seq_sem("f_hp"), seq_sem("f_hs"), seq_sem("f_gh")
        b_proj, b_vs = seq_sem("b_proj"), seq_sem("b_vs")
        b_split, b_ones, b_mparts, b_mT, b_mTs = (seq_sem(n) for n in ("b_split", "b_ones", "b_mparts", "b_mT", "b_mTs"))
        b_mrows = [seq_sem("b_mrows0"), seq_sem("b_mrows1")]
        b_st = seq_sem("b_st")
        b_spread = seq_sem("b_spread")
        b_sc, b_max, b_exp = seq_sem("b_sc"), seq_sem("b_max"), seq_sem("b_exp")
        b_pv, b_od, b_ot, b_ots = seq_sem("b_pv"), seq_sem("b_od"), seq_sem("b_ot"), seq_sem("b_ots")
        c_zp, c_zs, c_cv, c_lp, c_pws = seq_sem("c_zp"), seq_sem("c_zs"), seq_sem("c_cv"), seq_sem("c_lp"), seq_sem("c_pws")
        c_up, c_mag, c_frac, c_trig = seq_sem("c_up"), seq_sem("c_mag"), seq_sem("c_frac"), seq_sem("c_trig")
        c_pwx, c_ab, c_prod, c_sum = seq_sem("c_pwx"), seq_sem("c_ab"), seq_sem("c_prod"), seq_sem("c_sum")
        c_query, c_weighted = seq_sem("c_query"), seq_sem("c_weighted")
        c_norm, c_silu = seq_sem("c_norm"), seq_sem("c_silu")
        e_w, e_qk, e_rope, e_add = seq_sem("e_w"), seq_sem("e_qk"), seq_sem("e_rope"), seq_sem("e_add")
        e_vp, e_vs, e_sc, e_evac = seq_sem("e_vp"), seq_sem("e_vs"), seq_sem("e_sc"), seq_sem("e_evac")
        e_dma = [seq_sem(f"e_dma{q}") for q in range(4)]
        e_zero = seq_sem("e_zero")
        e_m1, e_hadd, e_gelu, e_m2 = seq_sem("e_m1"), seq_sem("e_hadd"), seq_sem("e_gelu"), seq_sem("e_m2")
        e_fk, e_fin, e_nmx, e_exp = seq_sem("e_fk"), seq_sem("e_fin"), seq_sem("e_nmx"), seq_sem("e_exp")
        e_tp, e_ptc, e_pv, e_div = seq_sem("e_tp"), seq_sem("e_ptc"), seq_sem("e_pv"), seq_sem("e_div")
        e_ots, e_y, e_x = seq_sem("e_ots"), seq_sem("e_y"), seq_sem("e_x")

        def width(ib, g):
            return P * ib + STEP * (g // 4 + 1)

        def table_at(ib, g):
            return T - 1 - (P * ib + QROWS * g)

        Q_PARTS, K_PARTS = (0, 0, 1, 0, 2, 1), (0, 1, 0, 2, 0, 1)
        B_ROWS = len(Q_PARTS) * B_HD


        block = ctx.enter_context(nc.Block())


        @block.sync
        def _(sp):
            sp.dma_start(row_tile[:, :], rows[:, :]).then_inc(rows_loaded, 16)
            for g in PARTS:
                sp.dma_start(weight_tiles[g][:, :], weights_in[g][:, :]).then_inc(w_loaded[g], 16)
            with sp.Fori(0, B) as b:
                sp.dma_start(X[:, :, :], x[bass.ds(b, 1)].rearrange("o (t p) d -> p (o t) d", p=P)).then_inc(x_loaded, 16)
                sp.dma_start(proj, w_proj[:, :]).then_inc(e_w, 16)
                if last >= 3:
                    sp.wait_ge(b_ones, 1)
                    for which, (parts, dst) in enumerate(((Q_PARTS, b_qs), (K_PARTS, b_ks))):
                        for part in range(3):
                            sp.wait_ge(b_split, 3 * which + part + 1)
                            for prod in range(6):
                                for a in range(2):
                                    if parts[prod] == part:
                                        at = 64 * a + B_HD * prod
                                        sp.dma_start(dst[at:at + B_HD, :, :], b_parts[64 * a:64 * a + 64, 3 * which + part, :]).then_inc(b_spread, 16)
                    for ib in range(TT):
                        sp.wait_ge(b_mTs, ib + 1)
                        for a in range(2):
                            at = 64 * a + B_ROWS
                            sp.dma_start(b_qs[at:at + 3, :, P * ib:P * (ib + 1)],
                                         b_maxT[24 * a:24 * a + 24, ib % 2, :]).then_inc(b_mrows[ib % 2], 16)
                if last >= 7:
                    for ib in range(TT):
                        sp.wait_ge(e_evac, 16 * (ib + 1))
                        if ib == 0:
                            sp.wait_ge(e_qk, 16)
                            sp.wait_ge(e_vp, 8)
                        else:
                            sp.wait_ge(e_tp, 4 * sum(range(1, ib + 1)))
                        for g in range(GROUPS):
                            n = width(ib, g)
                            sp.dma_start(FREG[:, g, 0:n],
                                         S[QROWS * g:QROWS * (g + 1), :, 0:n]).then_inc(e_dma[g // 4], 16)
                sp.wait_ge(x_done, 1)
                sp.dma_start(out[bass.ds(b, 1)].rearrange("o (t p) d -> p (o t) d", p=P), X[:, :, :]).then_inc(out_stored, 16)
                sp.wait_ge(out_stored, 16)
                sp.wait_ge(e_w, 16)
                sp.wait_ge(sequence_ended, 4)
                for s in cleared:
                    sp.sem_clear(s)
                sp.sem_inc(sequence_go, 1)

        @block.gpsimd
        def _(pool):
            def settle(ins):
                pool_count[0] += 1
                ins.then_inc(pool_step, 1)
                pool.wait_ge(pool_step, pool_count[0])

            pool_count = [0]
            nc.gpsimd.memset(half_pi, HALF_PI).then_inc(setup_pool, 1)
            nc.gpsimd.memset(one_col, 1.0).then_inc(setup_pool, 1)
            nc.gpsimd.memset(neg_half, -0.5).then_inc(setup_pool, 1)
            nc.gpsimd.memset(const[:, 6:7], 0.5).then_inc(setup_pool, 1)
            nc.gpsimd.memset(v_aug[:, :, D:D + 1], 1.0).then_inc(setup_pool, 1)
            nc.gpsimd.memset(b_val[:, :, :, B_HD:B_HD + 1], 1.0).then_inc(setup_pool, 1)
            pool.wait_ge(setup_pool, 6)

            def ln(k):
                pool.wait_ge(ln_var, k + 1)
                nc.gpsimd.tensor_tensor(rstd[:, :], varp[:, :], neg_half, ALU.pow).then_inc(ln_rstd, 1)

            def mixture(k, ln_no):
                ln(ln_no)
                pool.wait_ge(f_d2, k + 1)
                d = f_near.rearrange("p t e -> p (t e)")
                nc.gpsimd.tensor_tensor(d, d, const[:, 6:7].to_broadcast([P, TT * 2]), ALU.pow).then_inc(f_dist, 1)

            with pool.Fori(0, B) as b:
                pool_count[0] = 0
                for k in range(3):
                    ln(k)
                if last >= 2:
                    mixture(0, 3)
                if last >= 3:
                    ln(4)
                    pool.wait_ge(tr_in, 4)
                    nc.gpsimd.memset(b_ks[32:64, :, :], 1.0)
                    nc.gpsimd.memset(b_ks[96:128, :, :], 1.0).then_inc(b_ones, 1)
                if last >= 4:
                    mixture(1, 5)
                if last >= 5:
                    ln(6)
                if last >= 6:
                    ln(7)
                if last >= 7:
                    ln(8)
                    for n in range(16):
                        pool.wait_ge(e_rope, n + 1)
                        dst = QT if n % 2 == 0 else KT
                        pair = tmp[:, 2 * (n % 2):2 * (n % 2) + 2, :]
                        nc.gpsimd.tensor_tensor(dst[:, n // 2, :], pair[:, 0, :], pair[:, 1, :], ALU.add).then_inc(e_add, 1)
                    for ib in range(TT):
                        if ib == 0:
                            pool.wait_ge(e_qk, 16)
                            pool.wait_ge(e_vp, 8)
                        else:
                            pool.wait_ge(e_tp, 4 * sum(range(1, ib + 1)))
                        for gq in range(3):
                            nc.gpsimd.memset(FREG[:, 4 * gq:4 * gq + 4, width(ib, 4 * gq):P * (ib + 1)], 0.0).then_inc(e_zero, 1)
                        for g in range(GROUPS):
                            n = GROUPS * ib + g
                            w = width(ib, g)
                            pool.wait_ge(e_m1, 2 * (n + 1))
                            f = FREG[:, g, 0:w]
                            nc.gpsimd.tensor_tensor(f, f, e_bias_table[:, table_at(ib, g):table_at(ib, g) + w],
                                                    ALU.add).then_inc(e_fk, 1)
                if last >= 8:
                    ln(9)
                pool.drain().then_inc(sequence_ended, 1)
                pool.wait_ge(sequence_go, b + 1)

        @block.scalar
        def _(act):
            A = nc.scalar.activation
            act_count = [0]

            def settle(ins):
                act_count[0] += 1
                ins.then_inc(act_step, 1)
                act.wait_ge(act_step, act_count[0])

            act.wait_ge(setup_pool, 6)
            act.wait_ge(w_loaded["c"], 16)
            sp_in = W["softplus_in"]
            A(small[:, 0:3], sp_in, ACT.Abs).then_inc(setup_act, 1)
            act.wait_ge(setup_act, 1)
            A(small[:, 3:6], small[:, 0:3], ACT.Exp, scale=-1.0).then_inc(setup_act, 1)
            act.wait_ge(setup_act, 2)
            A(small[:, 6:9], small[:, 3:6], ACT.Ln, bias=one_col).then_inc(setup_act, 1)
            act.wait_ge(w_loaded["e"], 16)
            act.wait_ge(setup_dve, 1)
            A(e_kerple, e_kerple, ACT.Ln, scale=small[:, 11:12], bias=one_col).then_inc(setup_act, 1)
            act.wait_ge(setup_pe, 1)
            A(f_p2[:, :], PS[:, 0, 0:N_EXPERT], ACT.Copy).then_inc(setup_act, 1)
            act.wait_ge(setup_pe, 2)
            A(tmp[0:4, 0, 0:P], PS[0:4, 1, 0:P], ACT.Copy).then_inc(setup_act, 1)
            act.wait_ge(setup_pe, 3)
            A(tmp[0:50, 1, 0:P], PS[0:50, 2, 0:P], ACT.Copy).then_inc(setup_act, 1)

            def feature_layout(k):
                act.wait_ge(tr_psum, k + 1)
                A(XT[:, :], PS[:, 7, :], ACT.Copy).then_inc(xT_ready, 1)

            def linear_attention():
                feature_layout(0)
                act.wait_ge(a_proj, 1)
                A(a_qT, PS[:, 0, :], ACT.Copy).then_inc(a_qk, 1)
                act.wait_ge(a_proj, 2)
                A(a_kT, PS[:, 1, :], ACT.Copy).then_inc(a_qk, 1)
                for n in range(8):
                    act.wait_ge(a_neg, n + 1)
                    A(tmp[:, n % 2, :], tmp[:, n % 2, :], ACT.Exp).then_inc(a_exp, 1)
                feature_layout(1)
                for c in range(4):
                    act.wait_ge(a_h, c + 1)
                    A(a_hT[:, c, :], PS[:, c, :], ACT.Gelu, bias=W["a_b1"][:, c:c + 1]).then_inc(a_gelu, 1)

            def mixture(k, tr):
                act.wait_ge(tr_in, tr + 1)
                for tt in range(TT):
                    A(f_sq[:, tt, :], XN[:, tt, :], ACT.Square, accum_out=f_xx[:, tt:tt + 1]).then_inc(f_xxd, 1)
                feature_layout(tr)
                for c in range(4):
                    act.wait_ge(f_hp, 4 * k + c + 1)
                    A(f_h[:, c, :], PS[:, 2 + c % 2, :], ACT.Copy).then_inc(f_hs, 1)
                act.wait_ge(f_diff, k + 1)
                A(f_w[:, 1, :], f_w[:, 0, :], ACT.Exp, scale=f_negtinv[:, 0:1]).then_inc(f_e2, 1)
                act.wait_ge(f_gT, k + 1)
                A(f_gateT[0:N_EXPERT, :], PS[0:N_EXPERT, 1, :], ACT.Copy).then_inc(f_gTs, 1)

            def causal_attention():
                feature_layout(3)
                act.wait_ge(b_proj, 3)
                A(b_val[:, :, :, 0:B_HD], PS[:, 4, :].rearrange("p (t h d) -> p t h d", t=TT, h=B_HEADS),
                  ACT.Copy).then_inc(b_vs, 1)
                def maxima_rows(ib):
                    act.wait_ge(b_mT, ib + 1)
                    if ib >= 2:
                        act.wait_ge(b_mrows[ib % 2], 32)
                    A(b_maxT[0:48, ib % 2, :], PS[:, 3, :].bitcast(BF16)[0:48, 0:P], ACT.Copy).then_inc(b_mTs, 1)

                maxima_rows(0)
                for n in range(64):
                    w = P * (n // 16 + 1)
                    if n % 16 == 8 and n // 16 + 1 < TT:
                        maxima_rows(n // 16 + 1)
                    act.wait_ge(b_st, n + 1)
                    if n >= 4:
                        act.wait_ge(b_pv, n - 3)
                    A(b_pT[:, n % 4, 0:w], PS[:, 4 + n % 2, 0:w], ACT.Exp, scale=B_SCALE).then_inc(b_exp, 1)
                act.wait_ge(b_ot, 1)
                A(b_oT, PS[:, 4, :], ACT.Copy).then_inc(b_ots, 1)

            def phase_memory():
                feature_layout(5)
                for j in range(2):
                    act.wait_ge(c_zp, j + 1)
                    A(c_z[:, j, 0:3], const[:, 0:3], ACT.Copy, scale=0.0).then_inc(c_zs, 1)
                    A(c_z[:, j, 3:3 + T], PS[:, j, :], ACT.Copy).then_inc(c_zs, 1)
                act.wait_ge(c_lp, 1)
                A(c_pw, c_pw, ACT.Exp).then_inc(c_pws, 1)
                for c in range(C_CHUNKS):
                    act.wait_ge(c_up, c + 1)
                    if c >= 2:
                        act.wait_ge(c_frac, c - 1)
                    A(c_rr[:, c % 2, :], PS[:, c % 2, :], ACT.Copy, bias=MAGIC).then_inc(c_mag, 1)
                    act.wait_ge(c_frac, c + 1)
                    if c >= 2:
                        act.wait_ge(c_prod, 2 * (c - 1))
                    A(c_im[:, c % 2, :], c_ff[:, c % 2, :], ACT.Sin, scale=-TWO_PI).then_inc(c_trig, 1)
                    A(c_re[:, c % 2, :], c_ff[:, c % 2, :], ACT.Abs).then_inc(c_ab, 1)
                    act.wait_ge(c_ab, c + 1)
                    A(c_re[:, c % 2, :], c_re[:, c % 2, :], ACT.Sin, scale=-TWO_PI, bias=half_pi).then_inc(c_trig, 1)
                act.wait_ge(c_norm, 1)
                A(c_y, c_y, ACT.Silu).then_inc(c_silu, 1)

            def mixed_attention():
                feature_layout(7)
                for r in range(8):
                    act.wait_ge(e_vp, r + 1)
                    A(V[:, r // 2, 8 * (r % 2):8 * (r % 2) + 8, 0:E_HD],
                      PS[:, 4 + r % 2, :].rearrange("p (h d) -> p h d", h=8), ACT.Copy).then_inc(e_vs, 1)
                for ib in range(TT):
                    w = P * (ib + 1)
                    if ib:
                        act.wait_ge(e_pv, 2 * ib)
                    for h in range(E_HEADS):
                        act.wait_ge(e_sc, 16 * ib + h + 1)
                        A(S[:, h, 0:w], PS[:, h % 2, 0:w], ACT.Copy, scale=E_SCALE).then_inc(e_evac, 1)
                    for g in range(GROUPS):
                        n = GROUPS * ib + g
                        act.wait_ge(e_hadd, 2 * n + 2)
                        hid = e_hidden[:, n % 2, :, 0:width(ib, g)]
                        A(hid, hid, ACT.Gelu).then_inc(e_gelu, 1)
                    act.wait_ge(e_nmx, ib + 1)
                    for g in range(GROUPS):
                        f = FREG[:, g, 0:width(ib, g)]
                        A(f, f, ACT.Exp, bias=negmx[:, g:g + 1], accum_out=e_sum[:, g:g + 1]).then_inc(e_exp, 1)
                    for j in range(2):
                        act.wait_ge(e_pv, 2 * ib + j + 1)
                        A(e_oT[:, 512 * j:512 * (j + 1)], PS[:, 4 + j, :], ACT.Copy).then_inc(e_ots, 1)

            with act.Fori(0, B) as b:
                act_count[0] = 0
                linear_attention()
                if last >= 2:
                    mixture(0, 2)
                if last >= 3:
                    causal_attention()
                if last >= 4:
                    mixture(1, 4)
                if last >= 5:
                    phase_memory()
                if last >= 6:
                    feature_layout(6)
                if last >= 7:
                    mixed_attention()
                if last >= 8:
                    feature_layout(8)
                act.drain().then_inc(sequence_ended, 1)
                act.wait_ge(sequence_go, b + 1)

        @block.vector
        def _(dve):
            V_ = nc.vector
            count = [0]

            def settle(ins):
                count[0] += 1
                ins.then_inc(dve_step, 1)
                dve.wait_ge(dve_step, count[0])

            done = [0]

            def setup(ins):
                done[0] += 1
                ins.then_inc(setup_dve, 1)
                dve.wait_ge(setup_dve, done[0])
            dve.wait_ge(w_loaded["c"], 16)
            dve.wait_ge(w_loaded["d"], 16)
            dve.wait_ge(w_loaded["e"], 16)
            dve.wait_ge(setup_act, 3)
            setup(V_.scalar_tensor_tensor(small[:, 9:12], W["softplus_in"], 0.0, small[:, 6:9], ALU.max, ALU.add))
            setup(V_.tensor_scalar(c_logdecay, c_logdecay, small[:, 9:10], -1.0, ALU.mult, ALU.mult))
            setup(V_.tensor_scalar(W["c_theta"], W["c_theta"], float(1.0 / (2.0 * np.pi)), None, ALU.mult))
            setup(V_.tensor_tensor(W["c_norm"], W["c_norm"], W["c_diag"], ALU.mult))
            c1, c2 = (W["c_norm"][:, j * P:(j + 1) * P].unsqueeze(1).to_broadcast([P, C_KQ, P]) for j in range(2))
            qre, qim = (W[n].rearrange("p (k n) -> p k n", k=C_KQ) for n in ("c_qre", "c_qim"))
            t1, t2, t3, t4 = (tmp[:, j, :].rearrange("p (k n) -> p k n", k=C_KQ) for j in range(4))
            for dst, q, c in ((t1, qre, c1), (t2, qim, c2), (t3, qim, c1), (t4, qre, c2)):
                setup(V_.tensor_tensor(dst, q, c, ALU.mult))
            setup(V_.tensor_tensor(qre, t1, t2, ALU.subtract))
            setup(V_.tensor_tensor(qim, t3, t4, ALU.add))
            dve.wait_ge(w_loaded["f"], 16)
            setup(V_.tensor_tensor(f_proto2[:, :], W["f_proto"], W["f_proto"], ALU.mult))
            setup(V_.tensor_scalar(small[:, 12:13], W["f_temp"], -1.0, None, ALU.mult))
            setup(V_.tensor_tensor(small[:, 12:13], small[:, 12:13], W["f_temp"], ALU.max))
            setup(V_.tensor_scalar(small[:, 12:13], small[:, 12:13], 0.1, -1.0, ALU.max, ALU.mult))
            setup(V_.reciprocal(f_negtinv[:, :], small[:, 12:13]))
            dve.wait_ge(setup_pe, 4)
            setup(V_.tensor_tensor(d_weight[:, :], PS[:, 3, 0:D], W["d_w"], ALU.add))
            dve.wait_ge(w_loaded["a"], 16)
            setup(V_.tensor_copy(mask_tile[:, 0:2 * P], W["causal_masks"]))
            setup(V_.tensor_copy(ident_bf, ident))
            dve.wait_ge(setup_act, 4)
            setup(V_.tensor_scalar(e_kerple, e_kerple, small[:, 10:11], -1.0, ALU.mult, ALU.mult))
            KERPLE_READY = done[0]
            setup(V_.scalar_tensor_tensor(e_bias_table, e_kerple, W["e_b2"], e_bias_table, ALU.add, ALU.add))
            for half in range(2):
                dve.wait_ge(setup_pe, 5 + half)
                setup(V_.tensor_scalar(e_hidden_table[:, half, 0:512], PS[:, 4 + half, :], W["e_b1"], None, ALU.add))
                setup(V_.tensor_scalar(e_hidden_table[:, half, 512:TABLE], PS[:, 6 + half, 0:STEP], W["e_b1"], None, ALU.add))
            assert KERPLE_READY == SETUP_KERPLE and done[0] == SETUP_DVE

            def ln_stats(k, src):
                for tt in range(TT):
                    ins = V_.bn_stats(stats[:, tt, :], src[:, tt, :])
                settle(ins)
                for tt in range(TT):
                    ins = V_.bn_aggr(mv[:, tt, :], stats[:, tt, :])
                settle(ins)
                V_.tensor_scalar(varp[:, :], mv[:, :, 1], EPS_LN, None, ALU.add).then_inc(ln_var, 1)
                dve.wait_ge(ln_rstd, k + 1)

            def normalise(dst, src):
                for tt in range(TT):
                    ins = V_.tensor_scalar(dst[:, tt, :], src[:, tt, :], mv[:, tt, 0:1], rstd[:, tt:tt + 1],
                                           ALU.subtract, ALU.mult)
                return ins

            def layer_norm(k):
                ln_stats(k, X)
                normalise(XN, X).then_inc(tr_in, 1)

            def add_y(y_no):
                dve.wait_ge(y_psum, y_no)
                settle(V_.tensor_tensor(X[:, :, :], PS[:, 6, :].rearrange("p (t d) -> p t d", t=TT), X[:, :, :], ALU.add))

            def scaled_and_shifted(buf):
                for name, op in (("a_gamma", ALU.mult), ("a_beta", ALU.add)):
                    row = W[name].unsqueeze(1).to_broadcast([P, TT, D])
                    ins = V_.tensor_tensor(buf, buf, row, op)
                    if name == "a_gamma":
                        settle(ins)
                return ins

            def linear_attention():
                layer_norm(0)
                dve.wait_ge(tr_in, 1)
                dve.wait_ge(a_proj, 3)
                V_.tensor_copy(v_aug[:, :, 0:D], PS[:, 2, :].rearrange("p (t d) -> p t d", t=TT)).then_inc(a_v, 1)
                feats = [a_qf[:, c, :] for c in range(4)] + [a_kf[:, c, :] for c in range(4)]
                for n in range(9):
                    if n < 8:
                        dve.wait_ge(a_fpre, n + 1)
                        if n >= 2:
                            dve.wait_ge(a_feat, n - 1)
                        V_.tensor_scalar(tmp[:, n % 2, :], PS[:, 3 + n % 3, :], 0.0, None, ALU.min).then_inc(a_neg, 1)
                    if n >= 1:
                        m = n - 1
                        dve.wait_ge(a_exp, m + 1)
                        V_.scalar_tensor_tensor(feats[m], PS[:, 3 + m % 3, :], 0.0, tmp[:, m % 2, :],
                                                ALU.max, ALU.add).then_inc(a_feat, 1)
                mask = W["a_kv_mask"].rearrange("p (c n) -> p c n", c=4)
                for c in range(4):
                    dve.wait_ge(a_kv, 2 * (c // 2) + 2)
                    at = (c % 2) * (D + 1)
                    V_.tensor_tensor(a_kvbd[:, c, :], PS[:, c // 2, at:at + D], mask[:, c, :], ALU.mult).then_inc(a_masked, 1)
                    V_.tensor_scalar(a_zbd[:, c, :], mask[:, c, :], PS[:, c // 2, at + D:at + D + 1], None, ALU.mult).then_inc(a_masked, 1)
                dve.wait_ge(a_att, 2)
                settle(V_.tensor_scalar(a_z, PS[:, 3, :], EPS_ATTN, None, ALU.add))
                settle(V_.reciprocal(a_z, a_z))
                V_.tensor_tensor(a_attn, PS[:, 2, :], a_z, ALU.mult).then_inc(a_attn_ready, 1)
                dve.wait_ge(y_psum, 1)
                settle(V_.tensor_tensor(a_r, PS[:, 6, :].rearrange("p (t d) -> p t d", t=TT), XN[:, :, :], ALU.add))
                ln_stats(1, a_r)
                settle(normalise(a_r, a_r))
                scaled_and_shifted(a_r).then_inc(tr_in, 1)
                dve.wait_ge(tr_in, 2)
                dve.wait_ge(y_psum, 2)
                settle(V_.tensor_tensor(a_y, PS[:, 6, :].rearrange("p (t d) -> p t d", t=TT), a_r, ALU.add))
                ln_stats(2, a_y)
                settle(normalise(a_y, a_y))
                settle(scaled_and_shifted(a_y))
                settle(V_.tensor_tensor(X[:, :, :], X[:, :, :], a_y, ALU.add))

            def mixture(k, ln_no, y_no):
                layer_norm(ln_no)
                dve.wait_ge(f_xp, k + 1)
                dve.wait_ge(f_xxd, 4 * (k + 1))
                for tt in range(TT):
                    ins = V_.tensor_scalar(f_d[:, tt, :], f_p2[:, :], f_xx[:, tt:tt + 1], None, ALU.add)
                settle(ins)
                settle(V_.scalar_tensor_tensor(f_d, PS[:, 0, 0:TT * N_EXPERT].rearrange("p (t e) -> p t e", t=TT), 2.0,
                                               f_d, ALU.mult, ALU.subtract))
                settle(V_.tensor_scalar(f_d, f_d, 0.0, None, ALU.min))
                for tt in range(TT):
                    ins = V_.max(f_top[:, tt, :], f_d[:, tt, :])
                settle(ins)
                V_.tensor_scalar(f_near, f_top[:, :, 0:2], -1.0, None, ALU.mult).then_inc(f_d2, 1)
                idx = f_idx.bitcast(U32)
                for tt in range(TT):
                    ins = V_.max_index(idx[:, tt, :], f_top[:, tt, :], f_d[:, tt, :])
                settle(ins)
                settle(V_.tensor_copy(f_idxf, idx))
                dve.wait_ge(f_dist, k + 1)
                V_.tensor_tensor(f_w[:, 0, :], f_near[:, :, 1], f_near[:, :, 0], ALU.subtract).then_inc(f_diff, 1)
                dve.wait_ge(f_e2, k + 1)
                settle(V_.tensor_scalar(f_w[:, 2, :], f_w[:, 1, :], 1.0, None, ALU.add))
                settle(V_.reciprocal(f_w[:, 2, :], f_w[:, 2, :]))
                settle(V_.tensor_tensor(f_w[:, 3, :], f_w[:, 1, :], f_w[:, 2, :], ALU.mult))
                for tt in range(TT):
                    for j in range(2):
                        ins = V_.tensor_scalar(f_gate[:, TT * j + tt, :], W["expert_no"], f_idxf[:, tt, j:j + 1],
                                               f_w[:, 2 + j, tt:tt + 1], ALU.is_equal, ALU.mult)
                settle(ins)
                V_.tensor_tensor(f_gate[:, 0:TT, :], f_gate[:, 0:TT, :], f_gate[:, TT:, :], ALU.add).then_inc(f_gated, 1)
                dve.wait_ge(f_hs, 4 * (k + 1))
                for c in range(4):
                    dve.wait_ge(f_spread_up, 4 * k + c + 1)
                    V_.tensor_tensor(f_h[:, c, :], PS[:, 2 + c, :], f_h[:, c, :], ALU.mult).then_inc(f_gh, 1)
                add_y(y_no)

            def causal_attention():
                layer_norm(4)
                for j, dst in enumerate((b_q, b_k)):
                    dve.wait_ge(b_proj, j + 1)
                    bias = W["b_bias"]
                    V_.scalar_tensor_tensor(tmp[:, 0, :], PS[:, 2 * j, :], bias[:, 2 * j:2 * j + 1], W["b_cos"], ALU.add, ALU.mult)
                    settle(V_.scalar_tensor_tensor(tmp[:, 1, :], PS[:, 2 * j + 1, :], bias[:, 2 * j + 1:2 * j + 2],
                                                   W["b_sin"], ALU.add, ALU.mult))
                    settle(V_.tensor_tensor(dst, tmp[:, 0, :], tmp[:, 1, :], ALU.add))
                    V_.tensor_copy(b_parts[:, 3 * j, :], dst).then_inc(b_split, 1)
                    dve.wait_ge(b_split, 3 * j + 1)
                    settle(V_.tensor_tensor(b_rest, dst, b_parts[:, 3 * j, :], ALU.subtract))
                    V_.tensor_copy(b_parts[:, 3 * j + 1, :], b_rest).then_inc(b_split, 1)
                    dve.wait_ge(b_split, 3 * j + 2)
                    V_.tensor_tensor(b_parts[:, 3 * j + 2, :], b_rest, b_parts[:, 3 * j + 1, :], ALU.subtract).then_inc(b_split, 1)

                def row_max(ib, h):
                    n = 16 * ib + h
                    dve.wait_ge(b_sc, n + 1)
                    V_.tensor_reduce(mx[:, h:h + 1], PS[:, n % 3, 0:P * (ib + 1)], AX.X, ALU.max).then_inc(b_max, 1)

                def max_parts(ib):
                    dve.wait_ge(b_max, 16 * (ib + 1))
                    if ib:
                        dve.wait_ge(b_mT, ib)
                    settle(V_.tensor_scalar(b_negmax, mx[:, 0:16], -1.0, None, ALU.mult))
                    neg, rest = (v.rearrange("p (b a) -> p a b", a=2) for v in (b_negmax, b_maxrest))
                    parts = b_maxparts.rearrange("p (a s b) -> p a s b", a=2, s=3)
                    settle(V_.tensor_copy(parts[:, :, 0, :], neg))
                    settle(V_.tensor_tensor(rest, neg, parts[:, :, 0, :], ALU.subtract))
                    settle(V_.tensor_copy(parts[:, :, 1, :], rest))
                    V_.tensor_tensor(parts[:, :, 2, :], rest, parts[:, :, 1, :], ALU.subtract).then_inc(b_mparts, 1)

                def normalised(ib):
                    dve.wait_ge(b_pv, 16 * (ib + 1))
                    if ib:
                        dve.wait_ge(b_od, ib)
                    o = PS[:, 6 + ib % 2, 0:B_HEADS * (B_HD + 1)].rearrange("p (h d) -> p h d", h=B_HEADS)
                    settle(V_.reciprocal(b_rs, o[:, :, B_HD]))
                    V_.tensor_tensor(b_o[:, ib, :].rearrange("p (h d) -> p h d", h=B_HEADS), o[:, :, 0:B_HD],
                                     b_rs.unsqueeze(2).to_broadcast([P, B_HEADS, B_HD]), ALU.mult).then_inc(b_od, 1)

                for ib in range(2):
                    for h in range(16):
                        row_max(ib, h)
                    max_parts(ib)
                for ib in range(TT):
                    if ib + 2 < TT:
                        for h in range(16):
                            row_max(ib + 2, h)
                        max_parts(ib + 2)
                    normalised(ib)
                add_y(4)

            def phase_memory():
                layer_norm(6)
                taps = [W["c_taps_key"], W["c_taps_decay"]]
                for j in range(2):
                    dve.wait_ge(c_zs, 2 * j + 2)
                    settle(V_.tensor_scalar(c_conv[:, j, :], c_z[:, j, 0:T], taps[j][:, 0:1], None, ALU.mult))
                    for s in range(1, C_TAPS):
                        ins = V_.scalar_tensor_tensor(c_conv[:, j, :], c_z[:, j, s:s + T], taps[j][:, s:s + 1],
                                                      c_conv[:, j, :], ALU.mult, ALU.add)
                        if s < C_TAPS - 1:
                            settle(ins)
                    ins.then_inc(c_cv, 1)
                dve.wait_ge(c_cv, 2)
                settle(V_.tensor_scalar(c_pw, c_conv[:, 1, :], W["c_score_scale"], 20.0, ALU.mult, ALU.min))
                V_.scalar_tensor_tensor(c_pw, c_pw, -20.0, c_logdecay, ALU.max, ALU.add).then_inc(c_lp, 1)
                ones = one_col.to_broadcast([P, T])
                dve.wait_ge(c_pws, 1)
                settle(V_.tensor_tensor_scan(c_inv, ones, c_pw, 0.0, ALU.mult, ALU.add))
                settle(V_.tensor_scalar(c_inv, c_inv, 0.0001, None, ALU.max))
                settle(V_.reciprocal(c_inv, c_inv))
                for c in range(C_CHUNKS):
                    i = c % 2
                    dve.wait_ge(c_mag, c + 1)
                    if c >= 2:
                        dve.wait_ge(c_trig, 2 * (c - 1))
                        dve.wait_ge(c_ab, c - 1)
                    V_.scalar_tensor_tensor(c_ff[:, i, :], c_rr[:, i, :], MAGIC, PS[:, i, :], ALU.subtract, ALU.subtract).then_inc(c_frac, 1)
                    dve.wait_ge(c_trig, 2 * c + 2)
                    dve.wait_ge(c_pwx, c + 1)
                    if c >= 2:
                        dve.wait_ge(c_sum, c - 1)
                    V_.tensor_tensor(c_pr[:, i, :], PS[:, 2 + i, :], c_re[:, i, :], ALU.mult)
                    V_.tensor_tensor(c_pi[:, i, :], PS[:, 2 + i, :], c_im[:, i, :], ALU.mult).then_inc(c_prod, 2)
                    dve.wait_ge(c_prod, 2 * c + 2)
                    V_.tensor_tensor_scan(c_nr[:, i, :], ones, c_pr[:, i, :], 0.0, ALU.mult, ALU.add)
                    settle(V_.tensor_tensor_scan(c_ni[:, i, :], ones, c_pi[:, i, :], 0.0, ALU.mult, ALU.add))
                    dve.wait_ge(c_query, c // 2 + 1)
                    V_.tensor_tensor(c_pr[:, i, :], PS[:, 4, :], c_nr[:, i, :], ALU.mult)
                    V_.tensor_tensor(c_pi[:, i, :], PS[:, 5, :], c_ni[:, i, :], ALU.mult).then_inc(c_weighted, 1)
                dve.wait_ge(c_sum, C_CHUNKS)
                V_.tensor_tensor(c_y, PS[:, 6, :], c_inv, ALU.mult).then_inc(c_norm, 1)
                add_y(6)

            def mixed_attention():
                layer_norm(8)
                for n in range(16):
                    dve.wait_ge(e_qk, n + 1)
                    if n >= 2:
                        dve.wait_ge(e_add, n - 1)
                    k = 2 * (n % 2)
                    V_.tensor_tensor(tmp[:, k, :], PS[:, k, :], W["e_cos"], ALU.mult)
                    V_.tensor_tensor(tmp[:, k + 1, :], PS[:, k + 1, :], W["e_sin"], ALU.mult).then_inc(e_rope, 1)
                for ib in range(TT):
                    def hidden(n):
                        g = n % GROUPS
                        w, at = width(ib, g), table_at(ib, g)
                        for half in range(2):
                            dve.wait_ge(e_m1, 2 * n + half + 1)
                            if half == 0 and n >= 2:
                                dve.wait_ge(e_m2, n - 1)
                            V_.tensor_tensor(e_hidden[:, n % 2, half, 0:w], PS[:, 2 + 2 * (n % 2) + half, 0:w],
                                             e_hidden_table[:, half, at:at + w], ALU.add).then_inc(e_hadd, 1)

                    hidden(GROUPS * ib)
                    for g in range(GROUPS):
                        n = GROUPS * ib + g
                        w = width(ib, g)
                        if g + 1 < GROUPS:
                            hidden(n + 1)
                        dve.wait_ge(e_m2, n + 1)
                        dve.wait_ge(e_fk, n + 1)
                        f = FREG[:, g, 0:w]
                        V_.tensor_tensor_reduce(out=f, in0=PS[:, 6 + n % 2, 0:w], in1=f, scale=1.0, scalar=-3e38,
                                                op0=ALU.add, op1=ALU.max, accum_out=mx[:, g:g + 1]).then_inc(e_fin, 1)
                    dve.wait_ge(e_fin, GROUPS * (ib + 1))
                    V_.tensor_scalar(negmx[:, :], mx[:, :], -1.0, None, ALU.mult).then_inc(e_nmx, 1)
                    first = 4 * sum(range(1, ib + 1))

                    def divide(gq):
                        q = slice(4 * gq, 4 * gq + 4)
                        dve.wait_ge(e_exp, GROUPS * ib + 4 * gq + 4)
                        settle(V_.reciprocal(e_rs[:, q], e_sum[:, q]))
                        for g in range(4 * gq, 4 * gq + 4):
                            f = FREG[:, g, 0:width(ib, g)]
                            ins = V_.tensor_scalar(f, f, e_rs[:, g:g + 1], None, ALU.mult)
                        ins.then_inc(e_div, 1)

                    divide(0)
                    for k in range(4 * (ib + 1)):
                        gq, jb = k // (ib + 1), k % (ib + 1)
                        if jb == 0 and gq < 3:
                            divide(gq + 1)
                        dve.wait_ge(e_tp, first + k + 1)
                        V_.tensor_copy(PT[:, jb, 32 * gq:32 * gq + 32, :].rearrange("p i h -> p (i h)"),
                                       PS[:, 2 + k % 4, :]).then_inc(e_ptc, 1)
                    dve.wait_ge(e_y, ib + 1)
                    V_.tensor_tensor(X[:, ib, :], PS[:, 7, 0:D], X[:, ib, :], ALU.add).then_inc(e_x, 1)
                dve.wait_ge(e_x, TT)

            with dve.Fori(0, B) as b:
                count[0] = 0
                dve.wait_ge(x_loaded, 16)
                linear_attention()
                if last >= 2:
                    mixture(0, 3, 3)
                if last >= 3:
                    causal_attention()
                if last >= 4:
                    mixture(1, 5, 5)
                if last >= 5:
                    phase_memory()
                if last >= 6:
                    layer_norm(7)
                    add_y(7)
                if last >= 7:
                    mixed_attention()
                if last >= 8:
                    layer_norm(9)
                    add_y(8)
                dve.nop().then_inc(x_done, 1)
                dve.drain().then_inc(sequence_ended, 1)
                dve.wait_ge(sequence_go, b + 1)

        @block.tensor
        def _(pe):
            mm = nc.tensor.matmul

            pe.wait_ge(setup_pool, 6)
            pe.wait_ge(rows_loaded, 16)
            pe.wait_ge(setup_dve, 11)
            mm(PS[:, 0, 0:N_EXPERT], one_col.to_broadcast([P, P]), f_proto2[:, :], start=True, stop=True).then_inc(setup_pe, 1)
            pe.wait_ge(w_loaded["d"], 16)
            mm(PS[0:4, 1, 0:P], W["d_lora_down"][0:100, :], W["d_down_aux"][0:100, :], start=True, stop=True).then_inc(setup_pe, 1)
            pe.wait_ge(setup_act, 6)
            mm(PS[0:50, 2, 0:P], W["d_lora_up"][0:4, :], tmp[0:4, 0, 0:P], start=True, stop=True).then_inc(setup_pe, 1)
            pe.wait_ge(setup_act, 7)
            mm(PS[:, 3, 0:P], tmp[0:50, 1, 0:P], W["d_up_aux"][0:50, :], start=True, stop=True).then_inc(setup_pe, 1)
            pe.wait_ge(w_loaded["e"], 16)
            pe.wait_ge(setup_dve, SETUP_KERPLE)
            for half in range(2):
                w = W["e_mix_kerple"][:, P * half:P * (half + 1)]
                mm(PS[:, 4 + half, :], w, e_kerple[:, 0:512], start=True, stop=True)
                mm(PS[:, 6 + half, 0:STEP], w, e_kerple[:, 512:TABLE], start=True, stop=True).then_inc(setup_pe, 1)

            def feature_layout(k, src):
                pe.wait_ge(tr_in, k + 1)
                for tt in range(TT):
                    ins = nc.tensor.transpose(PS[:, 7, P * tt:P * (tt + 1)], src[:, tt, :], ident)
                ins.then_inc(tr_psum, 1)

            def tok(t, tt):
                return t[:, P * tt:P * (tt + 1)]

            def linear_attention():
                pe.wait_ge(w_loaded["a"], 16)
                feature_layout(0, XN)
                pe.wait_ge(xT_ready, 1)
                mm(PS[:, 0, :], W["a_qkv"][:, 0:D], XT[:, :], start=True, stop=True).then_inc(a_proj, 1)
                mm(PS[:, 1, :], W["a_qkv"][:, D:2 * D], XT[:, :], start=True, stop=True).then_inc(a_proj, 1)
                for tt in range(TT):
                    ins = mm(PS[:, 2, D * tt:D * (tt + 1)], tok(XT, tt), W["a_qkv"][:, 2 * D:3 * D], start=True, stop=True)
                ins.then_inc(a_proj, 1)
                for n in range(8):
                    c = n % 4
                    pe.wait_ge(a_qk, 1 if n < 4 else 2)
                    if n >= 3:
                        pe.wait_ge(a_feat, n - 2)
                    bank = PS[:, 3 + n % 3, :]
                    if n < 4:
                        ins = mm(bank, W["a_features"][:, P * c:P * (c + 1)], a_qT, start=True, stop=True)
                    else:
                        ins = mm(bank, tok(a_kT, c), W["a_features"], start=True, stop=True)
                    ins.then_inc(a_fpre, 1)
                pe.wait_ge(a_feat, 8)
                pe.wait_ge(a_v, 1)
                for c in range(4):
                    at = (c % 2) * (D + 1)
                    for tt in range(TT):
                        ins = mm(PS[:, c // 2, at:at + D + 1], a_kf[:, tt, P * c:P * (c + 1)], v_aug[:, tt, :],
                                 start=tt == 0, stop=tt == TT - 1)
                    ins.then_inc(a_kv, 1)
                pe.wait_ge(a_masked, 8)
                for bank, w in ((2, a_kvbd), (3, a_zbd)):
                    for c in range(4):
                        ins = mm(PS[:, bank, :], w[:, c, :], a_qf[:, c, :], start=c == 0, stop=c == 3)
                    ins.then_inc(a_att, 1)
                pe.wait_ge(a_attn_ready, 1)
                for tt in range(TT):
                    y = PS[:, 6, D * tt:D * (tt + 1)]
                    mm(y, tok(a_attn, tt), W["a_out"], start=True, stop=False)
                    ins = mm(y, R["ones"], R["a_bo"], start=False, stop=True)
                ins.then_inc(y_psum, 1)
                feature_layout(1, a_r)
                pe.wait_ge(xT_ready, 2)
                for c in range(4):
                    mm(PS[:, c, :], W["a_w1"][:, P * c:P * (c + 1)], XT[:, :], start=True, stop=True).then_inc(a_h, 1)
                pe.wait_ge(a_gelu, 4)
                w2 = W["a_w2"].rearrange("p (c d) -> p c d", c=4)
                for tt in range(TT):
                    y = PS[:, 6, D * tt:D * (tt + 1)]
                    for c in range(4):
                        mm(y, tok(a_hT[:, c, :], tt), w2[:, c, :], start=c == 0, stop=False)
                    ins = mm(y, R["ones"], R["a_b2"], start=False, stop=True)
                ins.then_inc(y_psum, 1)

            def mixture(k, tr):
                feature_layout(tr, XN)
                pe.wait_ge(xT_ready, tr + 1)
                for tt in range(TT):
                    d = PS[:, 0, N_EXPERT * tt:N_EXPERT * (tt + 1)]
                    ins = mm(d, tok(XT, tt), W["f_proto"], start=True, stop=True)
                ins.then_inc(f_xp, 1)
                for c in range(4):
                    if c >= 2:
                        pe.wait_ge(f_hs, 4 * k + c - 1)
                    mm(PS[:, 2 + c % 2, :], W["f_down"][:, P * c:P * (c + 1)], XT[:, :], start=True, stop=True).then_inc(f_hp, 1)
                pe.wait_ge(f_gated, k + 1)
                for tt in range(TT):
                    ins = nc.tensor.transpose(PS[0:N_EXPERT, 1, P * tt:P * (tt + 1)], f_gate[:, tt, :], ident)
                ins.then_inc(f_gT, 1)
                pe.wait_ge(f_gTs, k + 1)
                pe.wait_ge(f_hs, 4 * (k + 1))
                gT = f_gateT[0:N_EXPERT, :]
                for c in range(4):
                    mm(PS[:, 2 + c, :], W["f_spread"][0:N_EXPERT, P * c:P * (c + 1)], gT, start=True, stop=True).then_inc(f_spread_up, 1)
                pe.wait_ge(f_gh, 4 * (k + 1))
                up = W["f_up"].rearrange("p (c d) -> p c d", c=4)
                for tt in range(TT):
                    y = PS[:, 6, D * tt:D * (tt + 1)]
                    for c in range(4):
                        mm(y, tok(f_h[:, c, :], tt), up[:, c, :], start=c == 0, stop=False)
                    ins = mm(y, gT[:, P * tt:P * (tt + 1)], W["f_bias"][0:N_EXPERT, :], start=False, stop=True)
                ins.then_inc(y_psum, 1)

            def causal_attention():
                feature_layout(3, XN)
                pe.wait_ge(xT_ready, 4)
                for j, name in enumerate(("b_q", "b_qrot", "b_k", "b_krot")):
                    ins = mm(PS[:, j, :], W[name], XT[:, :], start=True, stop=True)
                    if j % 2 == 1:
                        ins.then_inc(b_proj, 1)
                for tt in range(TT):
                    v = PS[:, 4, D * tt:D * (tt + 1)]
                    mm(v, tok(XT, tt), W["b_v"], start=True, stop=False)
                    ins = mm(v, R["ones"], R["b_bv"], start=False, stop=True)
                ins.then_inc(b_proj, 1)

                def scores(ib, h):
                    n, at, blk = 16 * ib + h, 64 * (h % 2), h // 2
                    if n >= 3:
                        pe.wait_ge(b_max, n - 2)
                    mm(PS[:, n % 3, 0:P * (ib + 1)], b_qs[at:at + B_ROWS, blk, P * ib:P * (ib + 1)],
                       b_ks[at:at + B_ROWS, blk, 0:P * (ib + 1)], start=True, stop=False)
                    mm(PS[:, n % 3, P * ib:P * (ib + 1)], ident_bf, causal_mask, start=False, stop=True).then_inc(b_sc, 1)

                def maxima_T(ib):
                    pe.wait_ge(b_mparts, ib + 1)
                    if ib:
                        pe.wait_ge(b_mTs, ib)
                    nc.tensor.transpose(PS[:, 3, :].bitcast(BF16)[0:48, 0:P], b_maxparts, ident_bf).then_inc(b_mT, 1)

                def scores_T(n):
                    ib, h = n // 16, n % 16
                    at, blk = 64 * (h % 2), h // 2
                    rows = slice(at, at + B_ROWS + 3)
                    if n >= 2:
                        pe.wait_ge(b_exp, n - 1)
                    for jb in range(ib + 1):
                        ins = mm(PS[:, 4 + n % 2, P * jb:P * (jb + 1)], b_ks[rows, blk, P * jb:P * (jb + 1)],
                                 b_qs[rows, blk, P * ib:P * (ib + 1)], start=True, stop=jb < ib)
                    mm(PS[:, 4 + n % 2, P * ib:P * (ib + 1)], ident_bf, causal_mask_T, start=False, stop=True).then_inc(b_st, 1)

                def times_v(n):
                    ib, h = n // 16, n % 16
                    pe.wait_ge(b_exp, n + 1)
                    if h == 0 and ib >= 2:
                        pe.wait_ge(b_od, ib - 1)
                    o = PS[:, 6 + ib % 2, (B_HD + 1) * h:(B_HD + 1) * (h + 1)]
                    for jb in range(ib + 1):
                        ins = mm(o, b_pT[:, n % 4, P * jb:P * (jb + 1)], b_val[:, jb, h, :], start=jb == 0, stop=jb == ib)
                    ins.then_inc(b_pv, 1)

                pe.wait_ge(b_vs, 1)
                pe.wait_ge(b_spread, 24 * 16)
                for h in range(16):
                    scores(0, h)
                for h in range(16):
                    scores(1, h)
                    if h == 3:
                        maxima_T(0)
                for n in range(64):
                    ib, h = n // 16, n % 16
                    if h == 0:
                        pe.wait_ge(b_mrows[ib % 2], 32 * (ib // 2 + 1))
                    scores_T(n)
                    if n:
                        times_v(n - 1)
                    if ib + 2 < TT:
                        scores(ib + 2, h)
                    if h == 3 and ib + 1 < TT:
                        maxima_T(ib + 1)
                times_v(63)
                pe.wait_ge(b_od, TT)
                for ib in range(TT):
                    ins = nc.tensor.transpose(PS[:, 4, P * ib:P * (ib + 1)], b_o[:, ib, :], ident)
                ins.then_inc(b_ot, 1)
                pe.wait_ge(b_ots, 1)
                for tt in range(TT):
                    y = PS[:, 6, D * tt:D * (tt + 1)]
                    mm(y, tok(b_oT, tt), W["b_out"], start=True, stop=False)
                    ins = mm(y, R["ones"], R["b_bo"], start=False, stop=True)
                ins.then_inc(y_psum, 1)

            def phase_memory():
                feature_layout(5, XN)
                pe.wait_ge(xT_ready, 6)
                for j, name in enumerate(("c_key", "c_decay")):
                    mm(PS[:, j, :], W[name], XT[:, :], start=True, stop=True).then_inc(c_zp, 1)
                pe.wait_ge(c_zs, 4)
                pe.wait_ge(c_cv, 1)
                for c in range(C_CHUNKS):
                    cols = slice(P * c, P * (c + 1))
                    if c >= 2:
                        pe.wait_ge(c_frac, c - 1)
                    mm(PS[:, c % 2, :], W["c_theta"][:, cols], c_conv[:, 0, :], start=True, stop=True).then_inc(c_up, 1)
                    if c == 0:
                        pe.wait_ge(c_pws, 1)
                    if c >= 2:
                        pe.wait_ge(c_prod, 2 * (c - 1))
                    mm(PS[:, 2 + c % 2, :], W["c_spread"][:, cols], c_pw, start=True, stop=True).then_inc(c_pwx, 1)
                    if c >= 1:
                        gather(c - 1)
                    if c % 2 == 0:
                        kq = c // 2
                        mm(PS[:, 4, :], W["c_qre"][:, P * kq:P * (kq + 1)], XT[:, :], start=True, stop=True)
                        mm(PS[:, 5, :], W["c_qim"][:, P * kq:P * (kq + 1)], XT[:, :], start=True, stop=True).then_inc(c_query, 1)
                gather(C_CHUNKS - 1)
                pe.wait_ge(c_silu, 1)
                for tt in range(TT):
                    ins = mm(PS[:, 6, D * tt:D * (tt + 1)], tok(c_y, tt), W["c_out"], start=True, stop=True)
                ins.then_inc(y_psum, 1)

            def gather(c):
                pe.wait_ge(c_weighted, c + 1)
                w = W["c_gather"][:, P * c:P * (c + 1)]
                mm(PS[:, 6, :], w, c_pr[:, c % 2, :], start=c == 0, stop=False)
                mm(PS[:, 6, :], w, c_pi[:, c % 2, :], start=False, stop=c == C_CHUNKS - 1).then_inc(c_sum, 1)

            def adapted_linear(tr):
                feature_layout(tr, XN)
                pe.wait_ge(xT_ready, tr + 1)
                for tt in range(TT):
                    y = PS[:, 6, D * tt:D * (tt + 1)]
                    mm(y, tok(XT, tt), d_weight[:, :], start=True, stop=False)
                    ins = mm(y, R["ones"], R["d_b"], start=False, stop=True)
                ins.then_inc(y_psum, 1)

            def mixed_attention():
                feature_layout(7, XN)
                pe.wait_ge(xT_ready, 8)
                pe.wait_ge(e_w, 16)
                n_ch = E_HEADS * E_HD
                for n in range(16):
                    at = 2 * n_ch * (n % 2) + P * (n // 2)
                    k = 2 * (n % 2)
                    if n >= 2:
                        pe.wait_ge(e_rope, n - 1)
                    mm(PS[:, k, :], proj[:, at:at + P], XT[:, :], start=True, stop=True)
                    mm(PS[:, k + 1, :], proj[:, at + n_ch:at + n_ch + P], XT[:, :], start=True, stop=True).then_inc(e_qk, 1)
                for r in range(8):
                    if r >= 2:
                        pe.wait_ge(e_vs, r - 1)
                    mm(PS[:, 4 + r % 2, :], tok(XT, r // 2), proj[:, 4 * n_ch + 512 * (r % 2):4 * n_ch + 512 * (r % 2 + 1)],
                       start=True, stop=True).then_inc(e_vp, 1)
                pe.wait_ge(e_rope, 16)
                pe.wait_ge(e_add, 16)
                pe.wait_ge(e_vs, 8)

                def scores(ib):
                    w = P * (ib + 1)
                    for h in range(E_HEADS):
                        n = 16 * ib + h
                        if n >= 2:
                            pe.wait_ge(e_evac, n - 1)
                        at = 64 * (h % 2)
                        mm(PS[:, h % 2, 0:w], QT[at:at + 64, h // 2, P * ib:P * (ib + 1)], KT[at:at + 64, h // 2, 0:w],
                           start=True, stop=True).then_inc(e_sc, 1)

                scores(0)
                for ib in range(TT):
                    def mix(n):
                        g = n % GROUPS
                        pe.wait_ge(e_dma[g // 4], 64 * (ib + 1))
                        if g == 0 and ib:
                            pe.wait_ge(e_x, ib)
                        if n >= 2:
                            pe.wait_ge(e_hadd, 2 * (n - 1))
                        for half in range(2):
                            mm(PS[:, 2 + 2 * (n % 2) + half, 0:width(ib, g)], W["e_mix_scores"][:, P * half:P * (half + 1)],
                               FREG[:, g, 0:width(ib, g)], start=True, stop=True).then_inc(e_m1, 1)

                    mix(GROUPS * ib)
                    for g in range(GROUPS):
                        n = GROUPS * ib + g
                        if g + 1 < GROUPS:
                            mix(n + 1)
                        pe.wait_ge(e_gelu, n + 1)
                        if n >= 2:
                            pe.wait_ge(e_fin, n - 1)
                        for half in range(2):
                            ins = mm(PS[:, 6 + n % 2, 0:width(ib, g)], W["e_mix_back"][:, P * half:P * (half + 1)],
                                     e_hidden[:, n % 2, half, 0:width(ib, g)], start=half == 0, stop=half == 1)
                        ins.then_inc(e_m2, 1)
                    first = 4 * sum(range(1, ib + 1))
                    pe.wait_ge(e_zero, 3 * (ib + 1))
                    for k in range(4 * (ib + 1)):
                        gq, jb = k // (ib + 1), k % (ib + 1)
                        pe.wait_ge(e_div, 4 * ib + gq + 1)
                        if k >= 4:
                            pe.wait_ge(e_ptc, first + k - 3)
                        for g4 in range(4):
                            ins = nc.tensor.transpose(PS[:, 2 + k % 4, P * g4:P * (g4 + 1)],
                                                      FREG[:, 4 * gq + g4, P * jb:P * (jb + 1)], ident)
                        ins.then_inc(e_tp, 1)
                    pe.wait_ge(e_ptc, first + 4 * (ib + 1))
                    for c in range(8):
                        for a in range(2):
                            o = PS[64 * a:64 * a + E_HD, 4 + c // 4, P * (c % 4):P * (c % 4 + 1)]
                            for jb in range(ib + 1):
                                ins = mm(o, V[:, jb, 2 * c + a, :], PT[:, jb, :, 2 * c + a], start=jb == 0, stop=jb == ib)
                        if c % 4 == 3:
                            ins.then_inc(e_pv, 1)
                    if ib + 1 < TT:
                        scores(ib + 1)
                    for c in range(8):
                        pe.wait_ge(e_ots, 2 * ib + c // 4 + 1)
                        ins = mm(PS[:, 7, 0:D], e_oT[:, P * c:P * (c + 1)], W["e_out"][:, D * c:D * (c + 1)],
                                 start=c == 0, stop=c == 7)
                    ins.then_inc(e_y, 1)

            with pe.Fori(0, B) as b:
                linear_attention()
                if last >= 2:
                    mixture(0, 2)
                if last >= 3:
                    causal_attention()
                if last >= 4:
                    mixture(1, 4)
                if last >= 5:
                    phase_memory()
                if last >= 6:
                    adapted_linear(6)
                if last >= 7:
                    mixed_attention()
                if last >= 8:
                    adapted_linear(8)
                pe.drain().then_inc(sequence_ended, 1)
                pe.wait_ge(sequence_go, b + 1)


def _pack(group, pieces):
    got = []
    for name, n in PARTS[group]:
        a = np.asarray(pieces[name])
        a = a.reshape(a.shape[0], -1)
        assert a.shape[1] == n, (name, a.shape)
        got.append(np.concatenate([a, np.zeros((P - a.shape[0], n), np.float32)]) if a.shape[0] < P else a)
    return np.ascontiguousarray(np.concatenate(got, axis=1), dtype=np.float32)


def _layout(i):
    g = {k: np.asarray(v) for k, v in i.items()}
    f4 = np.float32
    eye = np.eye(P, dtype=f4)
    col = np.arange(P)
    out = {}
    proj = g["L0_attn_a_proj"]
    feats = np.zeros((P, A_FEATS), f4)
    for h in range(A_HEADS):
        feats[A_HD * h:A_HD * (h + 1), A_F * h:A_F * (h + 1)] = proj[h]
    kv_mask = np.zeros((P, 4, P), f4)
    for c in range(4):
        kv_mask[:, c, :] = (4 * c + col[:, None] // A_F) == (col[None, :] // A_HD)
    rep = lambda v, n=P: np.broadcast_to(v.reshape(1, -1), (n, v.size))
    out["w_a"] = _pack("a", dict(
        a_qkv=g["L0_attn_a_w_qkv"].T, a_features=feats, a_out=g["L0_attn_a_w_out"].T, a_w1=g["L0_attn_a_w1"].T,
        a_w2=g["L0_attn_a_w2"].T.reshape(4, P, D).transpose(1, 0, 2), a_gamma=rep(g["L0_attn_a_gamma"]),
        a_beta=rep(g["L0_attn_a_beta"]), a_b1=g["L0_attn_a_b1"].reshape(4, P).T, identity=eye, a_kv_mask=kv_mask))
    spread = np.zeros((N_EXPERT, N_EXPERT * RANK), f4)
    for e in range(N_EXPERT):
        spread[e, RANK * e:RANK * (e + 1)] = 1
    out["w_f"] = _pack("f", dict(
        f_proto=g["L0_ffn_prototypes"].T, f_down=g["L0_ffn_B"].reshape(-1, D).T,
        f_up=g["L0_ffn_A"].transpose(0, 2, 1).reshape(4, P, D).transpose(1, 0, 2), f_bias=g["L0_ffn_bias"],
        f_temp=np.broadcast_to(g["L0_ffn_temp"].reshape(1, 1), (P, 1)), expert_no=rep(np.arange(N_EXPERT, dtype=f4)),
        f_spread=spread))
    def rope(hd, n):
        inv = (1.0 / np.float32(10000.0) ** (np.arange(0, hd, 2, dtype=f4) / f4(hd))).astype(f4)
        fr = np.arange(T, dtype=f4)[None, :] * inv[:, None]
        cos, sin = np.cos(fr), np.sin(fr)
        return (np.tile(np.concatenate([cos, cos]), (n, 1)).astype(f4), np.tile(np.concatenate([-sin, sin]), (n, 1)).astype(f4))

    def rot(hd, n):
        return (np.arange(n) // hd) * hd + (np.arange(n) % hd + hd // 2) % hd
    w, bias = g["L0_attn_b_qkv_w"], g["L0_attn_b_qkv_b"]
    o = B_HD * (2 * (col % 8) + col // 64) + col // 8 % 8
    r = rot(B_HD, D)[o]
    cos, sin = (t[o] for t in rope(B_HD, B_HEADS))
    out["w_b"] = _pack("b", dict(
        b_q=w[0:D][o].T, b_qrot=w[0:D][r].T, b_k=w[D:2 * D][o].T, b_krot=w[D:2 * D][r].T, b_v=w[2 * D:].T,
        b_bias=np.stack([bias[0:D][o], bias[0:D][r], bias[D:2 * D][o], bias[D:2 * D][r]], 1), b_out=g["L0_attn_b_proj_w"].T,
        b_cos=cos, b_sin=sin))
    W_in, ck = g["L1_attn_a_W_in"], g["L1_attn_a_conv_k"][:, 0, :]
    key_of = col // C_H
    theta = np.zeros((P, C_CHUNKS, P), f4)
    c_spread = np.zeros((P, C_CHUNKS, P), f4)
    c_gather = np.zeros((P, C_CHUNKS, P), f4)
    k4, hh, m = col // (C_H * C_M), col // C_M % C_H, col % C_M
    for c in range(C_CHUNKS):
        row = (4 * c + k4) * C_H + hh
        theta[row, c, col] = g["L1_attn_a_theta"][0, 0, 4 * c + k4, hh, m]
        c_spread[row, c, col] = 1
        c_gather[col, c, row] = 1
    q = W_in[:, D + C_K:].reshape(D, C_KQ, C_H, C_M, 2)
    rep_q = lambda a: np.broadcast_to(a[:, :, None], (D, C_KQ, 4, C_H, C_M)).reshape(D, C_KQ * P)
    ns = g["L1_attn_a_norm_scale"]
    d_re, d_im = (g[f"L1_attn_a_W_{x}"][np.arange(C_H), np.arange(C_H)] for x in ("re", "im"))
    pos = np.arange(T, dtype=f4)
    steps = np.where((key_of < C_K - C_ANCHOR)[:, None], f4(T - 1) - pos[None], pos[None]).astype(f4)
    slopes = np.concatenate([g["L1_attn_a_decay_slopes"], g["L1_attn_a_anchor_slopes"]])[key_of]
    eh = col % E_HEADS
    out["w_c"] = _pack("c", dict(
        c_key=W_in[:, 0:D], c_decay=W_in[:, D + key_of], c_taps_key=ck[:, 0:D].T, c_taps_decay=ck[:, D + key_of].T,
        c_score_scale=g["L1_attn_a_score_scale"][key_of][:, None],
        softplus_in=np.stack([slopes, g["L1_attn_b_log_p"].reshape(-1)[eh], g["L1_attn_b_log_a"].reshape(-1)[eh]], 1),
        c_theta=theta, c_qre=rep_q(q[..., 0]), c_qim=rep_q(q[..., 1]),
        c_out=g["L1_attn_a_W_out"], c_steps=steps, c_spread=c_spread, c_gather=c_gather))
    out["w_d"] = _pack("d", dict(
        causal_masks=np.concatenate([np.where(col[None, :] <= col[:, None], 0, MASKED),
                                     np.where(col[:, None] <= col[None, :], 0, MASKED)], 1),
        c_norm=np.concatenate([rep(ns[hh]), rep(ns[C_H + hh])], 1), c_diag=np.concatenate([rep(d_re[hh]), rep(d_im[hh])], 1),
        d_w=g["L1_ffn_W"].T, d_lora_down=g["L1_ffn_lora_down"].T, d_down_aux=g["L1_ffn_down_aux"],
        d_lora_up=g["L1_ffn_lora_up"].T, d_up_aux=g["L1_ffn_up_aux"].T))
    w1, w2 = g["L1_attn_b_w1"], g["L1_attn_b_w2"]
    s1, k1, s2 = (np.zeros((P, 2, P), f4) for _ in range(3))
    for i in range(QROWS):
        half, i4 = i // 4, i % 4
        rows_, cols_ = slice(E_HEADS * i, E_HEADS * (i + 1)), slice(E_CH * i4, E_CH * (i4 + 1))
        s1[rows_, half, cols_] = w1[0:E_HEADS]
        k1[rows_, half, cols_] = w1[E_HEADS:]
        s2[cols_, half, rows_] = w2
    dist = (col // E_HEADS)[:, None] + (T - 1) - np.arange(TABLE)[None, :]
    cos, sin = rope(E_HD, 2)
    out["w_e"] = _pack("e", dict(
        e_out=g["L1_attn_b_w_o"].reshape(8, P, D).transpose(1, 0, 2), e_mix_scores=s1, e_mix_kerple=k1, e_mix_back=s2,
        e_b1=g["L1_attn_b_b1"][col % E_CH][:, None], e_b2=g["L1_attn_b_b2"][eh][:, None], e_cos=cos, e_sin=sin,
        e_dist=np.abs(dist).astype(f4), e_mask=np.where(dist >= 0, 0, MASKED).astype(f4)))
    wq = g["L1_attn_b_w_qkv"].reshape(P, 3, E_HEADS * E_HD)
    r = rot(E_HD, E_HEADS * E_HD)
    out["w_proj"] = np.ascontiguousarray(np.concatenate([wq[:, 0], wq[:, 0][:, r], wq[:, 1], wq[:, 1][:, r], wq[:, 2]], 1))
    rows = dict(ones=np.ones(P, f4), a_bo=g["L0_attn_a_b_out"], a_b2=g["L0_attn_a_b2"], b_bv=bias[2 * D:],
                b_bo=g["L0_attn_b_proj_b"], d_b=g["L1_ffn_b"])
    out["rows"] = np.ascontiguousarray(np.concatenate([rows[n] for n, _ in ROWS]).reshape(1, -1))
    return out


ORDER = ["w_a", "w_f", "w_b", "w_c", "w_d", "w_e", "w_proj", "rows"]
LAST = 8


def kernel(**inputs):
    import concourse.bacc as bacc
    from concourse.bass_utils import run_bass_kernel_spmd

    x = np.ascontiguousarray(inputs["L0_attn_a_x"])
    arrays = {"x": x, **_layout(inputs)}
    nc = bacc.Bacc("TRN2", target_bir_lowering=False, num_devices=1)
    args = [nc.dram_tensor(n + "_dram", arrays[n].shape, mybir.dt.from_np(arrays[n].dtype), kind="ExternalInput").ap()
            for n in ["x"] + ORDER]
    out = nc.dram_tensor("out_dram", x.shape, F32, kind="ExternalOutput").ap()
    build(nc, *args, out, last=LAST)
    got = run_bass_kernel_spmd(nc, [{n + "_dram": a for n, a in arrays.items()}], core_ids=[0])
    return got.results[0]["out_dram"]
```

```python
from contextlib import ExitStack

import numpy as np
import concourse.bass as bass
from concourse import mybir

F32 = mybir.dt.float32
BF16 = mybir.dt.bfloat16
U32 = mybir.dt.uint32
ALU = mybir.AluOpType
ACT = mybir.ActivationFunctionType
AX = mybir.AxisListType

P = 128
D = 128
T = 512
TT = T // P
EPS_LN = 1e-5
A_HEADS, A_F = 16, 32
A_HD = D // A_HEADS
A_FEATS = A_HEADS * A_F
A_HIDDEN = 4 * D
EPS_ATTN = 1e-8
N_EXPERT, RANK = 32, 16
B_HEADS = 16
B_HD = D // B_HEADS
QUARTER = P // 4
B_SCALE = float(1.0 / np.sqrt(B_HD))
C_K, C_KQ, C_ANCHOR, C_M, C_TAPS = 32, 4, 4, 8, 4
C_H = D // C_K
C_CHUNKS = C_K * C_H * C_M // P
MAGIC = 1.5 * 2.0 ** 23
TWO_PI = 6.283185
HALF_PI = 1.5707963
E_HEADS, E_HD = 16, 64
E_CH = 2 * E_HEADS
QROWS = P // E_HEADS
STEP = 32
TABLE = T + STEP
GROUPS = P // QROWS
E_SCALE = 1.0 / 8.0
MASKED = -1e30
TWO_BF16_ONES = float(np.array([0x3F803F80], np.uint32).view(np.float32)[0])

PARTS = {
    "a": [("a_qkv", 3 * D), ("a_features", A_FEATS), ("a_out", D), ("a_w1", A_HIDDEN), ("a_w2", A_HIDDEN),
          ("a_gamma", D), ("a_beta", D), ("a_b1", 4), ("identity", P), ("a_kv_mask", 4 * P)],
    "f": [("f_proto", N_EXPERT), ("f_down", N_EXPERT * RANK), ("f_up", 4 * D), ("f_bias", D), ("f_temp", 1),
          ("expert_no", N_EXPERT), ("f_spread", N_EXPERT * RANK)],
    "b": [("b_q", D), ("b_qrot", D), ("b_k", D), ("b_krot", D), ("b_v", D), ("b_bias", 4), ("b_out", D),
          ("b_cos", T), ("b_sin", T)],
    "c": [("c_key", D), ("c_decay", D), ("c_taps_key", C_TAPS), ("c_taps_decay", C_TAPS), ("c_score_scale", 1),
          ("softplus_in", 3), ("c_theta", C_CHUNKS * P), ("c_qre", C_KQ * P), ("c_qim", C_KQ * P),
          ("c_out", D),
          ("c_steps", T), ("c_spread", C_CHUNKS * P), ("c_gather", C_CHUNKS * P)],
    "d": [("causal_masks", 2 * P), ("c_norm", 2 * P), ("c_diag", 2 * P), ("d_w", D), ("d_lora_down", 4), ("d_down_aux", D), ("d_lora_up", 50), ("d_up_aux", D)],
    "e": [("e_out", 8 * D), ("e_mix_scores", 2 * P), ("e_mix_kerple", 2 * P), ("e_mix_back", 2 * P),
          ("e_b1", 1), ("e_b2", 1), ("e_cos", T), ("e_sin", T), ("e_dist", TABLE), ("e_mask", TABLE)],
}
WIDTH = {g: sum(n for _, n in parts) for g, parts in PARTS.items()}
ROWS = [("ones", P), ("a_bo", D), ("a_b2", D), ("b_bv", D), ("b_bo", D), ("d_b", D)]
ROW_WIDTH = sum(n for _, n in ROWS)
SETUP_KERPLE, SETUP_DVE = 19, 24
E_PROJ = 5 * E_HEADS * E_HD


def build(nc, x, w_a, w_f, w_b, w_c, w_d, w_e, w_proj, rows, out, last=8):
    B = x.shape[0]
    weights_in = dict(a=w_a, f=w_f, b=w_b, c=w_c, d=w_d, e=w_e)
    ctx = ExitStack()
    with ctx:
        def sb(name, cols, dt=F32, parts=P):
            shape = [parts] + (list(cols) if type(cols) in (tuple, list) else [cols])
            return ctx.enter_context(nc.sbuf_tensor(name, shape, dt))

        def sem(name):
            return ctx.enter_context(nc.semaphore(name))

        W, weight_tiles = {}, {}
        ARENA = 4096 * 2 + 8192
        arena = sb("arena", ARENA)
        for g, parts in PARTS.items():
            tile = weight_tiles[g] = arena[:, ARENA - WIDTH[g]:] if g == "d" else sb(f"weights_{g}", WIDTH[g])
            at = 0
            for name, n in parts:
                W[name] = tile[:, at:at + n]
                at += n
        row_tile = sb("rows", ROW_WIDTH, parts=1)
        R, at = {}, 0
        for name, n in ROWS:
            R[name] = row_tile[0:1, at:at + n]
            at += n
        ident = W["identity"]
        mask_tile = sb("masks_and_identity_bf16", 3 * P, BF16)
        causal_mask, causal_mask_T, ident_bf = (mask_tile[:, P * j:P * (j + 1)] for j in range(3))

        f_proto2 = sb("f_proto_squared", N_EXPERT)
        f_p2 = sb("f_proto_norm2", N_EXPERT)
        f_negtinv = sb("f_minus_inverse_temperature", 1)
        small = sb("prologue_small", 16)
        c_logdecay = W["c_steps"]
        d_weight = sb("d_weight", D)
        e_kerple = W["e_dist"]
        e_bias_table = W["e_mask"]
        e_hidden_table = sb("e_hidden_table", (2, TABLE))
        const = sb("constants", 8)
        half_pi, one_col, neg_half = const[:, 0:1], const[:, 1:2], const[:, 2:6]

        X = sb("x", (TT, D))
        XN = sb("x_normed", (TT, D))
        XT = sb("x_normed_feature", T)
        stats = sb("bn_stats", (TT, 6))
        mv = sb("mean_var", (TT, 2))
        varp = sb("var_plus_eps", TT)
        rstd = sb("rstd", TT)
        v_aug = sb("a_values_and_one", (TT, D + 1))
        V = sb("e_values", (TT, E_HEADS, E_HD))
        tmp = sb("tmp", (4, T))
        mx = sb("row_max", 16)
        negmx = sb("minus_row_max", 16)
        FREG = sb("mixed_scores", (GROUPS, T))
        proj = FREG[:, :, :].rearrange("p g j -> p (g j)")[:, 0:E_PROJ]

        def carve():
            at = [0]

            def take(*shape):
                n = int(np.prod(shape))
                v = arena[:, at[0]:at[0] + n]
                at[0] += n
                assert at[0] <= ARENA
                if len(shape) == 2:
                    v = v.rearrange("p (a b) -> p a b", a=shape[0])
                if len(shape) == 3:
                    v = v.rearrange("p (a b c) -> p a b c", a=shape[0], b=shape[1])
                return v
            return take
        x_in = V[:, :, :, :].rearrange("p t h d -> p (t h d)")[:, 0:TT * D].rearrange("p (t d) -> p t d", t=TT)
        t = carve()
        a_qT, a_kT, a_qf, a_kf = t(T), t(T), t(4, T), t(TT, A_FEATS)
        a_kvz = t(4, D + A_HEADS)
        a_token, a_z, a_attn = t(TT, D), t(TT, A_HEADS), t(T)
        a_r, a_hT, a_y = t(TT, D), t(4, T), t(TT, D)
        t = carve()
        f_xx, f_d, f_top, f_idx, f_idxf = t(TT), t(TT, N_EXPERT), t(TT, 8), t(TT, 8), t(TT, 8)
        f_w, f_gate, f_gateT, f_h, f_sq = t(8, TT), t(2 * TT, N_EXPERT), t(T), t(4, T), t(TT, D)
        f_near = t(TT, 2)
        t = carve()
        b_q, b_k, b_rest = t(T), t(T), t(T)
        b_parts = t(2 * 3, T // 2).bitcast(BF16)
        b_qs = FREG[:, :, :].rearrange("p g j -> p (g j)")[:, E_PROJ:E_PROJ + 8 * T // 2].rearrange("p (b t) -> p b t", b=8).bitcast(BF16)
        b_ks_flat = V[:, :, :, :].rearrange("p t h d -> p (t h d)")
        b_ks = b_ks_flat.rearrange("p (n t) -> p n t", n=16).bitcast(BF16)
        b_pT, b_rs, b_o, b_oT = t(8, T), t(16), t(TT, D), t(T)
        b_val = t(TT * B_HEADS, QUARTER).rearrange("p (t h) d -> p t h d", t=TT)
        b_of = t(T)
        b_negmax, b_maxrest = t(16), t(16)
        b_maxparts, b_maxT = t(24).bitcast(BF16), t(2, P // 2).bitcast(BF16)
        t = carve()
        c_z, c_conv, c_pw, c_inv, c_y = t(2, T + 4), t(2, T), t(T), t(T), t(T)
        c_rr, c_ff, c_re, c_im, c_pr, c_pi = t(2, T), t(2, T), t(2, T), t(2, T), t(2, T), t(2, T)
        c_nr, c_ni = t(2, T), t(2, T)
        c_qr, c_qi = t(2, T), t(2, T)
        t = carve()
        QT, KT, S = t(8, T), t(8, T), t(E_HEADS, T)
        REGIONS = [v.rearrange("p a b -> p (a b)") for v in (S, FREG)]
        e_hidden = sb("e_hidden", (2, 2, T))
        e_oT = tmp[:, 0:2, :].rearrange("p a b -> p (a b)")
        e_sum, e_rs = sb("e_row_sum", 16), sb("e_row_sum_inverse", 16)

        PS = ctx.enter_context(nc.psum_tensor("banks", [P, 8, 512], F32))

        rows_loaded = sem("rows_loaded")
        w_loaded = {g: sem(f"w_{g}_loaded") for g in PARTS}
        sequence_go = sem("sequence_go")
        x_loaded = sem("x_loaded")
        b_spread_pool = sem("b_spread_pool")
        out_stored = sem("out_stored")
        setup_act = sem("setup_act")
        setup_dve = sem("setup_dve")
        setup_pe = sem("setup_pe")
        setup_pool = sem("setup_pool")

        cleared = []

        def seq_sem(name):
            cleared.append(sem(name))
            return cleared[-1]
        sequence_ended = seq_sem("sequence_ended")
        dve_step = seq_sem("dve_step")
        act_step = seq_sem("act_step")
        pool_step = seq_sem("pool_step")
        ln_var = seq_sem("ln_var")
        ln_rstd = seq_sem("ln_rstd")
        tr_in = seq_sem("tr_in")
        tr_psum = seq_sem("tr_psum")
        xT_ready = seq_sem("xT_ready")
        y_psum = seq_sem("y_psum")
        x_shifted = seq_sem("x_shifted")
        x_done = seq_sem("x_done")
        a_proj, a_qk, a_v = seq_sem("a_proj"), seq_sem("a_qk"), seq_sem("a_v")
        a_fpre, a_neg, a_exp, a_feat = seq_sem("a_fpre"), seq_sem("a_neg"), seq_sem("a_exp"), seq_sem("a_feat")
        a_kv, a_masked, a_att, a_attn_ready = seq_sem("a_kv"), seq_sem("a_masked"), seq_sem("a_att"), seq_sem("a_attn")
        a_normed, a_attn_T = seq_sem("a_normed"), seq_sem("a_attn_T")
        a_h, a_gelu = seq_sem("a_h"), seq_sem("a_gelu")
        f_xp, f_xxd, f_d2, f_dist = seq_sem("f_xp"), seq_sem("f_xxd"), seq_sem("f_d2"), seq_sem("f_dist")
        f_spread_up = seq_sem("f_spread_up")
        f_diff, f_e2, f_gated = seq_sem("f_diff"), seq_sem("f_e2"), seq_sem("f_gated")
        f_gT, f_gTs, f_hp, f_hs, f_gh = seq_sem("f_gT"), seq_sem("f_gTs"), seq_sem("f_hp"), seq_sem("f_hs"), seq_sem("f_gh")
        b_proj, b_vs = seq_sem("b_proj"), seq_sem("b_vs")
        b_split, b_ones, b_mparts, b_mT, b_mTs = (seq_sem(n) for n in ("b_split", "b_ones", "b_mparts", "b_mT", "b_mTs"))
        b_mrows = [seq_sem("b_mrows0"), seq_sem("b_mrows1")]
        b_st = seq_sem("b_st")
        b_spread_even, b_spread_odd = seq_sem("b_spread_even"), seq_sem("b_spread_odd")
        b_sc, b_max, b_exp = seq_sem("b_sc"), seq_sem("b_max"), seq_sem("b_exp")
        b_of_ready, b_oq = seq_sem("b_of_ready"), seq_sem("b_oq")
        b_pv, b_od, b_ot, b_ots = seq_sem("b_pv"), seq_sem("b_od"), seq_sem("b_ot"), seq_sem("b_ots")
        c_zp, c_zs, c_cv, c_lp, c_pws = seq_sem("c_zp"), seq_sem("c_zs"), seq_sem("c_cv"), seq_sem("c_lp"), seq_sem("c_pws")
        c_up, c_mag, c_frac, c_trig = seq_sem("c_up"), seq_sem("c_mag"), seq_sem("c_frac"), seq_sem("c_trig")
        c_pwx, c_ab, c_prod, c_sum = seq_sem("c_pwx"), seq_sem("c_ab"), seq_sem("c_prod"), seq_sem("c_sum")
        c_query, c_weighted = seq_sem("c_query"), seq_sem("c_weighted")
        c_qs, c_scan = seq_sem("c_qs"), seq_sem("c_scan")
        c_norm, c_silu = seq_sem("c_norm"), seq_sem("c_silu")
        e_w, e_qk, e_rope, e_add = seq_sem("e_w"), seq_sem("e_qk"), seq_sem("e_rope"), seq_sem("e_add")
        e_vp, e_vs, e_sc, e_evac = seq_sem("e_vp"), seq_sem("e_vs"), seq_sem("e_sc"), seq_sem("e_evac")
        e_dma = [seq_sem(f"e_dma{q}") for q in range(4)]
        e_zero = seq_sem("e_zero")
        e_m1, e_hadd, e_gelu, e_m2 = seq_sem("e_m1"), seq_sem("e_hadd"), seq_sem("e_gelu"), seq_sem("e_m2")
        e_fk, e_fin, e_nmx, e_exp = seq_sem("e_fk"), seq_sem("e_fin"), seq_sem("e_nmx"), seq_sem("e_exp")
        e_ptc_act = seq_sem("e_ptc_act")
        e_tp, e_ptc, e_pv, e_div = seq_sem("e_tp"), seq_sem("e_ptc"), seq_sem("e_pv"), seq_sem("e_div")
        e_ots, e_y, e_x = seq_sem("e_ots"), seq_sem("e_y"), seq_sem("e_x")

        front_done = seq_sem("front_done")
        cleared_early = [s for s in cleared if s.name[:2] in ("a_", "f_", "b_", "c_")]

        def y_tile(tt):
            return PS[:, 6 - 2 * (tt // 2), D * (tt % 2):D * (tt % 2 + 1)]

        def y_half(half):
            return PS[:, 6 - 2 * half, 0:2 * D].rearrange("p (t d) -> p t d", t=2)

        def width(ib, g):
            return P * ib + STEP * (g // 4 + 1)

        def table_at(ib, g):
            return T - 1 - (P * ib + QROWS * g)

        def score_bank(h):
            return (6, 7, 0, 1)[h % 4]

        def dve_copies(ib):
            return 2 * (ib + 1) + (ib + 2) // 2

        def raw_scores(ib):
            return REGIONS[ib % 2].rearrange("p (h j) -> p h j", h=E_HEADS)

        def probs_T(ib):
            return REGIONS[ib % 2].rearrange("p (jb i h) -> p jb i h", jb=TT, h=E_HEADS)

        def mixed(ib, g, lo, hi):
            at = T * (4 * (3 - g // 4) + g % 4)
            return REGIONS[(ib + 1) % 2][:, at + lo:at + hi]

        Q_PARTS, K_PARTS = (0, 0, 1, 0, 2, 1), (0, 1, 0, 2, 0, 1)
        B_ROWS = len(Q_PARTS) * B_HD
        SPREAD = [(which, part, prod) for which, parts in enumerate((Q_PARTS, K_PARTS))
                  for part in range(3) for prod in range(6) if parts[prod] == part]

        MAX_AHEAD = 28
        POOL_SPREADS = 10

        def spread(eng, a, which, part, prod):
            at = 64 * a + B_HD * prod
            dst = (b_qs, b_ks[:, 8 * a:8 * a + 8, :])[which]
            return eng.dma_start(dst[at:at + B_HD, :, :], b_parts[64 * a:64 * a + 64, 3 * which + part, :])


        block = ctx.enter_context(nc.Block())


        @block.sync
        def _(sp):
            def load_x(b):
                sp.dma_start(x_in, x[bass.ds(b, 1)].rearrange("o (t p) d -> p (o t) d", p=P)).then_inc(x_loaded, 16)

            def sequence(b, load_next):
                sp.dma_start(proj, w_proj[:, :]).then_inc(e_w, 16)
                if last >= 3:
                    sp.wait_ge(b_ones, 1)
                    for which, part, prod in SPREAD:
                        sp.wait_ge(b_split, 3 * which + part + 1)
                        spread(sp, 0, which, part, prod).then_inc(b_spread_even, 16)
                    for which, part, prod in SPREAD[POOL_SPREADS:]:
                        spread(sp, 1, which, part, prod).then_inc(b_spread_odd, 16)
                    for ib in range(TT):
                        sp.wait_ge(b_mTs, ib + 1)
                        for a in range(2):
                            at = 64 * a + B_ROWS
                            sp.dma_start(b_qs[at:at + 3, :, P * ib:P * (ib + 1)],
                                         b_maxT[24 * a:24 * a + 24, ib % 2, :]).then_inc(b_mrows[ib % 2], 16)
                if last >= 7:
                    for ib in range(TT):
                        sp.wait_ge(e_evac, 16 * (ib + 1))
                        for g in range(GROUPS):
                            if g == 4 and ib == 0:
                                sp.wait_ge(e_vp, 8)
                            if g == 4 and ib:
                                sp.wait_ge(e_pv, 2 * ib)
                            n = width(ib, g)
                            sp.dma_start(mixed(ib, g, 0, n),
                                         raw_scores(ib)[QROWS * g:QROWS * (g + 1), :, 0:n]).then_inc(e_dma[g // 4], 16)
                if last >= 7:
                    sp.wait_ge(front_done, 4)
                    for s in cleared_early:
                        sp.sem_clear(s)
                    sp.wait_ge(e_pv, 2 * TT)
                    sp.wait_ge(e_w, 16)
                else:
                    sp.wait_ge(x_done, 1)
                if load_next:
                    load_x(b + 1)
                sp.wait_ge(x_done, 1)
                sp.dma_start(out[bass.ds(b, 1)].rearrange("o (t p) d -> p (o t) d", p=P), X[:, :, :]).then_inc(out_stored, 16)
                if last < 7:
                    sp.wait_ge(e_w, 16)
                sp.wait_ge(sequence_ended, 4)
                for s in cleared:
                    if last < 7 or s not in cleared_early:
                        sp.sem_clear(s)
                sp.sem_inc(sequence_go, 1)

            sp.sem_inc(out_stored, 1)
            load_x(0)
            sp.dma_start(row_tile[:, :], rows[:, :]).then_inc(rows_loaded, 16)
            for g in PARTS:
                sp.dma_start(weight_tiles[g][:, :], weights_in[g][:, :]).then_inc(w_loaded[g], 16)
            if B > 1:
                with sp.Fori(0, B - 1) as b:
                    sequence(b, True)
            sequence(B - 1, False)
            sp.wait_ge(out_stored, 16 * B + 1)

        @block.gpsimd
        def _(pool):
            def settle(ins):
                pool_count[0] += 1
                ins.then_inc(pool_step, 1)
                pool.wait_ge(pool_step, pool_count[0])

            pool_count = [0]
            nc.gpsimd.memset(half_pi, HALF_PI).then_inc(setup_pool, 1)
            nc.gpsimd.memset(one_col, 1.0).then_inc(setup_pool, 1)
            nc.gpsimd.memset(neg_half, -0.5).then_inc(setup_pool, 1)
            nc.gpsimd.memset(const[:, 6:7], 0.5).then_inc(setup_pool, 1)
            nc.gpsimd.memset(v_aug[:, :, D:D + 1], 1.0).then_inc(setup_pool, 1)
            pool.wait_ge(setup_pool, 5)

            def ln(k):
                pool.wait_ge(ln_var, k + 1)
                nc.gpsimd.tensor_tensor(rstd[:, :], varp[:, :], neg_half, ALU.pow).then_inc(ln_rstd, 1)

            def mixture(k, ln_no):
                ln(ln_no)
                pool.wait_ge(f_d2, k + 1)
                d = f_near.rearrange("p t e -> p (t e)")
                nc.gpsimd.tensor_tensor(d, d, const[:, 6:7].to_broadcast([P, TT * 2]), ALU.pow).then_inc(f_dist, 1)

            with pool.Fori(0, B) as b:
                pool_count[0] = 0
                for k in range(3):
                    ln(k)
                if last >= 2:
                    mixture(0, 3)
                pool.wait_ge(x_shifted, 1)
                settle(nc.gpsimd.memset(b_qs.rearrange("p b t -> p (b t)").bitcast(F32), 0.0))
                settle(nc.gpsimd.memset(b_ks_flat, 0.0))
                settle(nc.gpsimd.memset(b_ks_flat[32:64, 0:8 * T // 2], TWO_BF16_ONES))
                nc.gpsimd.memset(b_ks_flat[96:128, 8 * T // 2:], TWO_BF16_ONES).then_inc(b_ones, 1)
                pool.wait_ge(b_ones, 1)
                if last >= 3:
                    ln(4)
                    pool.wait_ge(tr_in, 4 * TT)
                    nc.gpsimd.memset(b_val[:, :, :, B_HD + 1:], 0.0)
                    nc.gpsimd.memset(b_val[:, :, :, B_HD:B_HD + 1], 1.0).then_inc(b_ones, 1)
                    for which, part, prod in SPREAD[:POOL_SPREADS]:
                        pool.wait_ge(b_split, 3 * which + part + 1)
                        spread(pool, 1, which, part, prod).then_inc(b_spread_pool, 16)
                if last >= 4:
                    mixture(1, 5)
                if last >= 5:
                    ln(6)
                    for c in range(C_CHUNKS):
                        i, kq = c % 2, c // 2 % 2
                        pool.wait_ge(c_scan, 2 * c + 1)
                        pool.wait_ge(c_qs, 2 * (c // 2) + 1)
                        nc.gpsimd.tensor_tensor(c_pr[:, i, :], c_qr[:, kq, :], c_nr[:, i, :], ALU.mult).then_inc(c_weighted, 1)
                        pool.wait_ge(c_scan, 2 * c + 2)
                        pool.wait_ge(c_qs, 2 * (c // 2) + 2)
                        nc.gpsimd.tensor_tensor(c_pi[:, i, :], c_qi[:, kq, :], c_ni[:, i, :], ALU.mult).then_inc(c_weighted, 1)
                if last >= 6:
                    ln(7)
                if last >= 7:
                    pool.drain().then_inc(front_done, 1)
                    ln(8)
                    for n in range(16):
                        pool.wait_ge(e_rope, n + 1)
                        dst = QT if n % 2 == 0 else KT
                        pair = tmp[:, 2 * (n % 2):2 * (n % 2) + 2, :]
                        nc.gpsimd.tensor_tensor(dst[:, n // 2, :], pair[:, 0, :], pair[:, 1, :], ALU.add).then_inc(e_add, 1)
                    for ib in range(TT):
                        for g in range(GROUPS):
                            n = GROUPS * ib + g
                            w = width(ib, g)
                            if g % 4 == 0 and g < 12:
                                if g == 0 and ib:
                                    pool.wait_ge(e_dma[3], 64 * ib)
                                if g == 4 and ib == 0:
                                    pool.wait_ge(e_vp, 8)
                                if g == 4 and ib:
                                    pool.wait_ge(e_pv, 2 * ib)
                                for g4 in range(g, g + 4):
                                    ins = nc.gpsimd.memset(mixed(ib, g4, w, P * (ib + 1)), 0.0)
                                ins.then_inc(e_zero, 1)
                            pool.wait_ge(e_m1, n + 1)
                            f = mixed(ib, g, 0, w)
                            nc.gpsimd.tensor_tensor(f, f, e_bias_table[:, table_at(ib, g):table_at(ib, g) + w],
                                                    ALU.add).then_inc(e_fk, 1)
                if last >= 8:
                    ln(9)
                pool.drain().then_inc(sequence_ended, 1)
                pool.wait_ge(sequence_go, b + 1)

        @block.scalar
        def _(act):
            A = nc.scalar.activation
            act_count = [0]

            def settle(ins):
                act_count[0] += 1
                ins.then_inc(act_step, 1)
                act.wait_ge(act_step, act_count[0])

            act.wait_ge(setup_pool, 5)
            act.wait_ge(w_loaded["c"], 16)
            sp_in = W["softplus_in"]
            A(small[:, 0:3], sp_in, ACT.Abs).then_inc(setup_act, 1)
            act.wait_ge(setup_act, 1)
            A(small[:, 3:6], small[:, 0:3], ACT.Exp, scale=-1.0).then_inc(setup_act, 1)
            act.wait_ge(setup_act, 2)
            A(small[:, 6:9], small[:, 3:6], ACT.Ln, bias=one_col).then_inc(setup_act, 1)
            act.wait_ge(w_loaded["e"], 16)
            act.wait_ge(setup_dve, 1)
            A(e_kerple, e_kerple, ACT.Ln, scale=small[:, 11:12], bias=one_col).then_inc(setup_act, 1)
            act.wait_ge(setup_pe, 1)
            A(f_p2[:, :], PS[:, 0, 0:N_EXPERT], ACT.Copy).then_inc(setup_act, 1)
            act.wait_ge(setup_pe, 2)
            A(tmp[0:4, 0, 0:P], PS[0:4, 1, 0:P], ACT.Copy).then_inc(setup_act, 1)
            act.wait_ge(setup_pe, 3)
            A(tmp[0:50, 1, 0:P], PS[0:50, 2, 0:P], ACT.Copy).then_inc(setup_act, 1)

            def feature_layout(k):
                for half in range(2):
                    cols = slice(T // 2 * half, T // 2 * (half + 1))
                    act.wait_ge(tr_psum, TT * k + TT // 2 * (half + 1))
                    A(XT[:, cols], PS[:, 7 - 2 * half, cols], ACT.Copy).then_inc(xT_ready, 1)

            def linear_attention():
                feature_layout(0)
                act.wait_ge(a_proj, 1)
                A(a_qT, PS[:, 0, :], ACT.Copy).then_inc(a_qk, 1)
                act.wait_ge(a_proj, 2)
                A(a_kT, PS[:, 1, :], ACT.Copy).then_inc(a_qk, 1)
                for n in range(8):
                    act.wait_ge(a_neg, n + 1)
                    A(tmp[:, n % 2, :], tmp[:, n % 2, :], ACT.Exp).then_inc(a_exp, 1)
                for half in range(2):
                    act.wait_ge(a_attn_T, half + 1)
                    A(a_attn[:, 2 * P * half:2 * P * (half + 1)], PS[:, half, 0:2 * P], ACT.Copy).then_inc(a_attn_ready, 1)
                feature_layout(1)
                for c in range(4):
                    act.wait_ge(a_h, c + 1)
                    A(a_hT[:, c, :], PS[:, c, :], ACT.Gelu, bias=W["a_b1"][:, c:c + 1]).then_inc(a_gelu, 1)

            def mixture(k, tr):
                for tt in range(TT):
                    act.wait_ge(tr_in, TT * tr + tt + 1)
                    A(f_sq[:, tt, :], XN[:, tt, :], ACT.Square, accum_out=f_xx[:, tt:tt + 1]).then_inc(f_xxd, 1)
                feature_layout(tr)
                for c in range(4):
                    if c == 2:
                        act.wait_ge(f_diff, k + 1)
                        A(f_w[:, 1, :], f_w[:, 0, :], ACT.Exp, scale=f_negtinv[:, 0:1]).then_inc(f_e2, 1)
                    act.wait_ge(f_hp, 4 * k + c + 1)
                    A(f_h[:, c, :], PS[:, 2 + c, :], ACT.Copy).then_inc(f_hs, 1)
                act.wait_ge(f_gT, k + 1)
                A(f_gateT[0:N_EXPERT, :], PS[0:N_EXPERT, 1, :], ACT.Copy).then_inc(f_gTs, 1)

            def causal_attention():
                feature_layout(3)
                act.wait_ge(b_proj, 3)
                A(b_val[:, :, :, 0:B_HD], PS[:, 4, :].rearrange("p (t h d) -> p t h d", t=TT, h=B_HEADS),
                  ACT.Copy).then_inc(b_vs, 1)
                def maxima_rows(ib):
                    act.wait_ge(b_mT, ib + 1)
                    if ib >= 2:
                        act.wait_ge(b_mrows[ib % 2], 32)
                    A(b_maxT[0:48, ib % 2, :], PS[:, 3, :].bitcast(BF16)[0:48, 0:P], ACT.Copy).then_inc(b_mTs, 1)

                def outputs_to_sbuf(ib):
                    act.wait_ge(b_pv, 4 * (ib + 1))
                    if ib:
                        act.wait_ge(b_oq, ib)
                    A(b_of, PS[:, 6 + ib % 2, :], ACT.Copy).then_inc(b_of_ready, 1)

                maxima_rows(0)
                for n in range(64):
                    w = P * (n // 16 + 1)
                    if n % 16 == 7 and n // 16 + 1 < TT:
                        maxima_rows(n // 16 + 1)
                    if n % 16 == 3 and n > 16:
                        outputs_to_sbuf(n // 16 - 1)
                    act.wait_ge(b_st, n + 1)
                    if n >= 8 and n % 4 == 0:
                        act.wait_ge(b_pv, n // 4 - 1)
                    A(b_pT[:, n % 8, 0:w], PS[:, 4 + n % 2, 0:w], ACT.Exp, scale=B_SCALE).then_inc(b_exp, 1)
                outputs_to_sbuf(TT - 1)
                act.wait_ge(b_ot, 1)
                A(b_oT, PS[:, 4, :], ACT.Copy).then_inc(b_ots, 1)

            def phase_memory():
                feature_layout(5)
                for j in range(2):
                    act.wait_ge(c_zp, j + 1)
                    A(c_z[:, j, 0:3], const[:, 0:3], ACT.Copy, scale=0.0).then_inc(c_zs, 1)
                    A(c_z[:, j, 3:3 + T], PS[:, j, :], ACT.Copy).then_inc(c_zs, 1)
                act.wait_ge(c_lp, 1)
                A(c_pw, c_pw, ACT.Exp).then_inc(c_pws, 1)

                def rounded(c):
                    act.wait_ge(c_up, c + 1)
                    if c >= 2:
                        act.wait_ge(c_frac, c - 1)
                    A(c_rr[:, c % 2, :], PS[:, c % 2, :], ACT.Copy, bias=MAGIC).then_inc(c_mag, 1)

                rounded(0)
                for c in range(C_CHUNKS):
                    if c + 1 < C_CHUNKS:
                        rounded(c + 1)
                    act.wait_ge(c_frac, c + 1)
                    if c >= 2:
                        act.wait_ge(c_prod, 2 * (c - 1))
                    A(c_re[:, c % 2, :], c_ff[:, c % 2, :], ACT.Abs).then_inc(c_ab, 1)
                    A(c_im[:, c % 2, :], c_ff[:, c % 2, :], ACT.Sin, scale=-TWO_PI).then_inc(c_trig, 1)
                    act.wait_ge(c_ab, c + 1)
                    A(c_re[:, c % 2, :], c_re[:, c % 2, :], ACT.Sin, scale=-TWO_PI, bias=half_pi).then_inc(c_trig, 1)
                    if c % 2 == 0:
                        kq = c // 2
                        act.wait_ge(c_query, kq + 1)
                        if kq >= 2:
                            act.wait_ge(c_weighted, 4 * (kq - 1))
                        A(c_qr[:, kq % 2, :], PS[:, 4, :], ACT.Copy).then_inc(c_qs, 1)
                        A(c_qi[:, kq % 2, :], PS[:, 5, :], ACT.Copy).then_inc(c_qs, 1)
                act.wait_ge(c_norm, 1)
                A(c_y, c_y, ACT.Silu).then_inc(c_silu, 1)

            def mixed_attention():
                feature_layout(7)

                def values_to_sbuf(r):
                    act.wait_ge(e_vp, r + 1)
                    A(V[:, r // 2, 8 * (r % 2):8 * (r % 2) + 8, 0:E_HD],
                      PS[:, 4 + r % 2, :].rearrange("p (h d) -> p h d", h=8), ACT.Copy).then_inc(e_vs, 1)

                def raw_to_sbuf(ib):
                    for h in range(E_HEADS):
                        w = P * (ib + 1)
                        act.wait_ge(e_sc, 16 * ib + h + 1)
                        A(raw_scores(ib)[:, h, 0:w], PS[:, score_bank(h), 0:w], ACT.Copy, scale=E_SCALE).then_inc(e_evac, 1)

                for r in range(0, 2):
                    values_to_sbuf(r)
                raw_to_sbuf(0)
                for r in range(2, 8):
                    values_to_sbuf(r)
                for ib in range(TT):
                    for g in range(GROUPS):
                        n = GROUPS * ib + g
                        act.wait_ge(e_hadd, n + 1)
                        hid = e_hidden[:, n % 2, :, 0:width(ib, g)]
                        A(hid, hid, ACT.Gelu).then_inc(e_gelu, 1)
                    for g in range(GROUPS):
                        if g % 4 == 0:
                            act.wait_ge(e_nmx, 4 * ib + g // 4 + 1)
                        f = mixed(ib, g, 0, width(ib, g))
                        A(f, f, ACT.Exp, bias=negmx[:, g:g + 1], accum_out=e_sum[:, g:g + 1]).then_inc(e_exp, 1)
                    for k in range(dve_copies(ib), 4 * (ib + 1)):
                        gq, jb = k // (ib + 1), k % (ib + 1)
                        act.wait_ge(e_tp, 4 * sum(range(1, ib + 1)) + k + 1)
                        A(probs_T(ib)[:, jb, 32 * gq:32 * gq + 32, :].rearrange("p i h -> p (i h)"), PS[:, 2 + k % 4, :],
                          ACT.Copy).then_inc(e_ptc_act, 1)
                    if ib + 1 < TT:
                        raw_to_sbuf(ib + 1)
                    for j in range(2):
                        act.wait_ge(e_pv, 2 * ib + j + 1)
                        A(e_oT[:, 512 * j:512 * (j + 1)], PS[:, 4 + j, :], ACT.Copy).then_inc(e_ots, 1)

            with act.Fori(0, B) as b:
                act_count[0] = 0
                linear_attention()
                if last >= 2:
                    mixture(0, 2)
                if last >= 3:
                    causal_attention()
                if last >= 4:
                    mixture(1, 4)
                if last >= 5:
                    phase_memory()
                if last >= 6:
                    feature_layout(6)
                if last >= 7:
                    act.drain().then_inc(front_done, 1)
                    mixed_attention()
                if last >= 8:
                    feature_layout(8)
                act.drain().then_inc(sequence_ended, 1)
                act.wait_ge(sequence_go, b + 1)

        @block.vector
        def _(dve):
            V_ = nc.vector
            count = [0]

            def settle(ins):
                count[0] += 1
                ins.then_inc(dve_step, 1)
                dve.wait_ge(dve_step, count[0])

            done = [0]

            def setup(ins):
                done[0] += 1
                ins.then_inc(setup_dve, 1)
                dve.wait_ge(setup_dve, done[0])
            dve.wait_ge(w_loaded["c"], 16)
            dve.wait_ge(w_loaded["d"], 16)
            dve.wait_ge(w_loaded["e"], 16)
            dve.wait_ge(setup_act, 3)
            setup(V_.scalar_tensor_tensor(small[:, 9:12], W["softplus_in"], 0.0, small[:, 6:9], ALU.max, ALU.add))
            setup(V_.tensor_scalar(c_logdecay, c_logdecay, small[:, 9:10], -1.0, ALU.mult, ALU.mult))
            setup(V_.tensor_scalar(W["c_theta"], W["c_theta"], float(1.0 / (2.0 * np.pi)), None, ALU.mult))
            setup(V_.tensor_tensor(W["c_norm"], W["c_norm"], W["c_diag"], ALU.mult))
            c1, c2 = (W["c_norm"][:, j * P:(j + 1) * P].unsqueeze(1).to_broadcast([P, C_KQ, P]) for j in range(2))
            qre, qim = (W[n].rearrange("p (k n) -> p k n", k=C_KQ) for n in ("c_qre", "c_qim"))
            t1, t2, t3, t4 = (tmp[:, j, :].rearrange("p (k n) -> p k n", k=C_KQ) for j in range(4))
            for dst, q, c in ((t1, qre, c1), (t2, qim, c2), (t3, qim, c1), (t4, qre, c2)):
                setup(V_.tensor_tensor(dst, q, c, ALU.mult))
            setup(V_.tensor_tensor(qre, t1, t2, ALU.subtract))
            setup(V_.tensor_tensor(qim, t3, t4, ALU.add))
            dve.wait_ge(w_loaded["f"], 16)
            setup(V_.tensor_tensor(f_proto2[:, :], W["f_proto"], W["f_proto"], ALU.mult))
            setup(V_.tensor_scalar(small[:, 12:13], W["f_temp"], -1.0, None, ALU.mult))
            setup(V_.tensor_tensor(small[:, 12:13], small[:, 12:13], W["f_temp"], ALU.max))
            setup(V_.tensor_scalar(small[:, 12:13], small[:, 12:13], 0.1, -1.0, ALU.max, ALU.mult))
            setup(V_.reciprocal(f_negtinv[:, :], small[:, 12:13]))
            dve.wait_ge(setup_pe, 4)
            setup(V_.tensor_tensor(d_weight[:, :], PS[:, 3, 0:D], W["d_w"], ALU.add))
            dve.wait_ge(w_loaded["a"], 16)
            setup(V_.tensor_copy(mask_tile[:, 0:2 * P], W["causal_masks"]))
            setup(V_.tensor_copy(ident_bf, ident))
            dve.wait_ge(setup_act, 4)
            setup(V_.tensor_scalar(e_kerple, e_kerple, small[:, 10:11], -1.0, ALU.mult, ALU.mult))
            KERPLE_READY = done[0]
            setup(V_.scalar_tensor_tensor(e_bias_table, e_kerple, W["e_b2"], e_bias_table, ALU.add, ALU.add))
            for half in range(2):
                dve.wait_ge(setup_pe, 5 + half)
                setup(V_.tensor_scalar(e_hidden_table[:, half, 0:512], PS[:, 4 + half, :], W["e_b1"], None, ALU.add))
                setup(V_.tensor_scalar(e_hidden_table[:, half, 512:TABLE], PS[:, 6 + half, 0:STEP], W["e_b1"], None, ALU.add))
            assert KERPLE_READY == SETUP_KERPLE and done[0] == SETUP_DVE

            def ln_stats(k, src, have_stats=False):
                if not have_stats:
                    for tt in range(TT):
                        ins = V_.bn_stats(stats[:, tt, :], src[:, tt, :])
                    settle(ins)
                for tt in range(TT):
                    ins = V_.bn_aggr(mv[:, tt, :], stats[:, tt, :])
                settle(ins)
                V_.tensor_scalar(varp[:, :], mv[:, :, 1], EPS_LN, None, ALU.add).then_inc(ln_var, 1)

            def normalise(dst, src, done=None):
                for tt in range(TT):
                    ins = V_.tensor_scalar(dst[:, tt, :], src[:, tt, :], mv[:, tt, 0:1], rstd[:, tt:tt + 1],
                                           ALU.subtract, ALU.mult)
                    if done is not None:
                        ins.then_inc(done, 1)
                return ins

            def layer_norm(k, src=X, have_stats=True):
                ln_stats(k, src, have_stats)
                dve.wait_ge(ln_rstd, k + 1)
                normalise(XN, src, tr_in)

            def add_y(y_no, dst=X, src=X):
                for half in range(2):
                    tiles = slice(2 * half, 2 * half + 2)
                    dve.wait_ge(y_psum, 2 * (y_no - 1) + half + 1)
                    settle(V_.tensor_tensor(dst[:, tiles, :], y_half(half), src[:, tiles, :], ALU.add))
                    for tt in range(2 * half, 2 * half + 2):
                        ins = V_.bn_stats(stats[:, tt, :], dst[:, tt, :])
                settle(ins)

            def scaled_norm(k, dst, src, shift, done):
                for tt in range(TT):
                    ins = V_.scalar_tensor_tensor(src[:, tt, :], src[:, tt, :], mv[:, tt, 0:1], W["a_gamma"], ALU.subtract, ALU.mult)
                settle(ins)
                dve.wait_ge(ln_rstd, k + 1)
                for tt in range(TT):
                    V_.scalar_tensor_tensor(dst[:, tt, :], src[:, tt, :], rstd[:, tt:tt + 1], shift(tt), ALU.mult, ALU.add).then_inc(done, 1)

            def linear_attention(b):
                layer_norm(0, x_in, have_stats=False)
                dve.wait_ge(tr_in, TT)
                dve.wait_ge(a_proj, 3)
                V_.tensor_copy(v_aug[:, :, 0:D], PS[:, 2, :].rearrange("p (t d) -> p t d", t=TT)).then_inc(a_v, 1)
                feats = [a_qf[:, c, :] for c in range(4)] + [a_kf[:, c, :] for c in range(4)]
                for n in range(9):
                    if n < 8:
                        dve.wait_ge(a_fpre, n + 1)
                        if n >= 2:
                            dve.wait_ge(a_feat, n - 1)
                        V_.tensor_scalar(tmp[:, n % 2, :], PS[:, 3 + n % 3, :], 0.0, None, ALU.min).then_inc(a_neg, 1)
                    if n >= 1:
                        m = n - 1
                        dve.wait_ge(a_exp, m + 1)
                        V_.scalar_tensor_tensor(feats[m], PS[:, 3 + m % 3, :], 0.0, tmp[:, m % 2, :],
                                                ALU.max, ALU.add).then_inc(a_feat, 1)
                mask = W["a_kv_mask"].rearrange("p (c n) -> p c n", c=4)
                for c in range(4):
                    dve.wait_ge(a_kv, 2 * (c // 2) + 2)
                    at = (c % 2) * (D + 1)
                    V_.tensor_tensor(a_kvz[:, c, 0:D], PS[:, c // 2, at:at + D], mask[:, c, :], ALU.mult).then_inc(a_masked, 1)
                    V_.tensor_scalar(a_kvz[:, c, D:], mask[:, c, 0:D:A_HD], PS[:, c // 2, at + D:at + D + 1], None, ALU.mult).then_inc(a_masked, 1)
                for half in range(2):
                    tiles = slice(2 * half, 2 * half + 2)
                    dve.wait_ge(a_att, half + 1)
                    at = PS[:, 2 + half, 0:2 * (D + A_HEADS)].rearrange("p (t n) -> p t n", t=2)
                    settle(V_.tensor_scalar(a_z[:, tiles, :], at[:, :, D:], EPS_ATTN, None, ALU.add))
                    settle(V_.reciprocal(a_z[:, tiles, :], a_z[:, tiles, :]))
                    V_.tensor_tensor(a_token[:, tiles, :].rearrange("p t (h d) -> p t h d", d=A_HD),
                                     at[:, :, 0:D].rearrange("p t (h d) -> p t h d", d=A_HD),
                                     a_z[:, tiles, :].unsqueeze(3).to_broadcast([P, 2, A_HEADS, A_HD]), ALU.mult).then_inc(a_normed, 1)
                add_y(1, a_r, XN)
                ln_stats(1, a_r, have_stats=True)
                scaled_norm(1, a_r, a_r, lambda tt: W["a_beta"], tr_in)
                dve.wait_ge(tr_in, 2 * TT)
                dve.wait_ge(out_stored, b * 16 + 1)
                V_.tensor_tensor(X[:, :, :], x_in, W["a_beta"].unsqueeze(1).to_broadcast([P, TT, D]), ALU.add).then_inc(x_shifted, 1)
                add_y(2, a_y, a_r)
                ln_stats(2, a_y, have_stats=True)
                dve.wait_ge(x_shifted, 1)
                scaled_norm(2, X, a_y, lambda tt: X[:, tt, :], x_shifted)
                dve.wait_ge(x_shifted, TT + 1)

            def mixture(k, ln_no, y_no):
                layer_norm(ln_no, have_stats=ln_no > 3)
                dve.wait_ge(f_xp, k + 1)
                dve.wait_ge(f_xxd, 4 * (k + 1))
                for tt in range(TT):
                    ins = V_.tensor_scalar(f_d[:, tt, :], f_p2[:, :], f_xx[:, tt:tt + 1], None, ALU.add)
                settle(ins)
                settle(V_.scalar_tensor_tensor(f_d, PS[:, 0, 0:TT * N_EXPERT].rearrange("p (t e) -> p t e", t=TT), 2.0,
                                               f_d, ALU.mult, ALU.subtract))
                settle(V_.tensor_scalar(f_d, f_d, 0.0, None, ALU.min))
                for tt in range(TT):
                    ins = V_.max(f_top[:, tt, :], f_d[:, tt, :])
                settle(ins)
                V_.tensor_scalar(f_near, f_top[:, :, 0:2], -1.0, None, ALU.mult).then_inc(f_d2, 1)
                idx = f_idx.bitcast(U32)
                for tt in range(TT):
                    ins = V_.max_index(idx[:, tt, :], f_top[:, tt, :], f_d[:, tt, :])
                settle(ins)
                settle(V_.tensor_copy(f_idxf, idx))
                dve.wait_ge(f_dist, k + 1)
                V_.tensor_tensor(f_w[:, 0, :], f_near[:, :, 1], f_near[:, :, 0], ALU.subtract).then_inc(f_diff, 1)
                dve.wait_ge(f_e2, k + 1)
                settle(V_.tensor_scalar(f_w[:, 2, :], f_w[:, 1, :], 1.0, None, ALU.add))
                settle(V_.reciprocal(f_w[:, 2, :], f_w[:, 2, :]))
                settle(V_.tensor_tensor(f_w[:, 3, :], f_w[:, 1, :], f_w[:, 2, :], ALU.mult))
                for tt in range(TT):
                    for j in range(2):
                        ins = V_.tensor_scalar(f_gate[:, TT * j + tt, :], W["expert_no"], f_idxf[:, tt, j:j + 1],
                                               f_w[:, 2 + j, tt:tt + 1], ALU.is_equal, ALU.mult)
                settle(ins)
                V_.tensor_tensor(f_gate[:, 0:TT, :], f_gate[:, 0:TT, :], f_gate[:, TT:, :], ALU.add).then_inc(f_gated, 1)
                dve.wait_ge(f_hs, 4 * (k + 1))
                for c in range(4):
                    dve.wait_ge(f_spread_up, 4 * k + c + 1)
                    V_.tensor_tensor(f_h[:, c, :], PS[:, 2 + c, :], f_h[:, c, :], ALU.mult).then_inc(f_gh, 1)
                add_y(y_no)

            def causal_attention():
                layer_norm(4)
                for j, dst in enumerate((b_q, b_k)):
                    dve.wait_ge(b_proj, j + 1)
                    bias = W["b_bias"]
                    V_.scalar_tensor_tensor(tmp[:, 0, :], PS[:, 2 * j, :], bias[:, 2 * j:2 * j + 1], W["b_cos"], ALU.add, ALU.mult)
                    settle(V_.scalar_tensor_tensor(tmp[:, 1, :], PS[:, 2 * j + 1, :], bias[:, 2 * j + 1:2 * j + 2],
                                                   W["b_sin"], ALU.add, ALU.mult))
                    settle(V_.tensor_tensor(dst, tmp[:, 0, :], tmp[:, 1, :], ALU.add))
                    V_.tensor_copy(b_parts[:, 3 * j, :], dst).then_inc(b_split, 1)
                    dve.wait_ge(b_split, 3 * j + 1)
                    settle(V_.tensor_tensor(b_rest, dst, b_parts[:, 3 * j, :], ALU.subtract))
                    V_.tensor_copy(b_parts[:, 3 * j + 1, :], b_rest).then_inc(b_split, 1)
                    dve.wait_ge(b_split, 3 * j + 2)
                    V_.tensor_tensor(b_parts[:, 3 * j + 2, :], b_rest, b_parts[:, 3 * j + 1, :], ALU.subtract).then_inc(b_split, 1)

                def row_max(n):
                    ib, h = n // 16, n % 16
                    dve.wait_ge(b_sc, n + 1)
                    V_.tensor_reduce(mx[:, h:h + 1], PS[:, n % 3, 0:P * (ib + 1)], AX.X, ALU.max).then_inc(b_max, 1)

                def max_parts(ib):
                    dve.wait_ge(b_max, 16 * (ib + 1))
                    if ib:
                        dve.wait_ge(b_mT, ib)
                    settle(V_.tensor_scalar(b_negmax, mx[:, 0:16], -1.0, None, ALU.mult))
                    neg, rest = (v.rearrange("p (b a) -> p a b", a=2) for v in (b_negmax, b_maxrest))
                    parts = b_maxparts.rearrange("p (a s b) -> p a s b", a=2, s=3)
                    settle(V_.tensor_copy(parts[:, :, 0, :], neg))
                    settle(V_.tensor_tensor(rest, neg, parts[:, :, 0, :], ALU.subtract))
                    settle(V_.tensor_copy(parts[:, :, 1, :], rest))
                    V_.tensor_tensor(parts[:, :, 2, :], rest, parts[:, :, 1, :], ALU.subtract).then_inc(b_mparts, 1)

                def normalised(ib):
                    dve.wait_ge(b_oq, ib + 1)
                    if ib:
                        dve.wait_ge(b_od, ib)
                    o = PS[:, 6 + ib % 2, :].rearrange("p (h d) -> p h d", h=B_HEADS)
                    settle(V_.reciprocal(b_rs, o[:, :, B_HD]))
                    V_.tensor_tensor(b_o[:, ib, :].rearrange("p (h d) -> p h d", h=B_HEADS), o[:, :, 0:B_HD],
                                     b_rs.unsqueeze(2).to_broadcast([P, B_HEADS, B_HD]), ALU.mult).then_inc(b_od, 1)

                for ib in range(TT):
                    for h in range(16):
                        row_max(16 * ib + h)
                        if ib == TT - 1 and h == 3:
                            normalised(0)
                    max_parts(ib)
                for ib in range(1, TT - 1):
                    normalised(ib)
                normalised(TT - 1)
                add_y(4)

            def phase_memory():
                layer_norm(6)
                taps = [W["c_taps_key"], W["c_taps_decay"]]
                for j in range(2):
                    dve.wait_ge(c_zs, 2 * j + 2)
                    settle(V_.tensor_scalar(c_conv[:, j, :], c_z[:, j, 0:T], taps[j][:, 0:1], None, ALU.mult))
                    for s in range(1, C_TAPS):
                        ins = V_.scalar_tensor_tensor(c_conv[:, j, :], c_z[:, j, s:s + T], taps[j][:, s:s + 1],
                                                      c_conv[:, j, :], ALU.mult, ALU.add)
                        if s < C_TAPS - 1:
                            settle(ins)
                    ins.then_inc(c_cv, 1)
                dve.wait_ge(c_cv, 2)
                settle(V_.tensor_scalar(c_pw, c_conv[:, 1, :], W["c_score_scale"], 20.0, ALU.mult, ALU.min))
                V_.scalar_tensor_tensor(c_pw, c_pw, -20.0, c_logdecay, ALU.max, ALU.add).then_inc(c_lp, 1)
                ones = one_col.to_broadcast([P, T])
                dve.wait_ge(c_pws, 1)

                def fraction(c):
                    i = c % 2
                    dve.wait_ge(c_mag, c + 1)
                    if c >= 2:
                        dve.wait_ge(c_trig, 2 * (c - 1))
                        dve.wait_ge(c_ab, c - 1)
                    V_.scalar_tensor_tensor(c_ff[:, i, :], c_rr[:, i, :], MAGIC, PS[:, i, :], ALU.subtract, ALU.subtract).then_inc(c_frac, 1)

                fraction(0)
                settle(V_.tensor_tensor_scan(c_inv, ones, c_pw, 0.0, ALU.mult, ALU.add))
                settle(V_.tensor_scalar(c_inv, c_inv, 0.0001, None, ALU.max))
                for c in range(C_CHUNKS):
                    i = c % 2
                    if c + 1 < C_CHUNKS:
                        fraction(c + 1)
                    dve.wait_ge(c_trig, 2 * c + 2)
                    dve.wait_ge(c_pwx, c + 1)
                    if c >= 2:
                        dve.wait_ge(c_sum, c - 1)
                    V_.tensor_tensor(c_pr[:, i, :], PS[:, 2 + i, :], c_re[:, i, :], ALU.mult).then_inc(c_prod, 1)
                    V_.tensor_tensor(c_pi[:, i, :], PS[:, 2 + i, :], c_im[:, i, :], ALU.mult).then_inc(c_prod, 1)
                    dve.wait_ge(c_prod, 2 * c + 1)
                    V_.tensor_tensor_scan(c_nr[:, i, :], ones, c_pr[:, i, :], 0.0, ALU.mult, ALU.add).then_inc(c_scan, 1)
                    dve.wait_ge(c_prod, 2 * c + 2)
                    V_.tensor_tensor_scan(c_ni[:, i, :], ones, c_pi[:, i, :], 0.0, ALU.mult, ALU.add).then_inc(c_scan, 1)
                settle(V_.reciprocal(c_inv, c_inv))
                dve.wait_ge(c_sum, C_CHUNKS)
                V_.tensor_tensor(c_y, PS[:, 6, :], c_inv, ALU.mult).then_inc(c_norm, 1)
                add_y(6)

            def mixed_attention():
                layer_norm(8)
                for n in range(16):
                    dve.wait_ge(e_qk, n + 1)
                    if n >= 2:
                        dve.wait_ge(e_add, n - 1)
                    k = 2 * (n % 2)
                    V_.tensor_tensor(tmp[:, k, :], PS[:, k, :], W["e_cos"], ALU.mult)
                    V_.tensor_tensor(tmp[:, k + 1, :], PS[:, k + 1, :], W["e_sin"], ALU.mult).then_inc(e_rope, 1)
                for ib in range(TT):
                    def hidden(n):
                        g = n % GROUPS
                        w, at = width(ib, g), table_at(ib, g)
                        dve.wait_ge(e_m1, n + 1)
                        if n >= 2:
                            dve.wait_ge(e_m2, n - 1)
                        k = 2 + 2 * (n % 2)
                        V_.tensor_tensor(e_hidden[:, n % 2, :, 0:w], PS[:, k:k + 2, 0:w],
                                         e_hidden_table[:, :, at:at + w], ALU.add).then_inc(e_hadd, 1)

                    hidden(GROUPS * ib)
                    for g in range(GROUPS):
                        n = GROUPS * ib + g
                        w = width(ib, g)
                        if g + 1 < GROUPS:
                            hidden(n + 1)
                        dve.wait_ge(e_m2, n + 1)
                        dve.wait_ge(e_fk, n + 1)
                        f = mixed(ib, g, 0, w)
                        if g == 0 and ib:
                            dve.wait_ge(e_exp, GROUPS * ib)
                        V_.tensor_tensor_reduce(out=f, in0=PS[:, 6 + n % 2, 0:w], in1=f, scale=1.0, scalar=-3e38,
                                                op0=ALU.add, op1=ALU.max, accum_out=mx[:, g:g + 1]).then_inc(e_fin, 1)
                        if g % 4 == 3:
                            q = slice(g - 3, g + 1)
                            dve.wait_ge(e_fin, n + 1)
                            V_.tensor_scalar(negmx[:, q], mx[:, q], -1.0, None, ALU.mult).then_inc(e_nmx, 1)
                    first = 4 * sum(range(1, ib + 1))

                    def divide(gq):
                        for g in range(4 * gq, 4 * gq + 4, 2):
                            dve.wait_ge(e_exp, GROUPS * ib + g + 2)
                            settle(V_.reciprocal(e_rs[:, g:g + 2], e_sum[:, g:g + 2]))
                            for k in (g, g + 1):
                                f = mixed(ib, k, 0, width(ib, k))
                                V_.tensor_scalar(f, f, e_rs[:, k:k + 1], None, ALU.mult).then_inc(e_div, 1)

                    divide(0)
                    for k in range(dve_copies(ib)):
                        gq, jb = k // (ib + 1), k % (ib + 1)
                        if jb == 0:
                            divide(gq + 1)
                        dve.wait_ge(e_tp, first + k + 1)
                        V_.tensor_copy(probs_T(ib)[:, jb, 32 * gq:32 * gq + 32, :].rearrange("p i h -> p (i h)"),
                                       PS[:, 2 + k % 4, :]).then_inc(e_ptc, 1)
                    dve.wait_ge(e_y, ib + 1)
                    V_.tensor_tensor(X[:, ib, :], PS[:, 7, 0:D], X[:, ib, :], ALU.add).then_inc(e_x, 1)
                    dve.wait_ge(e_x, ib + 1)
                    ins = V_.bn_stats(stats[:, ib, :], X[:, ib, :])
                settle(ins)

            with dve.Fori(0, B) as b:
                count[0] = 0
                dve.wait_ge(x_loaded, b * 16 + 16)
                linear_attention(b)
                if last >= 2:
                    mixture(0, 3, 3)
                if last >= 3:
                    causal_attention()
                if last >= 4:
                    mixture(1, 5, 5)
                if last >= 5:
                    phase_memory()
                if last >= 6:
                    layer_norm(7)
                    add_y(7)
                if last >= 7:
                    dve.drain().then_inc(front_done, 1)
                    mixed_attention()
                if last >= 8:
                    layer_norm(9)
                    add_y(8)
                dve.nop().then_inc(x_done, 1)
                dve.drain().then_inc(sequence_ended, 1)
                dve.wait_ge(sequence_go, b + 1)

        @block.tensor
        def _(pe):
            mm = nc.tensor.matmul

            pe.wait_ge(setup_pool, 5)
            pe.wait_ge(rows_loaded, 16)
            pe.wait_ge(setup_dve, 11)
            mm(PS[:, 0, 0:N_EXPERT], one_col.to_broadcast([P, P]), f_proto2[:, :], start=True, stop=True).then_inc(setup_pe, 1)
            pe.wait_ge(w_loaded["d"], 16)
            mm(PS[0:4, 1, 0:P], W["d_lora_down"][0:100, :], W["d_down_aux"][0:100, :], start=True, stop=True).then_inc(setup_pe, 1)
            pe.wait_ge(setup_act, 6)
            mm(PS[0:50, 2, 0:P], W["d_lora_up"][0:4, :], tmp[0:4, 0, 0:P], start=True, stop=True).then_inc(setup_pe, 1)
            pe.wait_ge(setup_act, 7)
            mm(PS[:, 3, 0:P], tmp[0:50, 1, 0:P], W["d_up_aux"][0:50, :], start=True, stop=True).then_inc(setup_pe, 1)
            pe.wait_ge(w_loaded["e"], 16)
            pe.wait_ge(setup_dve, SETUP_KERPLE)
            for half in range(2):
                w = W["e_mix_kerple"][:, P * half:P * (half + 1)]
                mm(PS[:, 4 + half, :], w, e_kerple[:, 0:512], start=True, stop=True)
                mm(PS[:, 6 + half, 0:STEP], w, e_kerple[:, 512:TABLE], start=True, stop=True).then_inc(setup_pe, 1)

            def feature_layout(k, src):
                for tt in range(TT):
                    pe.wait_ge(tr_in, TT * k + tt + 1)
                    nc.tensor.transpose(PS[:, 7 - 2 * (tt // 2), P * tt:P * (tt + 1)], src[:, tt, :], ident).then_inc(tr_psum, 1)

            def tok(t, tt):
                return t[:, P * tt:P * (tt + 1)]

            def linear_attention():
                pe.wait_ge(w_loaded["a"], 16)
                feature_layout(0, XN)
                pe.wait_ge(xT_ready, 2)
                mm(PS[:, 0, :], W["a_qkv"][:, 0:D], XT[:, :], start=True, stop=True).then_inc(a_proj, 1)
                mm(PS[:, 1, :], W["a_qkv"][:, D:2 * D], XT[:, :], start=True, stop=True).then_inc(a_proj, 1)
                for tt in range(TT):
                    ins = mm(PS[:, 2, D * tt:D * (tt + 1)], tok(XT, tt), W["a_qkv"][:, 2 * D:3 * D], start=True, stop=True)
                ins.then_inc(a_proj, 1)
                for n in range(8):
                    c = n % 4
                    pe.wait_ge(a_qk, 1 if n < 4 else 2)
                    if n >= 3:
                        pe.wait_ge(a_feat, n - 2)
                    bank = PS[:, 3 + n % 3, :]
                    if n < 4:
                        ins = mm(bank, W["a_features"][:, P * c:P * (c + 1)], a_qT, start=True, stop=True)
                    else:
                        ins = mm(bank, tok(a_kT, c), W["a_features"], start=True, stop=True)
                    ins.then_inc(a_fpre, 1)
                pe.wait_ge(a_feat, 8)
                pe.wait_ge(a_v, 1)
                for c in range(4):
                    at = (c % 2) * (D + 1)
                    for tt in range(TT):
                        ins = mm(PS[:, c // 2, at:at + D + 1], a_kf[:, tt, P * c:P * (c + 1)], v_aug[:, tt, :],
                                 start=tt == 0, stop=tt == TT - 1)
                    ins.then_inc(a_kv, 1)
                pe.wait_ge(a_masked, 8)
                for tt in range(TT):
                    for c in range(4):
                        at = (D + A_HEADS) * (tt % 2)
                        ins = mm(PS[:, 2 + tt // 2, at:at + D + A_HEADS], tok(a_qf[:, c, :], tt), a_kvz[:, c, :],
                                 start=c == 0, stop=c == 3)
                    if tt % 2:
                        ins.then_inc(a_att, 1)
                for half in range(2):
                    pe.wait_ge(a_normed, half + 1)
                    for tt in range(2 * half, 2 * half + 2):
                        ins = nc.tensor.transpose(PS[:, half, P * (tt % 2):P * (tt % 2 + 1)], a_token[:, tt, :], ident)
                    ins.then_inc(a_attn_T, 1)
                pe.wait_ge(a_attn_ready, 2)
                for tt in range(TT):
                    y = y_tile(tt)
                    mm(y, tok(a_attn, tt), W["a_out"], start=True, stop=False)
                    ins = mm(y, R["ones"], R["a_bo"], start=False, stop=True)
                    if tt % 2:
                        ins.then_inc(y_psum, 1)
                feature_layout(1, a_r)
                pe.wait_ge(xT_ready, 4)
                for c in range(4):
                    mm(PS[:, c, :], W["a_w1"][:, P * c:P * (c + 1)], XT[:, :], start=True, stop=True).then_inc(a_h, 1)
                pe.wait_ge(a_gelu, 4)
                w2 = W["a_w2"].rearrange("p (c d) -> p c d", c=4)
                for tt in range(TT):
                    y = y_tile(tt)
                    for c in range(4):
                        mm(y, tok(a_hT[:, c, :], tt), w2[:, c, :], start=c == 0, stop=False)
                    ins = mm(y, R["ones"], R["a_b2"], start=False, stop=True)
                    if tt % 2:
                        ins.then_inc(y_psum, 1)

            def mixture(k, tr):
                feature_layout(tr, XN)
                pe.wait_ge(xT_ready, 2 * (tr + 1))
                for tt in range(TT):
                    d = PS[:, 0, N_EXPERT * tt:N_EXPERT * (tt + 1)]
                    ins = mm(d, tok(XT, tt), W["f_proto"], start=True, stop=True)
                ins.then_inc(f_xp, 1)
                for c in range(4):
                    mm(PS[:, 2 + c, :], W["f_down"][:, P * c:P * (c + 1)], XT[:, :], start=True, stop=True).then_inc(f_hp, 1)
                pe.wait_ge(f_gated, k + 1)
                for tt in range(TT):
                    ins = nc.tensor.transpose(PS[0:N_EXPERT, 1, P * tt:P * (tt + 1)], f_gate[:, tt, :], ident)
                ins.then_inc(f_gT, 1)
                pe.wait_ge(f_gTs, k + 1)
                pe.wait_ge(f_hs, 4 * (k + 1))
                gT = f_gateT[0:N_EXPERT, :]
                for c in range(4):
                    mm(PS[:, 2 + c, :], W["f_spread"][0:N_EXPERT, P * c:P * (c + 1)], gT, start=True, stop=True).then_inc(f_spread_up, 1)
                pe.wait_ge(f_gh, 4 * (k + 1))
                up = W["f_up"].rearrange("p (c d) -> p c d", c=4)
                for tt in range(TT):
                    y = y_tile(tt)
                    for c in range(4):
                        mm(y, tok(f_h[:, c, :], tt), up[:, c, :], start=c == 0, stop=False)
                    ins = mm(y, gT[:, P * tt:P * (tt + 1)], W["f_bias"][0:N_EXPERT, :], start=False, stop=True)
                    if tt % 2:
                        ins.then_inc(y_psum, 1)

            def causal_attention(b):
                feature_layout(3, XN)
                pe.wait_ge(xT_ready, 8)
                for j, name in enumerate(("b_q", "b_qrot", "b_k", "b_krot")):
                    ins = mm(PS[:, j, :], W[name], XT[:, :], start=True, stop=True)
                    if j % 2 == 1:
                        ins.then_inc(b_proj, 1)
                for tt in range(TT):
                    v = PS[:, 4, D * tt:D * (tt + 1)]
                    mm(v, tok(XT, tt), W["b_v"], start=True, stop=False)
                    ins = mm(v, R["ones"], R["b_bv"], start=False, stop=True)
                ins.then_inc(b_proj, 1)

                def scores(n):
                    ib, h = n // 16, n % 16
                    blk = h // 2
                    if n >= 3:
                        pe.wait_ge(b_max, n - 2)
                    mm(PS[:, n % 3, 0:P * (ib + 1)], b_qs[:, blk, P * ib:P * (ib + 1)],
                       b_ks[:, 8 * (h % 2) + blk, 0:P * (ib + 1)], start=True, stop=False)
                    mm(PS[:, n % 3, P * ib:P * (ib + 1)], ident_bf, causal_mask, start=False, stop=True).then_inc(b_sc, 1)

                def maxima_T(ib):
                    pe.wait_ge(b_mparts, ib + 1)
                    if ib:
                        pe.wait_ge(b_mTs, ib)
                    nc.tensor.transpose(PS[:, 3, :].bitcast(BF16)[0:48, 0:P], b_maxparts, ident_bf).then_inc(b_mT, 1)

                def scores_T(n):
                    ib, h = n // 16, n % 16
                    blk = h // 2
                    if n >= 2:
                        pe.wait_ge(b_exp, n - 1)
                    for jb in range(ib + 1):
                        ins = mm(PS[:, 4 + n % 2, P * jb:P * (jb + 1)], b_ks[:, 8 * (h % 2) + blk, P * jb:P * (jb + 1)],
                                 b_qs[:, blk, P * ib:P * (ib + 1)], start=True, stop=jb < ib)
                    mm(PS[:, 4 + n % 2, P * ib:P * (ib + 1)], ident_bf, causal_mask_T, start=False, stop=True).then_inc(b_st, 1)

                def times_v(quad):
                    ib, g = quad // 4, quad % 4
                    pe.wait_ge(b_exp, 4 * quad + 4)
                    if g == 0 and ib >= 2:
                        pe.wait_ge(b_od, ib - 1)
                    for jb in range(ib + 1):
                        for k in range(4):
                            ins = mm(PS[QUARTER * k:QUARTER * (k + 1), 6 + ib % 2, P * g:P * (g + 1)],
                                     b_val[:, jb, 4 * g + k, :], b_pT[:, 4 * (quad % 2) + k, P * jb:P * (jb + 1)],
                                     start=jb == 0, stop=jb == ib)
                    ins.then_inc(b_pv, 1)

                def outputs_T(ib):
                    pe.wait_ge(b_of_ready, ib + 1)
                    for g in range(4):
                        ins = nc.tensor.transpose(PS[:, 6 + ib % 2, P * g:P * (g + 1)], b_of[:, P * g:P * (g + 1)], ident)
                    ins.then_inc(b_oq, 1)

                pe.wait_ge(b_vs, 1)
                pe.wait_ge(b_ones, 2)
                pe.wait_ge(b_spread_even, len(SPREAD) * 16)
                pe.wait_ge(b_spread_odd, (len(SPREAD) - POOL_SPREADS) * 16)
                pe.wait_ge(b_spread_pool, b * (POOL_SPREADS * 16) + POOL_SPREADS * 16)
                for n in range(MAX_AHEAD):
                    scores(n)
                    if n == 19:
                        maxima_T(0)
                for n in range(64):
                    ib, h = n // 16, n % 16
                    if h == 0:
                        pe.wait_ge(b_mrows[ib % 2], 32 * (ib // 2 + 1))
                    scores_T(n)
                    if n % 4 == 1 and n > 4:
                        times_v(n // 4 - 1)
                    if n + MAX_AHEAD < 64:
                        scores(n + MAX_AHEAD)
                    if h == 6 and ib + 1 < TT:
                        maxima_T(ib + 1)
                    if h == 5 and ib:
                        outputs_T(ib - 1)
                times_v(15)
                outputs_T(TT - 1)
                pe.wait_ge(b_od, TT)
                for ib in range(TT):
                    ins = nc.tensor.transpose(PS[:, 4, P * ib:P * (ib + 1)], b_o[:, ib, :], ident)
                ins.then_inc(b_ot, 1)
                pe.wait_ge(b_ots, 1)
                for tt in range(TT):
                    y = y_tile(tt)
                    mm(y, tok(b_oT, tt), W["b_out"], start=True, stop=False)
                    ins = mm(y, R["ones"], R["b_bo"], start=False, stop=True)
                    if tt % 2:
                        ins.then_inc(y_psum, 1)

            def phase_memory():
                feature_layout(5, XN)
                pe.wait_ge(xT_ready, 12)
                for j, name in enumerate(("c_key", "c_decay")):
                    mm(PS[:, j, :], W[name], XT[:, :], start=True, stop=True).then_inc(c_zp, 1)
                pe.wait_ge(c_zs, 4)
                pe.wait_ge(c_cv, 1)

                def turns(c):
                    if c >= 2:
                        pe.wait_ge(c_frac, c - 1)
                    mm(PS[:, c % 2, :], W["c_theta"][:, P * c:P * (c + 1)], c_conv[:, 0, :], start=True, stop=True).then_inc(c_up, 1)

                turns(0)
                turns(1)
                for c in range(C_CHUNKS):
                    if c == 0:
                        pe.wait_ge(c_pws, 1)
                    if c >= 2:
                        pe.wait_ge(c_prod, 2 * (c - 1))
                    mm(PS[:, 2 + c % 2, :], W["c_spread"][:, P * c:P * (c + 1)], c_pw, start=True, stop=True).then_inc(c_pwx, 1)
                    if c + 2 < C_CHUNKS:
                        turns(c + 2)
                    if c % 2 == 0:
                        kq = c // 2
                        if kq:
                            pe.wait_ge(c_qs, 2 * kq)
                        mm(PS[:, 4, :], W["c_qre"][:, P * kq:P * (kq + 1)], XT[:, :], start=True, stop=True)
                        mm(PS[:, 5, :], W["c_qim"][:, P * kq:P * (kq + 1)], XT[:, :], start=True, stop=True).then_inc(c_query, 1)
                    if c >= 1:
                        gather(c - 1)
                gather(C_CHUNKS - 1)
                pe.wait_ge(c_silu, 1)
                for tt in range(TT):
                    ins = mm(y_tile(tt), tok(c_y, tt), W["c_out"], start=True, stop=True)
                    if tt % 2:
                        ins.then_inc(y_psum, 1)

            def gather(c):
                pe.wait_ge(c_weighted, 2 * c + 2)
                w = W["c_gather"][:, P * c:P * (c + 1)]
                mm(PS[:, 6, :], w, c_pr[:, c % 2, :], start=c == 0, stop=False)
                mm(PS[:, 6, :], w, c_pi[:, c % 2, :], start=False, stop=c == C_CHUNKS - 1).then_inc(c_sum, 1)

            def adapted_linear(tr):
                feature_layout(tr, XN)
                pe.wait_ge(xT_ready, 2 * (tr + 1))
                for tt in range(TT):
                    y = y_tile(tt)
                    mm(y, tok(XT, tt), d_weight[:, :], start=True, stop=False)
                    ins = mm(y, R["ones"], R["d_b"], start=False, stop=True)
                    if tt % 2:
                        ins.then_inc(y_psum, 1)

            def mixed_attention():
                feature_layout(7, XN)
                pe.wait_ge(xT_ready, 16)
                pe.wait_ge(e_w, 16)
                n_ch = E_HEADS * E_HD
                for n in range(16):
                    at = 2 * n_ch * (n % 2) + P * (n // 2)
                    k = 2 * (n % 2)
                    if n >= 2:
                        pe.wait_ge(e_rope, n - 1)
                    mm(PS[:, k, :], proj[:, at:at + P], XT[:, :], start=True, stop=True)
                    mm(PS[:, k + 1, :], proj[:, at + n_ch:at + n_ch + P], XT[:, :], start=True, stop=True).then_inc(e_qk, 1)

                def values(r):
                    if r >= 2:
                        pe.wait_ge(e_vs, r - 1)
                    mm(PS[:, 4 + r % 2, :], tok(XT, r // 2), proj[:, 4 * n_ch + 512 * (r % 2):4 * n_ch + 512 * (r % 2 + 1)],
                       start=True, stop=True).then_inc(e_vp, 1)

                values(0)
                values(1)
                pe.wait_ge(e_rope, 16)
                pe.wait_ge(e_add, 16)

                def scores(ib):
                    w = P * (ib + 1)
                    for h in range(E_HEADS):
                        n = 16 * ib + h
                        if n >= 4 and h % 2 == 0:
                            pe.wait_ge(e_evac, n - 2)
                        at = 64 * (h % 2)
                        mm(PS[:, score_bank(h), 0:w], QT[at:at + 64, h // 2, P * ib:P * (ib + 1)], KT[at:at + 64, h // 2, 0:w],
                           start=True, stop=True).then_inc(e_sc, 1)

                scores(0)
                for r in range(2, 8):
                    values(r)
                pe.wait_ge(e_vs, 8)
                for ib in range(TT):
                    def mix(n):
                        g = n % GROUPS
                        pe.wait_ge(e_dma[g // 4], 64 * (ib + 1))
                        if g == 0 and ib:
                            pe.wait_ge(e_x, ib)
                        if n >= 2:
                            pe.wait_ge(e_hadd, n - 1)
                        for half in range(2):
                            ins = mm(PS[:, 2 + 2 * (n % 2) + half, 0:width(ib, g)], W["e_mix_scores"][:, P * half:P * (half + 1)],
                                     mixed(ib, g, 0, width(ib, g)), start=True, stop=True)
                        ins.then_inc(e_m1, 1)

                    mix(GROUPS * ib)
                    mix(GROUPS * ib + 1)
                    for g in range(GROUPS):
                        n = GROUPS * ib + g
                        if g + 2 < GROUPS:
                            mix(n + 2)
                        pe.wait_ge(e_gelu, n + 1)
                        if n >= 2:
                            pe.wait_ge(e_fin, n - 1)
                        for half in range(2):
                            at = 64 * half
                            ins = mm(PS[at:at + 64, 6 + n % 2, 0:width(ib, g)],
                                     W["e_mix_back"][:, P * half + at:P * half + at + 64],
                                     e_hidden[:, n % 2, half, 0:width(ib, g)], start=True, stop=True)
                        ins.then_inc(e_m2, 1)
                    first = 4 * sum(range(1, ib + 1))
                    pe.wait_ge(e_zero, 3 * (ib + 1))
                    for k in range(4 * (ib + 1)):
                        gq, jb = k // (ib + 1), k % (ib + 1)
                        if 4 <= k < dve_copies(ib) + 4:
                            pe.wait_ge(e_ptc, sum(dve_copies(i) for i in range(ib)) + k - 3)
                        if k >= dve_copies(ib) + 4:
                            pe.wait_ge(e_ptc_act, sum(4 * (i + 1) - dve_copies(i) for i in range(ib)) + k - 3 - dve_copies(ib))
                        for g4 in range(4):
                            if jb == 0:
                                pe.wait_ge(e_div, GROUPS * ib + 4 * gq + g4 + 1)
                            ins = nc.tensor.transpose(PS[:, 2 + k % 4, P * g4:P * (g4 + 1)],
                                                      mixed(ib, 4 * gq + g4, P * jb, P * (jb + 1)), ident)
                        ins.then_inc(e_tp, 1)
                    if ib + 1 < TT:
                        scores(ib + 1)
                    pe.wait_ge(e_ptc, sum(dve_copies(i) for i in range(ib + 1)))
                    pe.wait_ge(e_ptc_act, sum(4 * (i + 1) - dve_copies(i) for i in range(ib + 1)))
                    for c in range(8):
                        for a in range(2):
                            o = PS[64 * a:64 * a + E_HD, 4 + c // 4, P * (c % 4):P * (c % 4 + 1)]
                            for jb in range(ib + 1):
                                ins = mm(o, V[:, jb, 2 * c + a, :], probs_T(ib)[:, jb, :, 2 * c + a], start=jb == 0, stop=jb == ib)
                        if c % 4 == 3:
                            ins.then_inc(e_pv, 1)
                    if ib + 1 < TT:
                        pe.wait_ge(e_evac, 16 * (ib + 1) + 14)
                    for c in range(8):
                        pe.wait_ge(e_ots, 2 * ib + c // 4 + 1)
                        ins = mm(PS[:, 7, 0:D], e_oT[:, P * c:P * (c + 1)], W["e_out"][:, D * c:D * (c + 1)],
                                 start=c == 0, stop=c == 7)
                    ins.then_inc(e_y, 1)

            with pe.Fori(0, B) as b:
                linear_attention()
                if last >= 2:
                    mixture(0, 2)
                if last >= 3:
                    causal_attention(b)
                if last >= 4:
                    mixture(1, 4)
                if last >= 5:
                    phase_memory()
                if last >= 6:
                    adapted_linear(6)
                if last >= 7:
                    pe.drain().then_inc(front_done, 1)
                    mixed_attention()
                if last >= 8:
                    adapted_linear(8)
                pe.drain().then_inc(sequence_ended, 1)
                pe.wait_ge(sequence_go, b + 1)


def _pack(group, pieces):
    got = []
    for name, n in PARTS[group]:
        a = np.asarray(pieces[name])
        a = a.reshape(a.shape[0], -1)
        assert a.shape[1] == n, (name, a.shape)
        got.append(np.concatenate([a, np.zeros((P - a.shape[0], n), np.float32)]) if a.shape[0] < P else a)
    return np.ascontiguousarray(np.concatenate(got, axis=1), dtype=np.float32)


def _layout(i):
    g = {k: np.asarray(v) for k, v in i.items()}
    f4 = np.float32
    eye = np.eye(P, dtype=f4)
    col = np.arange(P)
    out = {}
    proj = g["L0_attn_a_proj"]
    feats = np.zeros((P, A_FEATS), f4)
    for h in range(A_HEADS):
        feats[A_HD * h:A_HD * (h + 1), A_F * h:A_F * (h + 1)] = proj[h]
    kv_mask = np.zeros((P, 4, P), f4)
    for c in range(4):
        kv_mask[:, c, :] = (4 * c + col[:, None] // A_F) == (col[None, :] // A_HD)
    rep = lambda v, n=P: np.broadcast_to(v.reshape(1, -1), (n, v.size))
    out["w_a"] = _pack("a", dict(
        a_qkv=g["L0_attn_a_w_qkv"].T, a_features=feats, a_out=g["L0_attn_a_w_out"].T, a_w1=g["L0_attn_a_w1"].T,
        a_w2=g["L0_attn_a_w2"].T.reshape(4, P, D).transpose(1, 0, 2), a_gamma=rep(g["L0_attn_a_gamma"]),
        a_beta=rep(g["L0_attn_a_beta"]), a_b1=g["L0_attn_a_b1"].reshape(4, P).T, identity=eye, a_kv_mask=kv_mask))
    spread = np.zeros((N_EXPERT, N_EXPERT * RANK), f4)
    for e in range(N_EXPERT):
        spread[e, RANK * e:RANK * (e + 1)] = 1
    out["w_f"] = _pack("f", dict(
        f_proto=g["L0_ffn_prototypes"].T, f_down=g["L0_ffn_B"].reshape(-1, D).T,
        f_up=g["L0_ffn_A"].transpose(0, 2, 1).reshape(4, P, D).transpose(1, 0, 2), f_bias=g["L0_ffn_bias"],
        f_temp=np.broadcast_to(g["L0_ffn_temp"].reshape(1, 1), (P, 1)), expert_no=rep(np.arange(N_EXPERT, dtype=f4)),
        f_spread=spread))
    def rope(hd, n):
        inv = (1.0 / np.float32(10000.0) ** (np.arange(0, hd, 2, dtype=f4) / f4(hd))).astype(f4)
        fr = np.arange(T, dtype=f4)[None, :] * inv[:, None]
        cos, sin = np.cos(fr), np.sin(fr)
        return (np.tile(np.concatenate([cos, cos]), (n, 1)).astype(f4), np.tile(np.concatenate([-sin, sin]), (n, 1)).astype(f4))

    def rot(hd, n):
        return (np.arange(n) // hd) * hd + (np.arange(n) % hd + hd // 2) % hd
    w, bias = g["L0_attn_b_qkv_w"], g["L0_attn_b_qkv_b"]
    o = B_HD * (2 * (col % 8) + col // 64) + col // 8 % 8
    r = rot(B_HD, D)[o]
    cos, sin = (t[o] for t in rope(B_HD, B_HEADS))
    out["w_b"] = _pack("b", dict(
        b_q=w[0:D][o].T, b_qrot=w[0:D][r].T, b_k=w[D:2 * D][o].T, b_krot=w[D:2 * D][r].T, b_v=w[2 * D:].T,
        b_bias=np.stack([bias[0:D][o], bias[0:D][r], bias[D:2 * D][o], bias[D:2 * D][r]], 1), b_out=g["L0_attn_b_proj_w"].T,
        b_cos=cos, b_sin=sin))
    W_in, ck = g["L1_attn_a_W_in"], g["L1_attn_a_conv_k"][:, 0, :]
    key_of = col // C_H
    theta = np.zeros((P, C_CHUNKS, P), f4)
    c_spread = np.zeros((P, C_CHUNKS, P), f4)
    c_gather = np.zeros((P, C_CHUNKS, P), f4)
    k4, hh, m = col // (C_H * C_M), col // C_M % C_H, col % C_M
    for c in range(C_CHUNKS):
        row = (4 * c + k4) * C_H + hh
        theta[row, c, col] = g["L1_attn_a_theta"][0, 0, 4 * c + k4, hh, m]
        c_spread[row, c, col] = 1
        c_gather[col, c, row] = 1
    q = W_in[:, D + C_K:].reshape(D, C_KQ, C_H, C_M, 2)
    rep_q = lambda a: np.broadcast_to(a[:, :, None], (D, C_KQ, 4, C_H, C_M)).reshape(D, C_KQ * P)
    ns = g["L1_attn_a_norm_scale"]
    d_re, d_im = (g[f"L1_attn_a_W_{x}"][np.arange(C_H), np.arange(C_H)] for x in ("re", "im"))
    pos = np.arange(T, dtype=f4)
    steps = np.where((key_of < C_K - C_ANCHOR)[:, None], f4(T - 1) - pos[None], pos[None]).astype(f4)
    slopes = np.concatenate([g["L1_attn_a_decay_slopes"], g["L1_attn_a_anchor_slopes"]])[key_of]
    eh = col % E_HEADS
    out["w_c"] = _pack("c", dict(
        c_key=W_in[:, 0:D], c_decay=W_in[:, D + key_of], c_taps_key=ck[:, 0:D].T, c_taps_decay=ck[:, D + key_of].T,
        c_score_scale=g["L1_attn_a_score_scale"][key_of][:, None],
        softplus_in=np.stack([slopes, g["L1_attn_b_log_p"].reshape(-1)[eh], g["L1_attn_b_log_a"].reshape(-1)[eh]], 1),
        c_theta=theta, c_qre=rep_q(q[..., 0]), c_qim=rep_q(q[..., 1]),
        c_out=g["L1_attn_a_W_out"], c_steps=steps, c_spread=c_spread, c_gather=c_gather))
    out["w_d"] = _pack("d", dict(
        causal_masks=np.concatenate([np.where(col[None, :] <= col[:, None], 0, MASKED),
                                     np.where(col[:, None] <= col[None, :], 0, MASKED)], 1),
        c_norm=np.concatenate([rep(ns[hh]), rep(ns[C_H + hh])], 1), c_diag=np.concatenate([rep(d_re[hh]), rep(d_im[hh])], 1),
        d_w=g["L1_ffn_W"].T, d_lora_down=g["L1_ffn_lora_down"].T, d_down_aux=g["L1_ffn_down_aux"],
        d_lora_up=g["L1_ffn_lora_up"].T, d_up_aux=g["L1_ffn_up_aux"].T))
    w1, w2 = g["L1_attn_b_w1"], g["L1_attn_b_w2"]
    s1, k1, s2 = (np.zeros((P, 2, P), f4) for _ in range(3))
    for i in range(QROWS):
        half, i4 = i // 4, i % 4
        rows_, cols_ = slice(E_HEADS * i, E_HEADS * (i + 1)), slice(E_CH * i4, E_CH * (i4 + 1))
        s1[rows_, half, cols_] = w1[0:E_HEADS]
        k1[rows_, half, cols_] = w1[E_HEADS:]
        s2[cols_, half, rows_] = w2
    dist = (col // E_HEADS)[:, None] + (T - 1) - np.arange(TABLE)[None, :]
    cos, sin = rope(E_HD, 2)
    out["w_e"] = _pack("e", dict(
        e_out=g["L1_attn_b_w_o"].reshape(8, P, D).transpose(1, 0, 2), e_mix_scores=s1, e_mix_kerple=k1, e_mix_back=s2,
        e_b1=g["L1_attn_b_b1"][col % E_CH][:, None], e_b2=g["L1_attn_b_b2"][eh][:, None], e_cos=cos, e_sin=sin,
        e_dist=np.abs(dist).astype(f4), e_mask=np.where(dist >= 0, 0, MASKED).astype(f4)))
    wq = g["L1_attn_b_w_qkv"].reshape(P, 3, E_HEADS * E_HD)
    r = rot(E_HD, E_HEADS * E_HD)
    out["w_proj"] = np.ascontiguousarray(np.concatenate([wq[:, 0], wq[:, 0][:, r], wq[:, 1], wq[:, 1][:, r], wq[:, 2]], 1))
    rows = dict(ones=np.ones(P, f4), a_bo=g["L0_attn_a_b_out"], a_b2=g["L0_attn_a_b2"], b_bv=bias[2 * D:],
                b_bo=g["L0_attn_b_proj_b"], d_b=g["L1_ffn_b"])
    out["rows"] = np.ascontiguousarray(np.concatenate([rows[n] for n, _ in ROWS]).reshape(1, -1))
    return out


ORDER = ["w_a", "w_f", "w_b", "w_c", "w_d", "w_e", "w_proj", "rows"]
LAST = 8


def kernel(**inputs):
    import concourse.bacc as bacc
    from concourse.bass_utils import run_bass_kernel_spmd

    x = np.ascontiguousarray(inputs["L0_attn_a_x"])
    arrays = {"x": x, **_layout(inputs)}
    nc = bacc.Bacc("TRN2", target_bir_lowering=False, num_devices=1)
    args = [nc.dram_tensor(n + "_dram", arrays[n].shape, mybir.dt.from_np(arrays[n].dtype), kind="ExternalInput").ap()
            for n in ["x"] + ORDER]
    out = nc.dram_tensor("out_dram", x.shape, F32, kind="ExternalOutput").ap()
    build(nc, *args, out, last=LAST)
    got = run_bass_kernel_spmd(nc, [{n + "_dram": a for n, a in arrays.items()}], core_ids=[0])
    return got.results[0]["out_dram"]
```
